# Optimizing a Trainium2 kernel written in Bass

```python
import numpy as np
import jax
import jax.numpy as jnp

def _softmax(x, axis=-1):
    return jax.nn.softmax(x, axis=axis)

def _gelu(x):
    return jax.nn.gelu(x, approximate=True)

def _silu(x):
    return jax.nn.silu(x)

def _sigmoid(x):
    return jax.nn.sigmoid(x)

def _layernorm(x, axis=-1, eps=1e-05):
    m = jnp.mean(x, axis=axis, keepdims=True)
    v = jnp.var(x, axis=axis, keepdims=True)
    return (x - m) / jnp.sqrt(v + eps)

def _scatter_add(tgt, idx, src, axis=0):
    return tgt.at[idx].add(src)

def _segment_sum(src, seg, n):
    return jax.ops.segment_sum(src, seg, n)
kernel_name = 'mk_metaformer_d2_conv_nhwc128_r4_4540d4'

def setup_inputs(seed: int=0):
    np.random.seed(seed)
    _w = jnp.asarray

    def _rec_inputs():
        import jax
        import jax.numpy as jnp
        _gk = jax.random.key(seed)
        x = -0.0003482 + 1 * jax.random.normal(jax.random.fold_in(_gk, 1), (16, 24, 24, 32), jnp.float32)
        return x
    x = _rec_inputs()

    def _L0_conv_setup():
        import jax, jax.numpy as jnp
        import numpy as np
        B, H, W, C = (16, 24, 24, 32)
        FOCAL_LEVEL = 3
        FOCAL_WINDOW = 3
        FOCAL_FACTOR = 2
        LN_EPS = 0.001

        def dwconv_same(x, k):
            return jax.lax.conv_general_dilated(x, k, window_strides=(1, 1), padding='SAME', dimension_numbers=('NHWC', 'HWIO', 'NHWC'), feature_group_count=x.shape[-1])
        key = jax.random.key(seed)
        ks = jax.random.split(key, 12)
        s = 0.02
        out_f = 2 * C + (FOCAL_LEVEL + 1)
        inp = {'x': jax.random.normal(ks[0], (B, H, W, C), dtype=jnp.float32), 'Wf': jax.random.normal(ks[1], (C, out_f), dtype=jnp.float32) * s, 'bf': jnp.zeros((out_f,), dtype=jnp.float32), 'Wh': jax.random.normal(ks[2], (C, C), dtype=jnp.float32) * s, 'bh': jnp.zeros((C,), dtype=jnp.float32), 'gamma': jnp.ones((C,), dtype=jnp.float32), 'beta': jnp.zeros((C,), dtype=jnp.float32), 'Wp': jax.random.normal(ks[3], (C, C), dtype=jnp.float32) * s, 'bp': jnp.zeros((C,), dtype=jnp.float32)}
        for l in range(FOCAL_LEVEL):
            kk = FOCAL_FACTOR * l + FOCAL_WINDOW
            inp[f'k{l}'] = jax.random.normal(ks[4 + l], (kk, kk, 1, C), dtype=jnp.float32) * s
        return inp
    _L0_conv_all = _L0_conv_setup()
    _L0_conv_in = {k: v for k, v in _L0_conv_all.items() if k in ('Wf', 'bf', 'k0', 'k1', 'k2', 'Wh', 'bh', 'gamma', 'beta', 'Wp', 'bp')}
    del _L0_conv_all

    def _L0_ffn_setup():
        import jax, jax.numpy as jnp
        import numpy as np
        BN_EPS = 1e-05
        key = jax.random.key(seed)
        k1, k2, k3 = jax.random.split(key, 3)
        B, T, I, H = (16, 512, 32, 32)
        x = jax.random.normal(k1, (B, T, I), dtype=jnp.float32)
        W = jax.random.normal(k2, (H, I), dtype=jnp.float32) * (1.0 / np.sqrt(I))
        V = jnp.linalg.qr(jax.random.normal(k3, (H, H), dtype=jnp.float32))[0]
        gamma = jnp.ones((H,), dtype=jnp.float32)
        beta = jnp.zeros((H,), dtype=jnp.float32)
        return {'x': x, 'W': W, 'V': V, 'gamma': gamma, 'beta': beta}
    _L0_ffn_all = _L0_ffn_setup()
    _L0_ffn_in = {k: v for k, v in _L0_ffn_all.items() if k in ('W', 'V', 'gamma', 'beta')}
    del _L0_ffn_all

    def _L1_conv_setup():
        import jax, jax.numpy as jnp
        from jax import lax
        import numpy as np
        D_MODEL = 32
        D_STATE = 16
        D_CONV = 4
        EXPAND = 2
        D_INNER = EXPAND * D_MODEL
        DT_RANK = (D_MODEL + 15) // 16
        B, H, W = (2, 28, 28)

        def _mamba(x, in_w, conv_w, conv_b, x_w, dt_w, dt_b, A_log, D, out_w):
            Bn, L, _ = x.shape
            xz = x @ in_w.T
            xc, z = jnp.split(xz, 2, axis=-1)
            xt = jnp.transpose(xc, (0, 2, 1))
            xt = lax.conv_general_dilated(xt, conv_w[:, None, :], window_strides=(1,), padding=[(D_CONV - 1, 0)], feature_group_count=D_INNER)
            xt = xt + conv_b[None, :, None]
            xc = jax.nn.silu(jnp.transpose(xt, (0, 2, 1)))
            dbl = xc @ x_w.T
            dt, Bm, Cm = jnp.split(dbl, [DT_RANK, DT_RANK + D_STATE], axis=-1)
            dt = jax.nn.softplus(dt @ dt_w.T + dt_b)
            A = -jnp.exp(A_log)
            dA = jnp.exp(dt[..., None] * A)
            dBx = dt[..., None] * Bm[:, :, None, :] * xc[..., None]

            def step(h, inp):
                dA_t, dBx_t, C_t = inp
                h = dA_t * h + dBx_t
                y = jnp.einsum('bds,bs->bd', h, C_t)
                return (h, y)
            h0 = jnp.zeros((Bn, D_INNER, D_STATE), x.dtype)
            _, ys = lax.scan(step, h0, (jnp.swapaxes(dA, 0, 1), jnp.swapaxes(dBx, 0, 1), jnp.swapaxes(Cm, 0, 1)))
            y = jnp.swapaxes(ys, 0, 1) + xc * D
            y = y * jax.nn.silu(z)
            return y @ out_w.T
        key = jax.random.key(seed)
        ks = jax.random.split(key, 8)
        s = 0.02
        return {'x': jax.random.normal(ks[0], (B, H, W, D_MODEL), jnp.float32), 'in_w': jax.random.normal(ks[1], (2 * D_INNER, D_MODEL), jnp.float32) * s, 'conv_w': jax.random.normal(ks[2], (D_INNER, D_CONV), jnp.float32) * s, 'conv_b': jnp.zeros((D_INNER,), jnp.float32), 'x_w': jax.random.normal(ks[3], (DT_RANK + 2 * D_STATE, D_INNER), jnp.float32) * s, 'dt_w': jax.random.normal(ks[4], (D_INNER, DT_RANK), jnp.float32) * s, 'dt_b': jax.random.normal(ks[5], (D_INNER,), jnp.float32) * 0.1, 'A_log': jnp.tile(jnp.log(jnp.arange(1, D_STATE + 1, dtype=jnp.float32)), (D_INNER, 1)), 'D': jnp.ones((D_INNER,), jnp.float32), 'out_w': jax.random.normal(ks[6], (D_MODEL, D_INNER), jnp.float32) * s}
    _L1_conv_all = _L1_conv_setup()
    _L1_conv_in = {k: v for k, v in _L1_conv_all.items() if k in ('in_w', 'conv_w', 'conv_b', 'x_w', 'dt_w', 'dt_b', 'A_log', 'D', 'out_w')}
    del _L1_conv_all

    def _L1_ffn_setup():
        import jax, jax.numpy as jnp
        import numpy as np
        B, N, D, C, E, K = (8, 2048, 32, 32, 8, 2)
        key = jax.random.key(seed)
        k0, k1, k2 = jax.random.split(key, 3)
        x = jax.random.normal(k0, (B, N, D), dtype=jnp.float32)
        router_w = jax.random.normal(k1, (D, E), dtype=jnp.float32) * 0.05
        router_b = jnp.zeros((E,), dtype=jnp.float32)
        expert_w = jax.random.normal(k2, (E, D, C), dtype=jnp.float32) * (1.0 / np.sqrt(D))
        expert_b = jnp.zeros((E, C), dtype=jnp.float32)
        return {'x': x, 'router_w': router_w, 'router_b': router_b, 'expert_w': expert_w, 'expert_b': expert_b}
    _L1_ffn_all = _L1_ffn_setup()
    _L1_ffn_in = {k: v for k, v in _L1_ffn_all.items() if k in ('router_w', 'router_b', 'expert_w', 'expert_b')}
    del _L1_ffn_all
    return {'x': x, 'L0_conv_Wf': _L0_conv_in['Wf'], 'L0_conv_bf': _L0_conv_in['bf'], 'L0_conv_k0': _L0_conv_in['k0'], 'L0_conv_k1': _L0_conv_in['k1'], 'L0_conv_k2': _L0_conv_in['k2'], 'L0_conv_Wh': _L0_conv_in['Wh'], 'L0_conv_bh': _L0_conv_in['bh'], 'L0_conv_gamma': _L0_conv_in['gamma'], 'L0_conv_beta': _L0_conv_in['beta'], 'L0_conv_Wp': _L0_conv_in['Wp'], 'L0_conv_bp': _L0_conv_in['bp'], 'L0_ffn_W': _L0_ffn_in['W'], 'L0_ffn_V': _L0_ffn_in['V'], 'L0_ffn_gamma': _L0_ffn_in['gamma'], 'L0_ffn_beta': _L0_ffn_in['beta'], 'L1_conv_in_w': _L1_conv_in['in_w'], 'L1_conv_conv_w': _L1_conv_in['conv_w'], 'L1_conv_conv_b': _L1_conv_in['conv_b'], 'L1_conv_x_w': _L1_conv_in['x_w'], 'L1_conv_dt_w': _L1_conv_in['dt_w'], 'L1_conv_dt_b': _L1_conv_in['dt_b'], 'L1_conv_A_log': _L1_conv_in['A_log'], 'L1_conv_D': _L1_conv_in['D'], 'L1_conv_out_w': _L1_conv_in['out_w'], 'L1_ffn_router_w': _L1_ffn_in['router_w'], 'L1_ffn_router_b': _L1_ffn_in['router_b'], 'L1_ffn_expert_w': _L1_ffn_in['expert_w'], 'L1_ffn_expert_b': _L1_ffn_in['expert_b']}

def reference(x, L0_conv_Wf, L0_conv_bf, L0_conv_k0, L0_conv_k1, L0_conv_k2, L0_conv_Wh, L0_conv_bh, L0_conv_gamma, L0_conv_beta, L0_conv_Wp, L0_conv_bp, L0_ffn_W, L0_ffn_V, L0_ffn_gamma, L0_ffn_beta, L1_conv_in_w, L1_conv_conv_w, L1_conv_conv_b, L1_conv_x_w, L1_conv_dt_w, L1_conv_dt_b, L1_conv_A_log, L1_conv_D, L1_conv_out_w, L1_ffn_router_w, L1_ffn_router_b, L1_ffn_expert_w, L1_ffn_expert_b):
    import jax
    import jax.numpy as jnp

    def _L0_conv_ref(x, Wf, bf, k0, k1, k2, Wh, bh, gamma, beta, Wp, bp):
        import jax, jax.numpy as jnp
        import numpy as np
        B, H, W, C = (16, 24, 24, 32)
        FOCAL_LEVEL = 3
        FOCAL_WINDOW = 3
        FOCAL_FACTOR = 2
        LN_EPS = 0.001

        def dwconv_same(x, k):
            return jax.lax.conv_general_dilated(x, k, window_strides=(1, 1), padding='SAME', dimension_numbers=('NHWC', 'HWIO', 'NHWC'), feature_group_count=x.shape[-1])
        gelu = lambda t: jax.nn.gelu(t, approximate=False)
        y = jnp.einsum('bhwc,cd->bhwd', x, Wf) + bf
        q = y[..., :C]
        ctx = y[..., C:2 * C]
        gates = y[..., 2 * C:]
        ctx_all = jnp.zeros_like(ctx)
        for l, k in enumerate((k0, k1, k2)):
            ctx = gelu(dwconv_same(ctx, k))
            ctx_all = ctx_all + ctx * gates[..., l:l + 1]
        ctx_global = gelu(jnp.mean(ctx, axis=(1, 2), keepdims=True))
        ctx_all = ctx_all + ctx_global * gates[..., FOCAL_LEVEL:]
        modulator = jnp.einsum('bhwc,cd->bhwd', ctx_all, Wh) + bh
        x_out = q * modulator
        mu = jnp.mean(x_out, axis=-1, keepdims=True)
        var = jnp.mean(jnp.square(x_out - mu), axis=-1, keepdims=True)
        x_out = (x_out - mu) * jax.lax.rsqrt(var + LN_EPS) * gamma + beta
        x_out = jnp.einsum('bhwc,cd->bhwd', x_out, Wp) + bp
        return x_out

    def _L0_ffn_ref(x, W, V, gamma, beta):
        import jax, jax.numpy as jnp
        import numpy as np
        BN_EPS = 1e-05
        B, T, H = (x.shape[0], x.shape[1], W.shape[0])
        Wx = jnp.einsum('bti,hi->bth', x, W)
        flat = Wx.reshape(B * T, H)
        mean = jnp.mean(flat, axis=0)
        var = jnp.var(flat, axis=0)
        Wx = ((flat - mean) * jax.lax.rsqrt(var + BN_EPS) * gamma + beta).reshape(B, T, H)
        Vt = V.T

        def step(yt, wx_t):
            yt = jax.nn.sigmoid(wx_t + yt @ Vt)
            return (yt, yt)
        y0 = jnp.zeros((B, H), dtype=Wx.dtype)
        _, ys = jax.lax.scan(step, y0, jnp.swapaxes(Wx, 0, 1))
        return jnp.swapaxes(ys, 0, 1)

    def _L1_conv_ref(x, in_w, conv_w, conv_b, x_w, dt_w, dt_b, A_log, D, out_w):
        import jax, jax.numpy as jnp
        from jax import lax
        import numpy as np
        D_MODEL = 32
        D_STATE = 16
        D_CONV = 4
        EXPAND = 2
        D_INNER = EXPAND * D_MODEL
        DT_RANK = (D_MODEL + 15) // 16
        B, H, W = (2, 28, 28)

        def _mamba(x, in_w, conv_w, conv_b, x_w, dt_w, dt_b, A_log, D, out_w):
            Bn, L, _ = x.shape
            xz = x @ in_w.T
            xc, z = jnp.split(xz, 2, axis=-1)
            xt = jnp.transpose(xc, (0, 2, 1))
            xt = lax.conv_general_dilated(xt, conv_w[:, None, :], window_strides=(1,), padding=[(D_CONV - 1, 0)], feature_group_count=D_INNER)
            xt = xt + conv_b[None, :, None]
            xc = jax.nn.silu(jnp.transpose(xt, (0, 2, 1)))
            dbl = xc @ x_w.T
            dt, Bm, Cm = jnp.split(dbl, [DT_RANK, DT_RANK + D_STATE], axis=-1)
            dt = jax.nn.softplus(dt @ dt_w.T + dt_b)
            A = -jnp.exp(A_log)
            dA = jnp.exp(dt[..., None] * A)
            dBx = dt[..., None] * Bm[:, :, None, :] * xc[..., None]

            def step(h, inp):
                dA_t, dBx_t, C_t = inp
                h = dA_t * h + dBx_t
                y = jnp.einsum('bds,bs->bd', h, C_t)
                return (h, y)
            h0 = jnp.zeros((Bn, D_INNER, D_STATE), x.dtype)
            _, ys = lax.scan(step, h0, (jnp.swapaxes(dA, 0, 1), jnp.swapaxes(dBx, 0, 1), jnp.swapaxes(Cm, 0, 1)))
            y = jnp.swapaxes(ys, 0, 1) + xc * D
            y = y * jax.nn.silu(z)
            return y @ out_w.T
        Bn, Hn, Wn, C = x.shape
        x_flat = x.reshape(Bn, Hn * Wn, C)
        params = (in_w, conv_w, conv_b, x_w, dt_w, dt_b, A_log, D, out_w)
        y_fwd = _mamba(x_flat, *params)
        y_bwd = jnp.flip(_mamba(jnp.flip(x_flat, axis=1), *params), axis=1)
        return (y_fwd + y_bwd).reshape(Bn, Hn, Wn, C)

    def _L1_ffn_ref(x, router_w, router_b, expert_w, expert_b):
        import jax, jax.numpy as jnp
        import numpy as np
        B, N, D, C, E, K = (8, 2048, 32, 32, 8, 2)
        router_probs = jax.nn.softmax(x @ router_w + router_b, axis=-1)
        top_p, top_i = jax.lax.top_k(router_probs, K)
        top_p = top_p / jnp.sum(top_p, axis=-1, keepdims=True)
        expert_out = jnp.einsum('bnd,edc->bnec', x, expert_w) + expert_b
        gathered = jnp.take_along_axis(expert_out, top_i[..., None], axis=2)
        return jnp.einsum('bnk,bnkc->bnc', top_p, gathered)

    def _gn(v, G=32, eps=1e-05):
        B_, H_, W_, C_ = v.shape
        g = v.reshape(B_, H_, W_, G, C_ // G)
        m = jnp.mean(g, axis=(1, 2, 4), keepdims=True)
        s = jnp.var(g, axis=(1, 2, 4), keepdims=True)
        return ((g - m) / jnp.sqrt(s + eps)).reshape(v.shape)

    def _ln_c(v, eps=1e-06):
        m = jnp.mean(v, axis=-1, keepdims=True)
        s = jnp.var(v, axis=-1, keepdims=True)
        return (v - m) / jnp.sqrt(s + eps)

    def _ln_t(v, eps=1e-05):
        m = jnp.mean(v, axis=-1, keepdims=True)
        s = jnp.var(v, axis=-1, keepdims=True)
        return (v - m) / jnp.sqrt(s + eps)

    def _to_tokens(v):
        B_, H_, W_, C_ = v.shape
        return v.reshape(B_, H_ * W_, C_)

    def _from_tokens(t, like):
        return t.reshape(like.shape)
    x = x + _L0_conv_ref(_ln_c(x), L0_conv_Wf, L0_conv_bf, L0_conv_k0, L0_conv_k1, L0_conv_k2, L0_conv_Wh, L0_conv_bh, L0_conv_gamma, L0_conv_beta, L0_conv_Wp, L0_conv_bp)
    t = _to_tokens(x)
    t = t + _L0_ffn_ref(_ln_t(t), L0_ffn_W, L0_ffn_V, L0_ffn_gamma, L0_ffn_beta)
    x = _from_tokens(t, x)
    x = x + _L1_conv_ref(_ln_c(x), L1_conv_in_w, L1_conv_conv_w, L1_conv_conv_b, L1_conv_x_w, L1_conv_dt_w, L1_conv_dt_b, L1_conv_A_log, L1_conv_D, L1_conv_out_w)
    t = _to_tokens(x)
    t = t + _L1_ffn_ref(_ln_t(t), L1_ffn_router_w, L1_ffn_router_b, L1_ffn_expert_w, L1_ffn_expert_b)
    x = _from_tokens(t, x)
    return x

_drawn_inputs = setup_inputs


def setup_inputs(seed=0):
    import zlib

    import numpy as np

    out = dict(_drawn_inputs(seed))
    spreads = {'L0_conv_bf': (0.0, 0.1),
     'L0_conv_bh': (0.0, 0.1),
     'L0_conv_gamma': (1.0, 0.2),
     'L0_conv_beta': (0.0, 0.1),
     'L0_conv_bp': (0.0, 0.1),
     'L0_ffn_gamma': (1.0, 0.2),
     'L0_ffn_beta': (0.0, 0.1),
     'L1_conv_conv_b': (0.0, 0.434),
     'L1_conv_D': (1.0, 0.6),
     'L1_ffn_router_b': (0.0, 0.1),
     'L1_ffn_expert_b': (0.0, 0.1)}
    factors = {'L0_conv_k0': 8.0,
     'L0_conv_k1': 25.79,
     'L0_conv_k2': 47.564,
     'L0_conv_Wh': 8.0,
     'L1_conv_in_w': 4.674,
     'L1_conv_conv_w': 8.0,
     'L1_conv_x_w': 8.0,
     'L1_conv_dt_w': 35.673,
     'L1_conv_dt_b': 8.0,
     'L1_conv_A_log': 28.332,
     'L1_conv_out_w': 4.134}
    for name, (base, spread) in spreads.items():
        noise = np.random.default_rng([zlib.crc32(name.encode()), seed]).standard_normal(out[name].shape)
        drawn = base * np.exp(spread * noise) if base else spread * noise
        out[name] = jnp.asarray(drawn.astype(out[name].dtype))
    for name, factor in factors.items():
        out[name] = (out[name] * factor).astype(out[name].dtype)
    return out
```

```python
import numpy as np
import concourse.bass as bass
from concourse import mybir
from contextlib import ExitStack

B, H, W, C = 16, 24, 24, 32
L = H * W
HALF = L // 2
GROUPS = 4
J = B // GROUPS
N = J * L
LEVELS = 3
KS = [3, 5, 7]
TAP0 = [0, 9, 34]
TAPS = 83
PAD = 3
HP, WP = H + 2 * PAD, W + 2 * PAD
CHUNK = 24
CHUNKS = L // CHUNK
WARM = 16
DI, DS, DC = 64, 16, 4
T2 = B * L
DR = 2
XIW = L + DC - 1
EX = 8
TOK = 96
KT = L // TOK
NT = B * KT
BANK = 512

MAIN = [("ident", 128), ("cent", 128), ("meanj", 128), ("gavg", 128), ("fw", 128), ("vt", 128),
        ("inx", 128), ("inz", 128), ("xwd", 128), ("dtw", 128), ("xwb", 96), ("xwc", 96),
        ("outw", 32), ("rw", EX), ("rb", EX), ("ew", EX * C), ("eb", EX * C), ("convw", DC),
        ("convb", 1), ("dvec", 1), ("dtb", 1), ("alog", DS), ("fgam", 1), ("fbet", 1), ("ones", 1)]
FRONT = [("wctx", 128), ("wq", 128), ("wg0", 128), ("wg1", 128), ("wg2", 128), ("wg3", 128),
         ("wh", 128), ("wp", 128), ("taps", TAPS), ("bctx", 1), ("bq", 1), ("bg", 4), ("bh", 1),
         ("gamma", 1), ("beta", 1), ("bp", 1)]


def places(fields):
    at, out = 0, {}
    for name, width in fields:
        out[name] = slice(at, at + width)
        at += width
    return out, at


MAIN_AT, MAIN_W = places(MAIN)
FRONT_AT, FRONT_W = places(FRONT)


def build_program(nc, x_in, main_in, front_in, sel_in, out):
    f32, bf16, i32 = mybir.dt.float32, mybir.dt.bfloat16, mybir.dt.int32
    ALU, ACT, AX = mybir.AluOpType, mybir.ActivationFunctionType, mybir.AxisListType
    ctx = ExitStack()
    with ctx:
        def sb(name, shape, dt=f32):
            return ctx.enter_context(nc.sbuf_tensor(name, shape, dt))[:, :]

        def sem(name):
            return ctx.enter_context(nc.semaphore(name))

        PM = sb("main_params", [128, MAIN_W])
        SEL = sb("selectors", [3 * 2 * DS, DS * 128], bf16)
        X = sb("residual", [128, N])
        XN = sb("normed", [128, N])
        RING = sb("ring", [128, 8 * L])
        EPS = sb("eps", [128, 3])
        SM = sb("small", [128, 128])
        WDT = sb("w_dt", [128, 128])
        NEGI = sb("neg_ident", [96, 96], bf16)
        FLAG = sb("flag", [1, 1], i32)
        DECAYS = sb("decays", [128, 2 * L])
        BIG = sb("big", [128, 4 * T2])
        PS = ctx.enter_context(nc.psum_tensor("banks", [128, 8, BANK], f32))

        pos = [0]

        def big(cols):
            v = BIG[:, pos[0]:pos[0] + cols]
            pos[0] += cols
            assert pos[0] <= 4 * T2
            return v

        PF = big(FRONT_W)
        DIAG = big(TAPS * 128)
        CP = [big(J * HP * WP).rearrange("p (j h w) -> p j h w", j=J, h=HP) for _ in range(2)]
        QS = big(N)
        GS = [big(N) for _ in range(LEVELS + 1)]
        ACC = big(5 * HALF)
        ALLC = big(N)
        MT = big(N)
        XO = MT
        WPG = big(128)
        pos[0] = 0
        WX = big(N)
        YP = big(J * (L + 1)).rearrange("p (j t) -> p j t", j=J)
        ENDS = big(J * CHUNKS).rearrange("p (j c) -> p j c", j=J)
        DIFF = big(J * CHUNKS).rearrange("p (j c) -> p j c", j=J)
        SDIAG = big(128)
        pos[0] = 0
        XC = big(T2)
        DT = big(T2)
        DTX = big(T2)
        SB = big(T2 // 2).bitcast(bf16)
        SC = big(T2 // 2).bitcast(bf16)
        XI = BIG[:, T2:T2 + B * XIW].rearrange("p (b t) -> p b t", b=B)
        YG = DT
        GZ = DTX
        SP = DTX
        pos[0] = 0
        LG, PR, S1, S2, RST, CNT = (big(NT * EX) for _ in range(6))
        MROW = big(2 * NT)
        PROD = [big(2 * EX * C) for _ in range(4)]
        YT = big(NT * C)
        EBF = big(EX * C)
        EBS = big(EX * C // 2).bitcast(bf16)
        EBT = big(EX * C // 2).bitcast(bf16)
        ONB = big(TOK // 2).bitcast(bf16)
        SQ = [RING[:, i * L:(i + 1) * L] for i in range(2)]
        STD = [RING[:, (2 + i) * L:(3 + i) * L] for i in range(2)]
        SELF = RING[0:3 * 2 * DS, 4 * L:4 * L + DS * 128]
        BS = [RING[:, i * L:(i + 1) * L] for i in range(2)]
        U = [RING[:, (2 + i) * L:(3 + i) * L] for i in range(2)]
        HS = [RING[:, (4 + i) * L:(5 + i) * L] for i in range(2)]
        DECAY = [DECAYS[:, i * L:(i + 1) * L] for i in range(2)]
        HC = [RING[:, (6 + i) * L:(7 + i) * L] for i in range(2)]
        AEXP, ANEG = SM[:, 0:DS], SM[:, DS:2 * DS]
        GSUM, GGLOB, BPG = SM[:, 32:37], SM[:, 40:44], SM[:, 44:45]
        MV, MEX, MEXT = SM[:, 48:50], SM[:, 52:54], SM[:, 54:56]
        MSQ, VAR, SDEV, RSD, BSCALE, MS, BBIAS, NDIFF = (SM[:, 56 + i:57 + i] for i in range(8))
        STATS = SM[:, 64:64 + 48]

        C_PAIR = (0, 2)

        def par(name):
            return PM[:, MAIN_AT[name]]

        def fpar(name):
            return PF[:, FRONT_AT[name]]

        def pair(p, rows=slice(0, 128)):
            return PS[rows, 2 * p:2 * p + 2, 0:HALF]

        def img(t, j, rows=slice(0, 128)):
            return t[rows, j * L:(j + 1) * L].rearrange("p (a c) -> p a c", a=2)

        def pair_matmul(p, lhsT, rhs, at, rows=slice(0, 128), start=True, stop=True, again=False):
            for a in range(2):
                last = nc.tensor.matmul(PS[rows, 2 * p + a, 0:HALF], lhsT,
                                        rhs[:, bass.ds(at + a * HALF, HALF)], start=start, stop=stop,
                                        skip_group_check=again)
            return last

        x_loaded = [sem(f"x_loaded{j}") for j in range(J)]
        main_loaded, front_loaded, sel_loaded = sem("main_loaded"), sem("front_loaded"), sem("sel_loaded")
        sel_set, eps_set, negi_set = sem("sel_set"), sem("eps_set"), sem("negi_set")
        ln = [{k: sem(f"ln{n}_{k}") for k in ("cent", "sq", "var", "std", "rstd", "out")} for n in range(5)]
        pads_zero, diag_made = sem("pads_zero"), sem("diag_made")
        ctx_mm, ctx_set, lin_mm, lin_set = sem("ctx_mm"), sem("ctx_set"), sem("lin_mm"), sem("lin_set")
        tap_dve, tap_pe, gelu_set = sem("tap_dve"), sem("tap_pe"), sem("gelu_set")
        gated, ctx_sum = sem("gated"), sem("ctx_sum")
        glob_sum, glob_set, glob_added = sem("glob_sum"), sem("glob_set"), sem("glob_added")
        mod_mm, xo_set = sem("mod_mm"), sem("xo_set")
        wpg_set, bp_mm, bp_set = sem("wpg_set"), sem("bp_mm"), sem("bp_set")
        proj_mm, x1_set = sem("proj_mm"), sem("x1_set")
        wx_mm, wx_set, stats_set, stats_mm = sem("wx_mm"), sem("wx_set"), sem("stats_set"), sem("stats_mm")
        bn_step, var_set, sdev_set, sdiag_set = sem("bn_step"), sem("var_set"), sem("sdev_set"), sem("sdiag_set")
        y_zero, rec_mm, rec_y = sem("y_zero"), sem("rec_mm"), sem("rec_y")
        ends_saved, diff_step, ndiff_set = sem("ends_saved"), sem("diff_step"), sem("ndiff_set")
        count_mm, flag_set = sem("count_mm"), sem("flag_set")
        slow_mm, slow_y, rec_done, x2_set = sem("slow_mm"), sem("slow_y"), sem("rec_done"), sem("x2_set")
        xi_pad, in_mm, xi_set = sem("xi_pad"), sem("in_mm"), sem("xi_set")
        conv_step, xc_set = sem("conv_step"), sem("xc_set")
        aexp_set, a_set, wdt_mm, wdt_set = sem("aexp_set"), sem("a_set"), sem("wdt_mm"), sem("wdt_set")
        dt_mm, abs_set, v_set, sp_step, sp_set = sem("dt_mm"), sem("abs_set"), sem("v_set"), sem("sp_step"), sem("sp_set")
        dt_set, dtx_set = sem("dt_set"), sem("dtx_set")
        part_mm = [sem(f"part{i}_mm") for i in range(3)]
        part_set = [sem(f"part{i}_set") for i in range(3)]
        u_begun = sem("u_begun")
        bbc_mm, bbc_copied, u_set, decay_set, scanned = (sem("bbc_mm"), sem("bbc_copied"), sem("u_set"),
                                                         sem("decay_set"), sem("scanned"))
        cbc_mm, weighted, y_added, y_read = sem("cbc_mm"), sem("weighted"), sem("y_added"), sem("y_read")
        z_mm, z_set, yg_set, out_mm, x3_set = sem("z_mm"), sem("z_set"), sem("yg_set"), sem("out_mm"), sem("x3_set")
        lg_mm, lg_step, lg_sub, lg_exp, weights_set = (sem("lg_mm"), sem("lg_step"), sem("lg_sub"), sem("lg_exp"),
                                                       sem("weights_set"))
        eb_step, eb_set, ex_mm, ex_prod, ex_sum = sem("eb_step"), sem("eb_set"), sem("ex_mm"), sem("ex_prod"), sem("ex_sum")
        xt_mm, yt_set, stored = sem("xt_mm"), sem("yt_set"), sem("stored")

        DVE_PIECES = [(0, 0, H), (1, 0, H), (2, 0, H // 2)]
        PE_UNITS = [(2, H // 2, 2), (3, 0, 0), (3, H // 2, 1)]
        NP = 5
        GELU_OF = [1, 2, 4, 5]

        REC_STEPS = list(range(CHUNK - WARM, CHUNK)) + 2 * list(range(CHUNK))

        def inside(cp, j, r0=0, rows=H):
            return cp[:, j, PAD + r0:PAD + r0 + rows, PAD:PAD + W]

        def window(cp, l, tap, j, r0, rows):
            dy, dx = tap // KS[l] - KS[l] // 2, tap % KS[l] - KS[l] // 2
            return cp[:, j, PAD + r0 + dy:PAD + r0 + dy + rows, PAD + dx:PAD + dx + W]

        def rows_of(t, j, r0=0, rows=H):
            return t[:, j * L + r0 * W:j * L + (r0 + rows) * W].rearrange("p (h w) -> p h w", w=W)

        def ln_pe(pe, n, src, ready):
            s = ln[n]
            for j in range(J + 1):
                if j < J:
                    ready(j)
                    if j >= 2:
                        pe.wait_ge(s["out"], j - 1)
                    pair_matmul(j % 2, par("cent"), src, j * L).then_inc(s["cent"], 1)
                if j >= 1:
                    i = j - 1
                    pe.wait_ge(s["sq"], i + 1)
                    if i >= 2:
                        pe.wait_ge(s["std"], i - 1)
                    pair_matmul(2 + i % 2, par("meanj"), SQ[i % 2], 0).then_inc(s["var"], 1)

        def ln_act(act, n, eps):
            s = ln[n]
            for j in range(J + 1):
                if j < J:
                    act.wait_ge(s["cent"], j + 1)
                    if j >= 2:
                        act.wait_ge(s["var"], j - 1)
                    nc.scalar.activation(img(SQ[j % 2], 0), pair(j % 2), ACT.Square).then_inc(s["sq"], 1)
                if j >= 1:
                    i = j - 1
                    act.wait_ge(s["var"], i + 1)
                    if i >= 2:
                        act.wait_ge(s["out"], i - 1)
                    nc.scalar.activation(img(STD[i % 2], 0), pair(2 + i % 2), ACT.Sqrt,
                                         bias=EPS[:, eps:eps + 1]).then_inc(s["std"], 1)

        def ln_dve(dve, n, dst):
            s = ln[n]
            for j in range(J):
                dve.wait_ge(s["std"], j + 1)
                nc.vector.reciprocal(STD[j % 2], STD[j % 2]).then_inc(s["rstd"], 1)
                dve.wait_ge(s["rstd"], j + 1)
                nc.vector.tensor_tensor(img(dst, j), pair(j % 2), img(STD[j % 2], 0), ALU.mult).then_inc(s["out"], 1)

        def add_experts(dve, u):
            dve.wait_ge(ex_prod, u + 1)
            nc.vector.tensor_reduce(YT[0:TOK, 2 * u * C:(2 * u + 2) * C].rearrange("p (t c) -> p t c", t=2),
                                    PROD[u % 4][0:TOK, :].rearrange("p (t e c) -> p t c e", t=2, e=EX),
                                    AX.X, ALU.add).then_inc(ex_sum, 1)

        def finish_images(dve, v):
            dve.wait_ge(xt_mm, v + 1)
            dve.wait_ge(ex_sum, (v + 1) * KT)
            here = YT[0:TOK, v * 2 * KT * C:(v + 1) * 2 * KT * C]
            nc.vector.tensor_tensor(here, here, PS[0:TOK, 6 + v % 2, 0:2 * KT * C], ALU.add).then_inc(yt_set, 1)

        block = ctx.enter_context(nc.Block())

        @block.sync
        def _(sp):
            sp.dma_start(X[:, 0:L], x_in[:, 0:L]).then_inc(x_loaded[0], 16)
            sp.dma_start(PM[:, :], main_in).then_inc(main_loaded, 16)
            for j in range(1, J):
                sp.dma_start(X[:, j * L:(j + 1) * L], x_in[:, j * L:(j + 1) * L]).then_inc(x_loaded[j], 16)
            out_v = out.rearrange("(n p) c -> p n c", p=TOK)
            for b in range(0, B, 2):
                sp.wait_ge(yt_set, b // 2 + 1)
                sp.dma_start(out_v[:, b * KT:(b + 2) * KT, :],
                             YT[0:TOK, b * KT * C:(b + 2) * KT * C].rearrange("p (n c) -> p n c", c=C)).then_inc(stored, 16)
            sp.wait_ge(stored, 16 * (B // 2))

        @block.gpsimd
        def _(pool):
            pool.dma_start(PF, front_in).then_inc(front_loaded, 16)
            pool.dma_start(SELF, sel_in).then_inc(sel_loaded, 16)
            for cp in CP:
                nc.gpsimd.memset(cp, 0.0).then_inc(pads_zero, 1)
            pool.wait_ge(main_loaded, 16)
            pool.wait_ge(front_loaded, 16)
            for t in range(TAPS):
                nc.gpsimd.tensor_scalar(DIAG[:, t * 128:(t + 1) * 128], par("ident"),
                                        fpar("taps")[:, t:t + 1], None, ALU.mult).then_inc(diag_made, 1)
            pool.wait_ge(lin_set, 5 * J)
            for l in range(LEVELS):
                for j in range(J):
                    pool.wait_ge(gelu_set, NP * l + GELU_OF[j])
                    if l == 0:
                        nc.gpsimd.tensor_tensor(rows_of(ALLC, j), inside(CP[1], j), rows_of(GS[0], j),
                                                ALU.mult).then_inc(gated, 1)
                    else:
                        if l == 2:
                            pool.wait_ge(ctx_sum, j + 1)
                        nc.gpsimd.tensor_tensor(rows_of(MT, j), inside(CP[(l + 1) % 2], j), rows_of(GS[l], j),
                                                ALU.mult).then_inc(gated, 1)
                        pool.wait_ge(gated, J * l + j + 1)
                        nc.gpsimd.tensor_tensor(ALLC[:, j * L:(j + 1) * L], ALLC[:, j * L:(j + 1) * L],
                                                MT[:, j * L:(j + 1) * L], ALU.add).then_inc(ctx_sum, 1)
            pool.wait_ge(x2_set, J)
            nc.gpsimd.memset(XI[:, :, 0:DC - 1], 0.0).then_inc(xi_pad, 1)
            for b in range(B):
                pool.wait_ge(v_set, b + 1)
                pool.wait_ge(sp_set, b + 1)
                here = slice(b * L, (b + 1) * L)
                nc.gpsimd.tensor_tensor(DT[:, here], DT[:, here], SP[:, here], ALU.add).then_inc(dt_set, 1)
                pool.wait_ge(dt_set, b + 1)
                nc.gpsimd.tensor_tensor(DTX[:, here], DT[:, here], XC[:, here], ALU.mult).then_inc(dtx_set, 1)
            pool.wait_ge(dtx_set, B)
            pool.sem_inc(u_set, 2)
            with pool.Fori(0, B) as b:
                for s in range(DS):
                    pool.wait_ge(scanned, b * DS + (s + 1))
                    pool.wait_ge(bbc_copied, b * DS + (s + 2))
                    pool.sem_inc(u_begun, 1)
                    nc.gpsimd.tensor_tensor(U[s % 2], DTX[:, bass.ds(b * L, L)], BS[s % 2], ALU.mult).then_inc(u_set, 1)

        @block.scalar
        def _(act):
            act.wait_ge(eps_set, 3)
            ln_act(act, 0, 0)
            act.wait_ge(front_loaded, 16)
            act.wait_ge(pads_zero, 2)
            for j in range(J):
                act.wait_ge(ctx_mm, j + 1)
                for a in range(2):
                    last = nc.scalar.activation(inside(CP[0], j, a * H // 2, H // 2),
                                                PS[:, 2 * (j % 2) + a, 0:HALF].rearrange("p (h w) -> p h w", w=W),
                                                ACT.Identity, bias=fpar("bctx"))
                last.then_inc(ctx_set, 1)
            for i in range(5 * J):
                m, j = i // J, i % J
                act.wait_ge(lin_mm, i + 1)
                dst = QS if m == 0 else GS[m - 1]
                bias = fpar("bq") if m == 0 else fpar("bg")[:, m - 1:m]
                nc.scalar.activation(img(dst, j), pair(2 + i % 2), ACT.Identity, bias=bias).then_inc(lin_set, 1)
            for l in range(LEVELS):
                dst = CP[(l + 1) % 2]
                if l == 2:
                    act.wait_ge(gated, J)
                for i, (j, r0, rows) in enumerate(DVE_PIECES):
                    act.wait_ge(tap_dve, 3 * (TAP0[l] + KS[l] ** 2 - 1) + i + 1)
                    acc = ACC[:, j * L:j * L + rows * W].rearrange("p (h w) -> p h w", w=W)
                    nc.scalar.activation(inside(dst, j, r0, rows), acc, ACT.Gelu,
                                         accum_out=GSUM[:, i:i + 1] if l == 2 else None).then_inc(gelu_set, 1)
                act.wait_ge(tap_pe, 2 * l + 1)
                nc.scalar.activation(inside(dst, 2, H // 2, H // 2), PS[:, 2, 0:HALF].rearrange("p (h w) -> p h w", w=W),
                                     ACT.Gelu, accum_out=GSUM[:, 4:5] if l == 2 else None).then_inc(gelu_set, 1)
                act.wait_ge(tap_pe, 2 * l + 2)
                nc.scalar.activation(inside(dst, 3).rearrange("p (a h) w -> p a h w", a=2),
                                     pair(0).rearrange("p a (h w) -> p a h w", w=W),
                                     ACT.Gelu, accum_out=GSUM[:, 3:4] if l == 2 else None).then_inc(gelu_set, 1)
            act.wait_ge(glob_sum, 1)
            nc.scalar.activation(GGLOB, GSUM[:, 0:4], ACT.Gelu, scale=1.0 / L).then_inc(glob_set, 1)
            ln_act(act, 1, 1)
            ln_act(act, 2, 2)
            for j in range(J):
                act.wait_ge(wx_mm, j + 1)
                nc.scalar.activation(img(WX, j), pair(j), ACT.Copy).then_inc(wx_set, 1)
            act.wait_ge(var_set, 1)
            nc.scalar.activation(SDEV, VAR, ACT.Sqrt, bias=EPS[:, 2:3]).then_inc(sdev_set, 1)
            act.wait_ge(sdiag_set, 1)

            def recur(k):
                return nc.scalar.activation(YP[:, :, k + 1:k + 2 + CHUNK * (CHUNKS - 1):CHUNK],
                                            PS[:, k % 2, 0:J * CHUNKS].rearrange("p (j c) -> p j c", j=J),
                                            ACT.Sigmoid, bias=BBIAS)

            for q, k in enumerate(REC_STEPS):
                act.wait_ge(rec_mm, q + 1)
                if q == len(REC_STEPS) - 1:
                    act.wait_ge(ends_saved, 1)
                recur(k).then_inc(rec_y, 1)
            act.wait_ge(flag_set, 1)
            moved = act.value_load(FLAG[0:1, 0:1], min_val=0, max_val=1)
            with act.If(moved == 1):
                act.sem_inc(slow_y, 1)
                with act.Fori(0, CHUNKS - 2) as p:
                    for k in range(CHUNK):
                        act.wait_ge(slow_mm, p * CHUNK + (k + 1))
                        recur(k).then_inc(slow_y, 1)
                act.wait_ge(slow_y, (CHUNKS - 2) * CHUNK + 1)
            act.sem_inc(rec_done, 1)
            ln_act(act, 3, 0)
            act.wait_ge(main_loaded, 16)
            for b in range(B):
                act.wait_ge(in_mm, b + 1)
                nc.scalar.activation(XI[0:64, b, DC - 1:].rearrange("p (a c) -> p a c", a=2),
                                     pair(b % 4, slice(0, 64)), ACT.Copy).then_inc(xi_set, 1)
                nc.scalar.activation(XI[64:128, b, DC - 1:][:, ::-1].rearrange("p (a c) -> p a c", a=2),
                                     pair(b % 4, slice(64, 128)), ACT.Copy).then_inc(xi_set, 1)
                if b >= 1:
                    act.wait_ge(conv_step, DC * b)
                    prev = XC[:, (b - 1) * L:b * L]
                    nc.scalar.activation(prev, prev, ACT.Silu, bias=par("convb")).then_inc(xc_set, 1)
            act.wait_ge(conv_step, DC * B)
            nc.scalar.activation(XC[:, (B - 1) * L:], XC[:, (B - 1) * L:], ACT.Silu, bias=par("convb")).then_inc(xc_set, 1)
            nc.scalar.activation(AEXP, par("alog"), ACT.Exp).then_inc(aexp_set, 1)
            for b in range(B):
                sp_b = SP[:, b * L:(b + 1) * L]
                act.wait_ge(dt_mm, b + 1)
                nc.scalar.activation(img(SP, b), pair(0), ACT.Abs, bias=par("dtb")).then_inc(abs_set, 1)
                for c in (2 * b, 2 * b + 1):
                    act.wait_ge(part_mm[0], c + 1)
                    nc.scalar.activation(img((SB, SC)[c % 2], b, slice(0, 96)), pair(1 + c % 3, slice(0, 96)),
                                         ACT.Copy).then_inc(part_set[0], 1)
                    if c % 2 == 0:
                        act.wait_ge(abs_set, b + 1)
                        nc.scalar.activation(sp_b, sp_b, ACT.Exp, scale=-1.0).then_inc(sp_step, 1)
            for b in range(B):
                sp_b = SP[:, b * L:(b + 1) * L]
                act.wait_ge(sp_step, b + 1)
                nc.scalar.activation(sp_b, sp_b, ACT.Ln, bias=1.0).then_inc(sp_set, 1)
            act.wait_ge(a_set, 1)
            act.wait_ge(dt_set, B)
            act.wait_ge(part_set[2], 2 * B)
            act.sem_inc(bbc_copied, 1)

            def copy_b(i, s):
                act.wait_ge(bbc_mm, i + 1)
                act.wait_ge(u_set, i + 1)
                nc.scalar.activation(img(BS[s % 2], 0), pair(1), ACT.Copy).then_inc(bbc_copied, 1)

            def decay(b, s, i):
                act.wait_ge(a_set, 1)
                act.wait_ge(scanned, i + 1)
                nc.scalar.activation(DECAY[s % 2], DT[:, bass.ds(b * L, L)], ACT.Exp,
                                     scale=ANEG[:, s:s + 1]).then_inc(decay_set, 1)

            copy_b(0, 0)
            copy_b(1, 1)
            decay(0, 0, 0)
            with act.Fori(0, B - 1) as b:
                for s in range(DS):
                    copy_b(b * DS + (s + 2), s)
                    decay(b + (s + 1) // DS, (s + 1) % DS, b * DS + (s + 1))
            for s in range(DS - 1):
                if s + 2 < DS:
                    copy_b((B - 1) * DS + s + 2, s)
                decay(B - 1, s + 1, (B - 1) * DS + s + 1)
            for i in range(B):
                j, b = i // GROUPS, (i % GROUPS) * J + i // GROUPS
                act.wait_ge(z_mm, i + 1)
                nc.scalar.activation(img(GZ, b), pair(i % 2), ACT.Silu).then_inc(z_set, 1)
            ln_act(act, 4, 2)
            act.wait_ge(lg_sub, 1)
            nc.scalar.activation(LG[0:TOK, :], LG[0:TOK, :], ACT.Exp).then_inc(lg_exp, 1)

        @block.vector
        def _(dve):
            for i, eps in enumerate((1e-6, 1e-3, 1e-5)):
                nc.vector.memset(EPS[:, i:i + 1], eps).then_inc(eps_set, 1)
            dve.wait_ge(sel_loaded, 16)
            nc.vector.tensor_copy(SEL[:, :], SELF).then_inc(sel_set, 1)
            dve.wait_ge(main_loaded, 16)
            nc.vector.tensor_scalar(NEGI[:, :], par("ident")[0:96, 0:96], -1.0, None, ALU.mult).then_inc(negi_set, 1)
            ln_dve(dve, 0, XN)
            dve.wait_ge(front_loaded, 16)
            for l in range(LEVELS):
                src = CP[l % 2]
                for t in range(KS[l] ** 2):
                    for i, (j, r0, rows) in enumerate(DVE_PIECES):
                        if t == 0 and l == 0:
                            dve.wait_ge(ctx_set, j + 1)
                        elif t == 0:
                            dve.wait_ge(gelu_set, NP * (l - 1) + GELU_OF[j])
                        n = 3 * (TAP0[l] + t) + i
                        acc = ACC[:, j * L:j * L + rows * W].rearrange("p (h w) -> p h w", w=W)
                        win = window(src, l, t, j, r0, rows)
                        tap = fpar("taps")[:, TAP0[l] + t:TAP0[l] + t + 1]
                        if t == 0:
                            nc.vector.tensor_scalar(acc, win, tap, None, ALU.mult).then_inc(tap_dve, 1)
                        else:
                            dve.wait_ge(tap_dve, n - 2)
                            nc.vector.scalar_tensor_tensor(out=acc, in0=win, scalar=tap, in1=acc, op0=ALU.mult,
                                                           op1=ALU.add).then_inc(tap_dve, 1)
            dve.wait_ge(gelu_set, NP * LEVELS)
            nc.vector.tensor_tensor(GSUM[:, 2:3], GSUM[:, 2:3], GSUM[:, 4:5], ALU.add).then_inc(glob_sum, 1)
            nc.vector.tensor_scalar(WPG, fpar("wp"), fpar("gamma"), None, ALU.mult).then_inc(wpg_set, 1)
            dve.wait_ge(glob_set, 1)
            for j in range(J):
                dve.wait_ge(ctx_sum, J * (LEVELS - 2) + j + 1)
                here = slice(j * L, (j + 1) * L)
                nc.vector.scalar_tensor_tensor(out=ALLC[:, here], in0=GS[LEVELS][:, here], scalar=GGLOB[:, j:j + 1],
                                               in1=ALLC[:, here], op0=ALU.mult, op1=ALU.add).then_inc(glob_added, 1)
            for j in range(J):
                dve.wait_ge(mod_mm, j + 1)
                nc.vector.scalar_tensor_tensor(out=img(XO, j), in0=pair(j), scalar=fpar("bh"), in1=img(QS, j),
                                               op0=ALU.add, op1=ALU.mult).then_inc(xo_set, 1)
            ln_dve(dve, 1, XN)
            dve.wait_ge(bp_mm, 1)
            nc.vector.tensor_tensor(BPG, PS[:, 7, 0:1], fpar("bp"), ALU.add).then_inc(bp_set, 1)
            dve.wait_ge(bp_set, 1)
            for j in range(J):
                dve.wait_ge(proj_mm, j + 1)
                nc.vector.scalar_tensor_tensor(out=img(X, j), in0=pair(j), scalar=BPG, in1=img(X, j),
                                               op0=ALU.add, op1=ALU.add).then_inc(x1_set, 1)
            ln_dve(dve, 2, XN)
            nc.vector.memset(YP[:, :, 0:1], 0.0).then_inc(y_zero, 1)
            nc.vector.memset(YP[:, :, CHUNK - WARM:L:CHUNK], 0.0).then_inc(y_zero, 1)
            for i in range(2 * J):
                dve.wait_ge(wx_set, i // 2 + 1)
                nc.vector.bn_stats(STATS[:, 6 * i:6 * i + 6], WX[:, i * HALF:(i + 1) * HALF]).then_inc(stats_set, 1)
            dve.wait_ge(stats_set, 2 * J)
            steps = [0]

            def step(ins):
                steps[0] += 1
                ins.then_inc(bn_step, 1)
                dve.wait_ge(bn_step, steps[0])

            step(nc.vector.bn_aggr(MV, STATS))
            step(nc.vector.tensor_copy(MEX[:, 0:1], MV[:, 0:1]))
            step(nc.vector.scalar_tensor_tensor(out=MEX[:, 1:2], in0=MV[:, 0:1], scalar=MV[:, 0:1], in1=MV[:, 1:2],
                                                op0=ALU.mult, op1=ALU.add))
            dve.wait_ge(stats_mm, 1)
            step(nc.vector.tensor_copy(MEXT, PS[:, 7, 0:2]))
            step(nc.vector.tensor_tensor(MSQ, MEXT[:, 0:1], MEXT[:, 0:1], ALU.mult))
            nc.vector.tensor_tensor(VAR, MEXT[:, 1:2], MSQ, ALU.subtract).then_inc(var_set, 1)
            dve.wait_ge(sdev_set, 1)
            step(nc.vector.reciprocal(RSD, SDEV))
            step(nc.vector.tensor_tensor(BSCALE, RSD, par("fgam"), ALU.mult))
            step(nc.vector.tensor_tensor(MS, MEXT[:, 0:1], BSCALE, ALU.mult))
            step(nc.vector.tensor_tensor(BBIAS, par("fbet"), MS, ALU.subtract))
            nc.vector.tensor_scalar(SDIAG, par("ident"), BSCALE, None, ALU.mult).then_inc(sdiag_set, 1)
            ends = YP[:, :, CHUNK:L + 1:CHUNK]
            dve.wait_ge(rec_y, len(REC_STEPS) - CHUNK)
            nc.vector.tensor_copy(ENDS, ends).then_inc(ends_saved, 1)
            dve.wait_ge(rec_y, len(REC_STEPS))
            nc.vector.tensor_tensor(DIFF, ends, ENDS, ALU.not_equal).then_inc(diff_step, 1)
            dve.wait_ge(diff_step, 1)
            nc.vector.tensor_reduce(NDIFF, DIFF, AX.XY, ALU.max).then_inc(ndiff_set, 1)
            dve.wait_ge(count_mm, 1)
            nc.vector.tensor_scalar(FLAG[0:1, 0:1], PS[0:1, 2, 0:1], 1.0, None, ALU.min).then_inc(flag_set, 1)
            for j in range(J):
                dve.wait_ge(rec_done, 1)
                nc.vector.tensor_tensor(X[:, j * L:(j + 1) * L], X[:, j * L:(j + 1) * L], YP[:, j, 1:L + 1],
                                        ALU.add).then_inc(x2_set, 1)
            ln_dve(dve, 3, XN)
            dve.wait_ge(xi_pad, 1)
            for b in range(B):
                dve.wait_ge(xi_set, 2 * (b + 1))
                dst = XC[:, b * L:(b + 1) * L]
                for k in range(DC):
                    tap = par("convw")[:, k:k + 1]
                    if k == 0:
                        nc.vector.tensor_scalar(dst, XI[:, b, 0:L], tap, None, ALU.mult).then_inc(conv_step, 1)
                    else:
                        dve.wait_ge(conv_step, DC * b + k)
                        nc.vector.scalar_tensor_tensor(out=dst, in0=XI[:, b, k:k + L], scalar=tap, in1=dst,
                                                       op0=ALU.mult, op1=ALU.add).then_inc(conv_step, 1)
            dve.wait_ge(wdt_mm, 1)
            nc.vector.tensor_copy(WDT[:, :], PS[:, 0, 0:128]).then_inc(wdt_set, 1)
            dve.wait_ge(aexp_set, 1)
            nc.vector.tensor_scalar(ANEG, AEXP, -1.0, None, ALU.mult).then_inc(a_set, 1)
            for q in range(2 * B + 2):
                if q < 2 * B and q % 2 == 0:
                    b = q // 2
                    dve.wait_ge(dt_mm, b + 1)
                    dve.wait_ge(abs_set, b + 1)
                    nc.vector.tensor_scalar(img(DT, b), pair(0), par("dtb"), 0.0, ALU.add, ALU.max).then_inc(v_set, 1)
                if 1 <= q <= 2 * B:
                    c = q - 1
                    dve.wait_ge(part_mm[1], c + 1)
                    nc.vector.tensor_copy(img((SB, SC)[c % 2], c // 2, slice(0, 64)),
                                          pair(1 + c % 3, slice(0, 64))).then_inc(part_set[1], 1)
                if q >= 2:
                    c = q - 2
                    dve.wait_ge(part_mm[2], c + 1)
                    nc.vector.tensor_copy(img((SB, SC)[c % 2], c // 2, slice(0, 32)),
                                          pair(1 + c % 3, slice(0, 32))).then_inc(part_set[2], 1)
            dve.wait_ge(part_set[2], 2 * B)
            dve.sem_inc(scanned, 2)
            dve.sem_inc(weighted, 2)
            dve.sem_inc(y_read, 1)

            def scan(b, s):
                dve.wait_ge(decay_set, b * DS + (s + 1))
                dve.wait_ge(u_set, b * DS + (s + 3))
                dve.wait_ge(weighted, b * DS + (s + 1))
                nc.vector.tensor_tensor_scan(HS[s % 2], DECAY[s % 2], U[s % 2], 0.0, ALU.mult, ALU.add).then_inc(scanned, 1)

            def weigh(b, s):
                dve.wait_ge(cbc_mm, b * DS + (s + 1))
                dve.wait_ge(scanned, b * DS + (s + 3))
                dve.wait_ge(y_added, b * DS + (s + 1))
                nc.vector.tensor_tensor(img(HC[s % 2], 0), img(HS[s % 2], 0), pair(C_PAIR[s % 2]),
                                        ALU.mult).then_inc(weighted, 1)

            def read_y(b):
                dve.wait_ge(y_added, b * DS + (DS + 2))
                xc = XC[:, bass.ds(b * L, L)].rearrange("p (a c) -> p a c", a=2)
                nc.vector.scalar_tensor_tensor(out=xc, in0=xc, scalar=par("dvec"), in1=pair(3), op0=ALU.mult,
                                               op1=ALU.add).then_inc(y_read, 1)

            for s in range(DS):
                scan(0, s)
                if s >= 1:
                    weigh(0, s - 1)
            with dve.Fori(1, B) as b:
                for s in range(DS):
                    scan(b, s)
                    if s == 2:
                        read_y(b - 1)
                    weigh(b, s - 1)
            weigh(B - 1, DS - 1)
            read_y(B - 1)
            dve.wait_ge(y_read, B + 1)
            for i in range(B + 2):
                if i % GROUPS == 1 and i > GROUPS:
                    j = i // GROUPS - 1
                    dve.wait_ge(out_mm, GROUPS * (j + 1))
                    nc.vector.tensor_tensor(img(X, j), pair(2 + j % 2), img(X, j), ALU.add).then_inc(x3_set, 1)
                if i >= B:
                    continue
                b = (i % GROUPS) * J + i // GROUPS
                here = slice(b * L, (b + 1) * L)
                dve.wait_ge(z_set, i + 1)
                nc.vector.tensor_tensor(YG[0:64, here], XC[0:64, here], GZ[0:64, here], ALU.mult).then_inc(yg_set, 1)
                nc.vector.tensor_tensor(YG[64:128, here], XC[64:128, here][:, ::-1], GZ[64:128, here],
                                        ALU.mult).then_inc(yg_set, 1)
            ln_dve(dve, 4, XN)
            n_lg = [0]

            def lstep(ins):
                n_lg[0] += 1
                ins.then_inc(lg_step, 1)
                dve.wait_ge(lg_step, n_lg[0])

            def t3(t):
                return t[0:TOK, :].rearrange("p (n e) -> p n e", e=EX)

            def over(t):
                return t.unsqueeze(2).to_broadcast([TOK, NT, EX])

            m = MROW[0:TOK, 0:NT]
            lstep(nc.vector.memset(RST[0:TOK, :], 1.0))
            lstep(nc.vector.memset(t3(RST)[:, :, 0:1], 0.0))
            dve.wait_ge(lg_mm, 1)
            rb = par("rb")[0:TOK, :].unsqueeze(1).to_broadcast([TOK, NT // GROUPS, EX])
            for g in range(GROUPS):
                lstep(nc.vector.tensor_tensor(t3(LG)[:, g * NT // GROUPS:(g + 1) * NT // GROUPS, :],
                                              PS[0:TOK, g, 0:NT // GROUPS * EX].rearrange("p (n e) -> p n e", e=EX), rb, ALU.add))
            lstep(nc.vector.tensor_reduce(m, t3(LG), AX.X, ALU.max))
            nc.vector.tensor_tensor(t3(LG), t3(LG), over(m), ALU.subtract).then_inc(lg_sub, 1)
            dve.wait_ge(lg_exp, 1)
            lstep(nc.vector.tensor_reduce(m, t3(LG), AX.X, ALU.add))
            lstep(nc.vector.reciprocal(m, m))
            lstep(nc.vector.tensor_tensor(t3(PR), t3(LG), over(m), ALU.mult))

            def first_largest(probs, sel, best):
                lstep(nc.vector.tensor_reduce(best, t3(probs), AX.X, ALU.max))
                lstep(nc.vector.tensor_tensor(t3(sel), t3(probs), over(best), ALU.is_equal))
                lstep(nc.vector.tensor_tensor_scan(CNT[0:TOK, :], RST[0:TOK, :], sel[0:TOK, :], 0.0, ALU.mult, ALU.add))
                lstep(nc.vector.scalar_tensor_tensor(out=sel[0:TOK, :], in0=CNT[0:TOK, :], scalar=1.0, in1=sel[0:TOK, :],
                                                     op0=ALU.is_equal, op1=ALU.mult))

            first_largest(PR, S1, m)
            m2 = MROW[0:TOK, NT:2 * NT]
            lstep(nc.vector.scalar_tensor_tensor(out=LG[0:TOK, :], in0=S1[0:TOK, :], scalar=-2.0, in1=PR[0:TOK, :],
                                                 op0=ALU.mult, op1=ALU.add))
            first_largest(LG, S2, m2)
            lstep(nc.vector.tensor_tensor(S1[0:TOK, :], S1[0:TOK, :], S2[0:TOK, :], ALU.add))
            lstep(nc.vector.tensor_tensor(S1[0:TOK, :], S1[0:TOK, :], PR[0:TOK, :], ALU.mult))
            lstep(nc.vector.tensor_tensor(m, m, m2, ALU.add))
            lstep(nc.vector.reciprocal(m, m))
            nc.vector.tensor_tensor(t3(PR), t3(S1), over(m), ALU.mult).then_inc(weights_set, 1)
            nc.vector.memset(ONB[0:TOK, :], 1.0).then_inc(eb_step, 1)
            n_eb = [1]

            def estep(ins):
                n_eb[0] += 1
                ins.then_inc(eb_step, 1)
                dve.wait_ge(eb_step, n_eb[0])

            eb = par("eb")
            estep(nc.vector.tensor_copy(EBS[0:96, :], eb[0:96, :]))
            estep(nc.vector.tensor_tensor(EBF[0:96, :], eb[0:96, :], EBS[0:96, :], ALU.subtract))
            estep(nc.vector.tensor_copy(EBT[0:96, :], EBF[0:96, :]))
            estep(nc.vector.tensor_copy(EBS[32:64, :], EBF[32:64, :]))
            estep(nc.vector.tensor_tensor(EBF[0:96, :], EBF[0:96, :], EBT[0:96, :], ALU.subtract))
            nc.vector.tensor_copy(EBS[64:96, :], EBF[64:96, :]).then_inc(eb_set, 1)
            dve.wait_ge(weights_set, 1)
            for u in range(NT // 2):
                dve.wait_ge(ex_mm, u + 1)
                prod = PROD[u % 4][0:TOK, :].rearrange("p (t e c) -> p t e c", t=2, e=EX)
                wts = t3(PR)[:, 2 * u:2 * u + 2, :].unsqueeze(3).to_broadcast([TOK, 2, EX, C])
                if u >= 4:
                    dve.wait_ge(ex_sum, u - 3)
                nc.vector.tensor_tensor(prod, PS[0:TOK, 2 + u % 4, :].rearrange("p (t e c) -> p t e c", t=2, e=EX),
                                        wts, ALU.mult).then_inc(ex_prod, 1)
                if u >= 1:
                    add_experts(dve, u - 1)
                if u >= 1 and u % KT == 0:
                    finish_images(dve, u // KT - 1)
            add_experts(dve, NT // 2 - 1)
            finish_images(dve, B // 2 - 1)

        @block.tensor
        def _(pe):
            def after(semaphore, value):
                return lambda j: pe.wait_ge(semaphore, value) if j == 0 else None

            pe.wait_ge(main_loaded, 16)
            ln_pe(pe, 0, X, lambda j: pe.wait_ge(x_loaded[j], 16))
            pe.wait_ge(front_loaded, 16)
            pe.wait_ge(ln[0]["out"], J)
            for j in range(J):
                if j >= 2:
                    pe.wait_ge(ctx_set, j - 1)
                pair_matmul(j % 2, fpar("wctx"), XN, j * L).then_inc(ctx_mm, 1)
            for i in range(5 * J):
                m, j = i // J, i % J
                if i >= 2:
                    pe.wait_ge(lin_set, i - 1)
                pair_matmul(2 + i % 2, fpar(["wq", "wg0", "wg1", "wg2", "wg3"][m]), XN, j * L).then_inc(lin_mm, 1)
            pe.wait_ge(ctx_set, J)
            for l in range(LEVELS):
                if l >= 1:
                    pe.wait_ge(gelu_set, NP * l)
                taps = KS[l] ** 2
                for t in range(taps):
                    pe.wait_ge(diag_made, TAP0[l] + t + 1)
                    for j, r0, bank in PE_UNITS:
                        last = nc.tensor.matmul(PS[:, bank, 0:HALF], DIAG[:, (TAP0[l] + t) * 128:(TAP0[l] + t + 1) * 128],
                                                window(CP[l % 2], l, t, j, r0, H // 2), start=t == 0, stop=t == taps - 1)
                        if t == taps - 1 and bank != 0:
                            last.then_inc(tap_pe, 1)
            pe.wait_ge(lin_set, 5 * J)
            for j in range(J):
                pe.wait_ge(glob_added, j + 1)
                pair_matmul(j, fpar("wh"), ALLC, j * L).then_inc(mod_mm, 1)
            ln_pe(pe, 1, XO, after(xo_set, J))
            pe.wait_ge(ln[1]["out"], J)
            nc.tensor.matmul(PS[:, 7, 0:1], fpar("wp"), fpar("beta"), start=True, stop=True).then_inc(bp_mm, 1)
            pe.wait_ge(wpg_set, 1)
            pe.wait_ge(bp_set, 1)
            for j in range(J):
                pair_matmul(j, WPG, XN, j * L).then_inc(proj_mm, 1)
            ln_pe(pe, 2, X, after(x1_set, J))
            pe.wait_ge(ln[2]["out"], J)
            for j in range(J):
                pair_matmul(j, par("fw"), XN, j * L).then_inc(wx_mm, 1)
            pe.wait_ge(wx_set, J)
            pe.wait_ge(bn_step, 3)
            nc.tensor.matmul(PS[:, 7, 0:2], par("gavg"), MEX, start=True, stop=True).then_inc(stats_mm, 1)
            pe.wait_ge(sdiag_set, 1)
            pe.wait_ge(y_zero, 2)

            def drive(k):
                return nc.tensor.matmul(PS[:, k % 2, 0:J * CHUNKS], SDIAG,
                                        WX.rearrange("p (j c k) -> p j c k", j=J, k=CHUNK)[:, :, :, k],
                                        start=True, stop=False)

            def feed(k):
                return nc.tensor.matmul(PS[:, k % 2, 0:J * CHUNKS], par("vt"),
                                        YP[:, :, k:k + 1 + CHUNK * (CHUNKS - 1):CHUNK], start=False, stop=True)

            drive(REC_STEPS[0])
            for q, k in enumerate(REC_STEPS):
                if q >= 1:
                    pe.wait_ge(rec_y, q)
                feed(k).then_inc(rec_mm, 1)
                if q + 1 < len(REC_STEPS):
                    drive(REC_STEPS[q + 1])
            pe.wait_ge(ndiff_set, 1)
            nc.tensor.matmul(PS[0:1, 2, 0:1], NDIFF, par("ones"), start=True, stop=True).then_inc(count_mm, 1)
            pe.wait_ge(flag_set, 1)
            moved = pe.value_load(FLAG[0:1, 0:1], min_val=0, max_val=1)
            with pe.If(moved == 1):
                with pe.Fori(0, CHUNKS - 2) as p:
                    for k in range(CHUNK):
                        pe.wait_ge(slow_y, p * CHUNK + (k + 1))
                        drive(k)
                        feed(k).then_inc(slow_mm, 1)
            ln_pe(pe, 3, X, after(x2_set, J))
            pe.wait_ge(ln[3]["out"], J)
            for b in range(B):
                g, j = b // J, b % J
                rows = slice(C * g, C * (g + 1))
                if b >= 4:
                    pe.wait_ge(xi_set, 2 * (b - 3))
                pair_matmul(b % 4, par("inx")[rows, :], XN[rows, :], j * L).then_inc(in_mm, 1)
            pe.wait_ge(xi_set, 2 * B)
            nc.tensor.matmul(PS[:, 0, 0:128], par("xwd")[0:4, :], par("dtw")[0:4, :], start=True, stop=True).then_inc(wdt_mm, 1)
            pe.wait_ge(wdt_set, 1)
            pe.wait_ge(negi_set, 1)
            for q in range(2 * B + 2):
                if q < 2 * B:
                    b = q // 2
                    if q % 2 == 0:
                        pe.wait_ge(xc_set, b + 1)
                        if b >= 1:
                            pe.wait_ge(v_set, b)
                        pair_matmul(0, WDT, XC, b * L).then_inc(dt_mm, 1)
                    if q >= 3:
                        pe.wait_ge(part_set[2], q - 2)
                    pair_matmul(1 + q % 3, par(("xwb", "xwc")[q % 2]), XC, b * L, slice(0, 96)).then_inc(part_mm[0], 1)
                for i in (1, 2):
                    c = q - i
                    if 0 <= c < 2 * B:
                        pe.wait_ge(part_set[i - 1], c + 1)
                        pair_matmul(1 + c % 3, NEGI, (SB, SC)[c % 2][0:96, :], (c // 2) * L, slice(0, 96),
                                    start=False, again=True).then_inc(part_mm[i], 1)
            pe.wait_ge(sel_set, 1)
            pe.wait_ge(part_set[2], 2 * B)
            pe.sem_inc(y_added, 2)

            def spread_b(b, s):
                pe.wait_ge(bbc_copied, b * DS + (s + 1))
                pair_matmul(1, SEL[:, s * 128:(s + 1) * 128], SB[0:96, :], b * L).then_inc(bbc_mm, 1)

            def spread_c(b, s):
                pe.wait_ge(weighted, b * DS + (s + 1))
                pair_matmul(C_PAIR[s % 2], SEL[:, s * 128:(s + 1) * 128], SC[0:96, :], b * L).then_inc(cbc_mm, 1)

            def add_state(b, s):
                pe.wait_ge(weighted, b * DS + (s + 3))
                if s == 0:
                    pe.wait_ge(y_read, b + 1)
                pair_matmul(3, par("ident"), HC[s % 2], 0, start=s == 0, stop=s == DS - 1).then_inc(y_added, 1)

            def states(b, first=False, last=False):
                for s in range(DS):
                    spread_c(b, s)
                    if s >= 2:
                        add_state(b, s - 2)
                    elif not first:
                        add_state(b - 1, DS - 2 + s)
                    if s + 3 < DS:
                        spread_b(b, s + 3)
                    elif not last:
                        spread_b(b + 1, s + 3 - DS)

            for s in range(3):
                spread_b(0, s)
            states(0, first=True)
            with pe.Fori(1, B - 1) as b:
                states(b)
            states(B - 1, last=True)
            add_state(B - 1, DS - 2)
            add_state(B - 1, DS - 1)
            pe.wait_ge(weighted, B * DS + 2)
            pe.wait_ge(bbc_copied, B * DS + 1)
            for i in range(B + 1):
                if i < B:
                    j, g = i // GROUPS, i % GROUPS
                    rows = slice(C * g, C * (g + 1))
                    if i >= 2:
                        pe.wait_ge(z_set, i - 1)
                    pair_matmul(i % 2, par("inz")[rows, :], XN[rows, :], j * L).then_inc(z_mm, 1)
                if i >= 1:
                    j, g = (i - 1) // GROUPS, (i - 1) % GROUPS
                    pe.wait_ge(yg_set, 2 * i)
                    if j >= 2 and g == 0:
                        pe.wait_ge(x3_set, j - 1)
                    pair_matmul(2 + j % 2, par("outw"), YG, (g * J + j) * L, slice(C * g, C * (g + 1))).then_inc(out_mm, 1)
            ln_pe(pe, 4, X, after(x3_set, J))
            pe.wait_ge(ln[4]["out"], J)

            def tokens(t, n):
                b, k = n // KT, n % KT
                g, j = b // J, b % J
                return t[C * g:C * (g + 1), j * L + k * TOK:j * L + (k + 1) * TOK], slice(C * g, C * (g + 1))

            for n in range(NT):
                mine, rows = tokens(XN, n)
                g, i = n // (NT // GROUPS), n % (NT // GROUPS)
                last = nc.tensor.matmul(PS[0:TOK, g, i * EX:(i + 1) * EX], mine,
                                        par("rw")[rows, :], start=True, stop=True)
            last.then_inc(lg_mm, 1)
            pe.wait_ge(eb_set, 1)
            for u in range(NT // 2):
                if u % KT == 0:
                    v = u // KT
                    if v >= 2:
                        pe.wait_ge(yt_set, v - 1)
                    for i in range(2 * KT):
                        mine, rows = tokens(X, v * 2 * KT + i)
                        last = nc.tensor.matmul(PS[0:TOK, 6 + v % 2, i * C:(i + 1) * C], mine,
                                                par("ident")[rows, rows], start=True, stop=True)
                    last.then_inc(xt_mm, 1)
                if u < 4:
                    pe.wait_ge(lg_step, 2 + GROUPS)
                else:
                    pe.wait_ge(ex_prod, u - 3)
                for t in range(2):
                    mine, rows = tokens(XN, 2 * u + t)
                    dst = PS[0:TOK, 2 + u % 4, t * EX * C:(t + 1) * EX * C]
                    nc.tensor.matmul(dst, mine, par("ew")[rows, :], start=True, stop=False)
                    last = nc.tensor.matmul(dst, ONB[0:96, :], EBS[0:96, :], start=False, stop=True)
                last.then_inc(ex_mm, 1)


def lay_out(inputs):
    a = {k: np.asarray(v) for k, v in inputs.items()}
    f = np.float32
    x = np.ascontiguousarray(a["x"].reshape(GROUPS, J, L, C).transpose(0, 3, 1, 2)).reshape(128, N)

    def blocks(w, times=GROUPS):
        r, c = w.shape
        o = np.zeros((times * r, times * c), f)
        for i in range(times):
            o[i * r:(i + 1) * r, i * c:(i + 1) * c] = w
        return o

    def down(w, times=GROUPS):
        return np.tile(w.reshape(w.shape[0], -1), (times, 1))

    main, front = np.zeros((128, MAIN_W), f), np.zeros((128, FRONT_W), f)

    def put(name, w):
        where = MAIN_AT if name in MAIN_AT else FRONT_AT
        (main if name in MAIN_AT else front)[0:w.shape[0], where[name]] = w

    eye, one = np.eye(128, dtype=f), blocks(np.full((C, C), 1.0 / C, f))
    put("ident", eye)
    put("cent", eye - one)
    put("meanj", one)
    put("gavg", np.tile(np.eye(C, dtype=f) / GROUPS, (GROUPS, GROUPS)))
    put("ones", np.ones((128, 1), f))
    sel = np.zeros((3, 2, DS, DS, 2, DI), f)
    for d in range(2):
        for s in range(DS):
            sel[:, d, s, s, d, :] = 1.0
    sel = sel.reshape(3 * 2 * DS, DS * 128)
    wf, bf = a["L0_conv_Wf"], a["L0_conv_bf"]
    put("wq", blocks(wf[:, 0:C]))
    put("wctx", blocks(wf[:, C:2 * C]))
    for l in range(LEVELS + 1):
        put(f"wg{l}", blocks(np.tile(wf[:, 2 * C + l:2 * C + l + 1], (1, C))))
    put("bq", down(bf[0:C]))
    put("bctx", down(bf[C:2 * C]))
    put("bg", np.tile(bf[2 * C:].reshape(1, -1), (128, 1)))
    put("wh", blocks(a["L0_conv_Wh"]))
    put("wp", blocks(a["L0_conv_Wp"]))
    put("taps", np.concatenate([down(a[f"L0_conv_k{l}"].reshape(-1, C).T) for l in range(LEVELS)], 1))
    for name, key in (("bh", "bh"), ("gamma", "gamma"), ("beta", "beta"), ("bp", "bp")):
        put(name, down(a["L0_conv_" + key]))
    put("fw", blocks(a["L0_ffn_W"].T))
    put("vt", blocks(a["L0_ffn_V"].T))
    put("fgam", down(a["L0_ffn_gamma"]))
    put("fbet", down(a["L0_ffn_beta"]))
    iw, xw = a["L1_conv_in_w"], a["L1_conv_x_w"]
    put("inx", np.tile(iw[0:DI].T, (GROUPS, 2)))
    put("inz", np.tile(iw[DI:].T, (GROUPS, 2)))
    put("xwd", blocks(xw[0:DR], 2))
    put("dtw", blocks(a["L1_conv_dt_w"].T, 2))
    for name, r0 in (("xwb", DR), ("xwc", DR + DS)):
        put(name, np.tile(blocks(xw[r0:r0 + DS].T, 2), (1, 3)))
    put("outw", down(a["L1_conv_out_w"].T, 2))
    put("convw", down(a["L1_conv_conv_w"], 2))
    put("convb", down(a["L1_conv_conv_b"], 2))
    put("dvec", down(a["L1_conv_D"], 2))
    put("dtb", down(a["L1_conv_dt_b"], 2))
    put("alog", down(a["L1_conv_A_log"], 2))
    put("rw", down(a["L1_ffn_router_w"]))
    put("rb", np.tile(a["L1_ffn_router_b"].reshape(1, EX), (128, 1)))
    put("ew", down(np.ascontiguousarray(a["L1_ffn_expert_w"].transpose(1, 0, 2)).reshape(C, EX * C)))
    eb = np.zeros((96, EX * C), f)
    eb[0:96:32] = a["L1_ffn_expert_b"].reshape(1, EX * C)
    put("eb", eb)
    return {"x_in": x, "main_in": main, "front_in": front, "sel_in": sel}


def kernel(**inputs):
    import concourse.bacc as bacc
    from concourse.bass_utils import run_bass_kernel_spmd

    nc = bacc.Bacc("TRN2", target_bir_lowering=False, num_devices=1)
    arrays = lay_out(inputs)
    args = [nc.dram_tensor(name, a.shape, mybir.dt.float32, kind="ExternalInput").ap() for name, a in arrays.items()]
    out = nc.dram_tensor("out", (B * L, C), mybir.dt.float32, kind="ExternalOutput").ap()
    build_program(nc, *args, out)
    r = run_bass_kernel_spmd(nc, [arrays], core_ids=[0])
    return r.results[0]["out"].reshape(B, H, W, C)
```

```python
import numpy as np
import concourse.bass as bass
from concourse import mybir
from contextlib import ExitStack

B, H, W, C = 16, 24, 24, 32
L = H * W
HALF = L // 2
GROUPS = 4
J = B // GROUPS
N = J * L
LEVELS = 3
KS = [3, 5, 7]
TAP0 = [0, 9, 34]
TAPS = 83
PAD = 3
HP, WP = H + 2 * PAD, W + 2 * PAD
CHUNK = 24
CHUNKS = L // CHUNK
WARM = 16
DI, DS, DC = 64, 16, 4
T2 = B * L
DR = 2
XIW = L + DC - 1
POOL_ROWS = 18
EX = 8
BANK = 512
TOK = 128
TI = N // TOK
NT = GROUPS * TI
XT = BANK // 128
BANKS_XT = (TI + XT - 1) // XT

MAIN = [("ident", 128), ("cent", 128), ("msel", 60), ("gavg", 128), ("fw", 128), ("vt", 128),
        ("xwd", 128), ("dtw", 128), ("xwb", 96), ("xwc", 96),
        ("outw", 32), ("rw", GROUPS * EX), ("rb", EX), ("eb", 2 * EX * C), ("convw", DC),
        ("convb", 1), ("dvec", 1), ("dtb", 1), ("alog", DS), ("fgam", 1), ("fbet", 1), ("ones", 1)]
FRONT = [("wctx", 128), ("wq", 128), ("wg0", 128), ("wg1", 128), ("wg2", 128), ("wg3", 128),
         ("wh", 128), ("wp", 128), ("taps", TAPS), ("bctx", 1), ("bq", 1), ("bg", 4), ("bh", 1),
         ("gamma", 1), ("beta", 1), ("bp", 1)]


def places(fields):
    at, out = 0, {}
    for name, width in fields:
        out[name] = slice(at, at + width)
        at += width
    return out, at


MAIN_AT, MAIN_W = places(MAIN)
FRONT_AT, FRONT_W = places(FRONT)


def build_program(nc, x_in, main_in, front_in, sel_in, rows_in, xz_in, experts_in, out):
    f32, bf16, i32 = mybir.dt.float32, mybir.dt.bfloat16, mybir.dt.int32
    ALU, ACT, AX = mybir.AluOpType, mybir.ActivationFunctionType, mybir.AxisListType
    ctx = ExitStack()
    with ctx:
        def sb(name, shape, dt=f32):
            return ctx.enter_context(nc.sbuf_tensor(name, shape, dt))[:, :]

        def sem(name):
            return ctx.enter_context(nc.semaphore(name))

        PM = sb("main_params", [128, MAIN_W])
        SEL = sb("selectors", [3 * 2 * DS, DS * 128], bf16)
        RSEL = sb("row_selectors", [128, 2 * J * 128])
        STD = sb("std", [128, HALF])
        EBS = sb("expert_bias", [96, 2 * EX * C], bf16)
        ONB = sb("bf16_ones", [96, TOK], bf16)
        INZ = sb("z_weights", [128, GROUPS * 128])
        X = sb("residual", [128, N])
        XN = sb("normed", [128, N])
        RING = sb("ring", [128, 8 * L])
        EPS = sb("eps", [128, 3])
        SM = sb("small", [128, 128])
        WDT = sb("w_dt", [128, 128])
        NEGI = sb("neg_ident", [96, 96], bf16)
        FLAG = sb("flag", [1, 1], i32)
        DECAYS = sb("decays", [128, 2 * L])
        BIG = sb("big", [128, 4 * T2])
        PS = ctx.enter_context(nc.psum_tensor("banks", [128, 8, BANK], f32))

        pos = [0]

        def big(cols):
            v = BIG[:, pos[0]:pos[0] + cols]
            pos[0] += cols
            assert pos[0] <= 4 * T2
            return v

        PF = big(FRONT_W)
        DIAG = big(TAPS * 128)
        CP = [big(J * HP * WP).rearrange("p (j h w) -> p j h w", j=J, h=HP) for _ in range(2)]
        QS = big(N)
        GS = [big(N) for _ in range(LEVELS + 1)]
        ACC = big(2 * L + POOL_ROWS * W)
        ALLC = big(N)
        MT = big(N)
        XO = MT
        WPG = big(128)
        pos[0] = 0
        WX = big(N)
        YP = big(J * (L + 1)).rearrange("p (j t) -> p j t", j=J)
        ENDS = big(J * CHUNKS).rearrange("p (j c) -> p j c", j=J)
        DIFF = big(J * CHUNKS).rearrange("p (j c) -> p j c", j=J)
        SDIAG = big(128)
        EBF = big(2 * EX * C)
        EBT = big(EX * C).bitcast(bf16)
        pos[0] = 0
        XC = big(T2)
        DT = big(T2)
        DTX = big(T2)
        SB = big(T2 // 2).bitcast(bf16)
        SC = big(T2 // 2).bitcast(bf16)
        XI = BIG[:, 4 * T2 - B * XIW:4 * T2].rearrange("p (b t) -> p b t", b=B)
        YG = DT
        GZ = DTX
        SP = DTX
        pos[0] = 0
        LG, PR, S1, S2, RST, CNT = (big(NT * EX) for _ in range(6))
        MROW = big(2 * NT)
        PROD = [big(2 * EX * C) for _ in range(4)]
        YT = big(NT * C)
        assert pos[0] <= T2
        EWB = BIG[:, 3 * T2:3 * T2 + GROUPS * EX * C]
        SQ = [RING[:, i * L:(i + 1) * L] for i in range(2)]
        SELF = RING[0:3 * 2 * DS, 4 * L:4 * L + DS * 128]
        INX = RING[:, 4 * L:4 * L + GROUPS * 128]
        PROD3 = [RING[:, 5 * L + i * POOL_ROWS * W:5 * L + (i + 1) * POOL_ROWS * W] for i in range(3)]
        SLOTS = 8
        SLOT = [RING[:, i * L:(i + 1) * L] for i in range(SLOTS)]
        DECAY = [DECAYS[:, i * L:(i + 1) * L] for i in range(2)]
        AEXP, ANEG = SM[:, 0:DS], SM[:, DS:2 * DS]
        GSUM, GGLOB, BPG = SM[:, 32:37], SM[:, 40:44], SM[:, 44:45]
        MV, MEX, MEXT = SM[:, 48:50], SM[:, 52:54], SM[:, 54:56]
        MSQ, VAR, SDEV, RSD, BSCALE, MS, BBIAS, NDIFF = (SM[:, 56 + i:57 + i] for i in range(8))
        STATS, SPARE = SM[:, 64:64 + 48], SM[:, 112:128]

        LEAD_B = 4
        C_PAIR = (0, 2)

        def par(name):
            return PM[:, MAIN_AT[name]]

        def fpar(name):
            return PF[:, FRONT_AT[name]]

        def pair(p, rows=slice(0, 128)):
            return PS[rows, 2 * p:2 * p + 2, 0:HALF]

        def img(t, j, rows=slice(0, 128)):
            return t[rows, j * L:(j + 1) * L].rearrange("p (a c) -> p a c", a=2)

        def pair_matmul(p, lhsT, rhs, at, rows=slice(0, 128), start=True, stop=True, again=False):
            for a in range(2):
                last = nc.tensor.matmul(PS[rows, 2 * p + a, 0:HALF], lhsT,
                                        rhs[:, bass.ds(at + a * HALF, HALF)], start=start, stop=stop,
                                        skip_group_check=again)
            return last

        x_loaded = [sem(f"x_loaded{j}") for j in range(J)]
        main_loaded, front_loaded, sel_loaded = sem("main_loaded"), sem("front_loaded"), sem("sel_loaded")
        rest_zero = sem("rest_zero")
        xz_loaded, rows_loaded, experts_loaded, spare_set = sem("xz_loaded"), sem("rows_loaded"), sem("experts_loaded"), sem("spare_set")
        sel_set, eps_set, negi_set = sem("sel_set"), sem("eps_set"), sem("negi_set")
        ln = [{k: sem(f"ln{n}_{k}") for k in ("cent", "copy", "sq", "var", "std", "rstd", "back", "out")} for n in range(5)]
        pads_zero, diag_made = sem("pads_zero"), sem("diag_made")
        ctx_mm, ctx_set, lin_mm, lin_set = sem("ctx_mm"), sem("ctx_set"), sem("lin_mm"), sem("lin_set")
        tap_dve, tap_pe, gelu_set = sem("tap_dve"), sem("tap_pe"), sem("gelu_set")
        diag2_made, prod_set, tap_pool = sem("diag2_made"), sem("prod_set"), sem("tap_pool")
        gated_dve, ctx_sum_dve = sem("gated_dve"), sem("ctx_sum_dve")
        gated, ctx_sum = sem("gated"), sem("ctx_sum")
        glob_sum, glob_set, glob_added = sem("glob_sum"), sem("glob_set"), sem("glob_added")
        mod_mm, xo_set = sem("mod_mm"), sem("xo_set")
        wpg_set, bp_mm, bp_set = sem("wpg_set"), sem("bp_mm"), sem("bp_set")
        proj_mm, x1_set = sem("proj_mm"), sem("x1_set")
        wx_mm, wx_set, stats_set, stats_mm = sem("wx_mm"), sem("wx_set"), sem("stats_set"), sem("stats_mm")
        bn_step, var_set, sdev_set, sdiag_set = sem("bn_step"), sem("var_set"), sem("sdev_set"), sem("sdiag_set")
        y_zero, rec_mm, rec_y = sem("y_zero"), sem("rec_mm"), sem("rec_y")
        ends_saved, diff_step, ndiff_set = sem("ends_saved"), sem("diff_step"), sem("ndiff_set")
        count_mm, flag_set = sem("count_mm"), sem("flag_set")
        slow_mm, slow_y, rec_done, x2_set = sem("slow_mm"), sem("slow_y"), sem("rec_done"), sem("x2_set")
        xi_pad, in_mm, xi_set = sem("xi_pad"), sem("in_mm"), sem("xi_set")
        conv_step, xc_set = sem("conv_step"), sem("xc_set")
        aexp_set, a_set, wdt_mm, wdt_set = sem("aexp_set"), sem("a_set"), sem("wdt_mm"), sem("wdt_set")
        dt_mm, abs_set, v_set, sp_step, sp_set = sem("dt_mm"), sem("abs_set"), sem("v_set"), sem("sp_step"), sem("sp_set")
        dve_dt_set = sem("dve_dt_set")
        dt_set, dtx_set = sem("dt_set"), sem("dtx_set")
        part_mm = [sem(f"part{i}_mm") for i in range(3)]
        part_set = [sem(f"part{i}_set") for i in range(3)]
        u_begun, decay_begun = sem("u_begun"), sem("decay_begun")
        bbc_mm, bbc_copied, u_set, decay_set, scanned = (sem("bbc_mm"), sem("bbc_copied"), sem("u_set"),
                                                         sem("decay_set"), sem("scanned"))
        cbc_mm, weighted, y_added, y_read = sem("cbc_mm"), sem("weighted"), sem("y_added"), sem("y_read")
        z_mm, z_set, yg_set, out_mm, x3_set = sem("z_mm"), sem("z_set"), sem("yg_set"), sem("out_mm"), sem("x3_set")
        lg_mm, lg_step, lg_sub, lg_exp, weights_set = (sem("lg_mm"), sem("lg_step"), sem("lg_sub"), sem("lg_exp"),
                                                       sem("weights_set"))
        eb_step, eb_set, ex_mm, ex_prod, ex_sum = sem("eb_step"), sem("eb_set"), sem("ex_mm"), sem("ex_prod"), sem("ex_sum")
        xt_mm, yt_set, stored = sem("xt_mm"), sem("yt_set"), sem("stored")

        DVE_PIECES = [(0, 0, H), (1, 0, H)]
        PE_UNITS = [(2, POOL_ROWS, H - POOL_ROWS, 2), (3, 0, H // 2, 0), (3, H // 2, H // 2, 1)]
        NP = 5
        GELU_OF = [1, 2, 4, 5]

        DVE_DT = [b for b in range(B) if b % 4 >= 2]

        def DT_STEP(b):
            return (8 * (b // 4) + 4 + b % 4 + 1) * 2 // 3 + 3

        REC_STEPS = list(range(CHUNK - WARM, CHUNK)) + 2 * list(range(CHUNK))

        def inside(cp, j, r0=0, rows=H):
            return cp[:, j, PAD + r0:PAD + r0 + rows, PAD:PAD + W]

        def window(cp, l, tap, j, r0, rows):
            dy, dx = tap // KS[l] - KS[l] // 2, tap % KS[l] - KS[l] // 2
            return cp[:, j, PAD + r0 + dy:PAD + r0 + dy + rows, PAD + dx:PAD + dx + W]

        POOL_ACC = ACC[:, 2 * L:2 * L + POOL_ROWS * W]

        def adds(l, t=0):
            return TAP0[l] - l + max(t - 1, 0)

        def rows_of(t, j, r0=0, rows=H):
            return t[:, j * L + r0 * W:j * L + (r0 + rows) * W].rearrange("p (h w) -> p h w", w=W)

        BACK_PAIR = (2, 0, 1, 2)

        def keep_warm(times):
            for _ in range(times):
                nc.tensor.matmul(PS[0:96, 6, :], NEGI, SEL[:, 0:BANK], start=True, stop=True)

        def ln_pe(pe, n, src, ready):
            s = ln[n]
            for j in range(J + 1):
                if j < J:
                    ready(j)
                    if j >= 2:
                        pe.wait_ge(s["copy"], j - 1)
                    pair_matmul(j % 2, par("cent"), src, j * L).then_inc(s["cent"], 1)
                if j == 1:
                    ready(J)
                    if n >= 1:
                        keep_warm(4)
                if j >= 1:
                    i = j - 1
                    pe.wait_ge(s["sq"], i + 1)
                    for a in range(2):
                        r0 = GROUPS * (2 * i + a)
                        last = nc.tensor.matmul(PS[0:32, 7, 0:HALF], par("msel")[:, 28 - r0:60 - r0],
                                                SQ[i % 2][:, a * HALF:(a + 1) * HALF],
                                                start=r0 == 0, stop=r0 == 28)
                    last.then_inc(s["var"], 1)
            if n >= 1:
                keep_warm(10)
            pe.wait_ge(s["rstd"], 1)
            if n == 0:
                pe.wait_ge(rows_loaded, 16)
                pe.wait_ge(rest_zero, 4)
            for j in range(J):
                if j == 3:
                    pe.wait_ge(s["out"], 1)
                for a in range(2):
                    r = 2 * j + a
                    last = nc.tensor.matmul(PS[:, 2 * BACK_PAIR[j] + a, 0:HALF], RSEL[:, r * 128:(r + 1) * 128],
                                            STD, start=True, stop=True)
                last.then_inc(s["back"], 1)

        def ln_act(act, n, eps, dst):
            s = ln[n]
            nc.scalar.activation(SPARE[:, n:n + 1], EPS[:, eps:eps + 1], ACT.Sqrt).then_inc(spare_set, 1)
            for j in range(J):
                act.wait_ge(s["copy"], j + 1)
                if j >= 2:
                    act.wait_ge(s["var"], j - 1)
                nc.scalar.activation(SQ[j % 2], dst[:, j * L:(j + 1) * L], ACT.Square).then_inc(s["sq"], 1)
            act.wait_ge(s["var"], J)
            nc.scalar.activation(STD[0:32, :], PS[0:32, 7, 0:HALF], ACT.Sqrt, bias=EPS[0:32, eps:eps + 1]).then_inc(s["std"], 1)

        def ln_dve(dve, n, dst):
            s = ln[n]
            for j in range(J):
                dve.wait_ge(s["cent"], j + 1)
                nc.vector.tensor_copy(img(dst, j), pair(j % 2)).then_inc(s["copy"], 1)
            dve.wait_ge(s["std"], 1)
            nc.vector.reciprocal(STD[0:32, :], STD[0:32, :]).then_inc(s["rstd"], 1)
            dve.wait_ge(s["copy"], J)
            for j in range(J):
                dve.wait_ge(s["back"], j + 1)
                nc.vector.tensor_tensor(img(dst, j), img(dst, j), pair(BACK_PAIR[j]), ALU.mult).then_inc(s["out"], 1)

        def tokens(t, i):
            return t[:, i:N:TI]

        YT4 = YT.rearrange("p (g i c) -> p g i c", g=GROUPS, i=TI)

        def add_experts(dve, u):
            i, h = u // 2, u % 2
            dve.wait_ge(ex_prod, u + 1)
            nc.vector.tensor_reduce(YT4[:, 2 * h:2 * h + 2, i, :],
                                    PROD[u % 4].rearrange("p (t e c) -> p t c e", t=2, e=EX),
                                    AX.X, ALU.add).then_inc(ex_sum, 1)

        def finish_tiles(dve, m):
            i0, i1 = XT * m, min(XT * (m + 1), TI)
            dve.wait_ge(xt_mm, m + 1)
            dve.wait_ge(ex_sum, 2 * i1)
            here = YT4[:, :, i0:i1, :].rearrange("p g i c -> p i g c")
            res = PS[:, m % 2, 0:(i1 - i0) * 128].rearrange("p (i g c) -> p i g c", g=GROUPS, c=C)
            nc.vector.tensor_tensor(here, here, res, ALU.add).then_inc(yt_set, 1)

        block = ctx.enter_context(nc.Block())

        @block.sync
        def _(sp):
            sp.dma_start(X[:, 0:L], x_in[:, 0:L]).then_inc(x_loaded[0], 16)
            sp.dma_start(PM[:, :], main_in).then_inc(main_loaded, 16)
            for j in range(1, J):
                sp.dma_start(X[:, j * L:(j + 1) * L], x_in[:, j * L:(j + 1) * L]).then_inc(x_loaded[j], 16)
            sp.dma_start(INZ, xz_in[:, GROUPS * 128:]).then_inc(xz_loaded, 16)
            sp.wait_ge(sel_set, 1)
            sp.dma_start(INX, xz_in[:, 0:GROUPS * 128]).then_inc(xz_loaded, 16)
            sp.wait_ge(bbc_copied, B * DS + 1)
            sp.dma_start(EWB, experts_in).then_inc(experts_loaded, 16)
            out_v = out.rearrange("(g p i) c -> p g (i c)", g=GROUPS, p=TOK)
            yt_v = YT.rearrange("p (g r) -> p g r", g=GROUPS)
            for m in range(0, BANKS_XT, 2):
                here = slice(XT * m * C, min(XT * (m + 2), TI) * C)
                sp.wait_ge(yt_set, min(m + 2, BANKS_XT))
                sp.dma_start(out_v[:, :, here], yt_v[:, :, here]).then_inc(stored, 16)
            sp.wait_ge(stored, 16 * ((BANKS_XT + 1) // 2))

        @block.gpsimd
        def _(pool):
            pool.dma_start(PF, front_in).then_inc(front_loaded, 16)
            pool.dma_start(RSEL[0:32, :], rows_in).then_inc(rows_loaded, 16)
            pool.dma_start(SELF, sel_in).then_inc(sel_loaded, 16)
            for cp in CP:
                nc.gpsimd.memset(cp, 0.0).then_inc(pads_zero, 1)
            pool.wait_ge(main_loaded, 16)
            pool.wait_ge(front_loaded, 16)
            for t in range(TAP0[2]):
                nc.gpsimd.tensor_scalar(DIAG[:, t * 128:(t + 1) * 128], par("ident"),
                                        fpar("taps")[:, t:t + 1], None, ALU.mult).then_inc(diag_made, 1)
            def add_taps(l):
                for t in range(1, KS[l] ** 2):
                    pool.wait_ge(prod_set, TAP0[l] + t + 1)
                    if t >= 2:
                        pool.wait_ge(tap_pool, adds(l, t))
                    nc.gpsimd.tensor_tensor(POOL_ACC, POOL_ACC, PROD3[(TAP0[l] + t) % 3], ALU.add).then_inc(tap_pool, 1)

            def gate(l, images):
                pool.wait_ge(lin_set, (l + 1) * J)
                for j in images:
                    pool.wait_ge(gelu_set, NP * l + GELU_OF[j])
                    if l == 0:
                        nc.gpsimd.tensor_tensor(rows_of(ALLC, j), inside(CP[1], j), rows_of(GS[0], j),
                                                ALU.mult).then_inc(gated, 1)
                    else:
                        if l == 2:
                            pool.wait_ge(ctx_sum, J)
                        nc.gpsimd.tensor_tensor(rows_of(MT, j), inside(CP[(l + 1) % 2], j), rows_of(GS[l], j),
                                                ALU.mult).then_inc(gated, 1)
                        pool.wait_ge(gated, J * l + (j + 1 if l == 1 else 1))
                        nc.gpsimd.tensor_tensor(ALLC[:, j * L:(j + 1) * L], ALLC[:, j * L:(j + 1) * L],
                                                MT[:, j * L:(j + 1) * L], ALU.add).then_inc(ctx_sum, 1)

            add_taps(0)
            add_taps(1)
            gate(0, range(J))
            add_taps(2)
            gate(1, range(J))
            gate(2, (J - 1,))
            pool.wait_ge(x2_set, J)
            nc.gpsimd.memset(XI[:, :, 0:DC - 1], 0.0).then_inc(xi_pad, 1)
            for b in range(B):
                pool.wait_ge(v_set, b + 1)
                pool.wait_ge(sp_set, b + 1)
                here = slice(b * L, (b + 1) * L)
                if b in DVE_DT:
                    pool.wait_ge(dve_dt_set, DVE_DT.index(b) + 1)
                else:
                    nc.gpsimd.tensor_tensor(DT[:, here], DT[:, here], SP[:, here], ALU.add).then_inc(dt_set, 1)
                    pool.wait_ge(dt_set, b - len([i for i in DVE_DT if i < b]) + 1)
                nc.gpsimd.tensor_tensor(DTX[:, here], DT[:, here], XC[:, here], ALU.mult).then_inc(dtx_set, 1)
            pool.wait_ge(dtx_set, B)
            with pool.Fori(0, B) as b:
                for s in range(0, DS, 2):
                    pool.wait_ge(bbc_copied, b * DS + (s + 3))
                    pool.sem_inc(u_begun, 1)
                    two = RING[:, s % SLOTS * L:(s % SLOTS + 2) * L].rearrange("p (s t) -> p s t", s=2)
                    nc.gpsimd.tensor_tensor(two, DTX[:, bass.ds(b * L, L)].unsqueeze(1).to_broadcast([128, 2, L]), two,
                                            ALU.mult).then_inc(u_set, 1)

        @block.scalar
        def _(act):
            act.wait_ge(eps_set, 3)
            ln_act(act, 0, 0, XN)
            act.wait_ge(front_loaded, 16)
            act.wait_ge(pads_zero, 2)
            for j in range(J):
                act.wait_ge(ctx_mm, j + 1)
                for a in range(2):
                    last = nc.scalar.activation(inside(CP[0], j, a * H // 2, H // 2),
                                                PS[:, 2 * (j % 2) + a, 0:HALF].rearrange("p (h w) -> p h w", w=W),
                                                ACT.Identity, bias=fpar("bctx"))
                last.then_inc(ctx_set, 1)

            def linear(i0, i1):
                for i in range(i0, i1):
                    m, j = i // J, i % J
                    act.wait_ge(lin_mm, i + 1)
                    dst = (GS[0], GS[1], GS[2], QS, GS[3])[m]
                    bias = fpar("bq") if m == 3 else fpar("bg")[:, min(m, 3):min(m, 3) + 1]
                    nc.scalar.activation(img(dst, j), pair(2 + i % 2), ACT.Identity, bias=bias).then_inc(lin_set, 1)

            act.wait_ge(sel_set, 1)
            for l in range(LEVELS):
                dst = CP[(l + 1) % 2]
                if l == 0:
                    act.wait_ge(ctx_set, 3)
                else:
                    act.wait_ge(gelu_set, NP * l)
                for t in range(KS[l] ** 2):
                    n = TAP0[l] + t
                    if t >= 1 and adds(l, t) >= 3:
                        act.wait_ge(tap_pool, adds(l, t - 2) if t >= 3 else adds(l, 0))
                    prod = POOL_ACC if t == 0 else PROD3[n % 3]
                    nc.scalar.activation(prod.rearrange("p (h w) -> p h w", w=W), window(CP[l % 2], l, t, 2, 0, POOL_ROWS),
                                         ACT.Identity, scale=fpar("taps")[:, n:n + 1]).then_inc(prod_set, 1)
                    if l == 1:
                        for m in range(2 * t, min(2 * t + 2, KS[2] ** 2)):
                            nc.scalar.activation(DIAG[:, (TAP0[2] + m) * 128:(TAP0[2] + m + 1) * 128], par("ident"),
                                                 ACT.Identity, scale=fpar("taps")[:, TAP0[2] + m:TAP0[2] + m + 1]
                                                 ).then_inc(diag2_made, 1)
                if l == 1:
                    linear(0, 2 * J)
                if l == 2:
                    linear(2 * J, 5 * J)
                    act.wait_ge(gated, J)
                for i, (j, r0, rows) in enumerate(DVE_PIECES):
                    act.wait_ge(tap_dve, 2 * (TAP0[l] + KS[l] ** 2 - 1) + i + 1)
                    acc = ACC[:, j * L:j * L + rows * W].rearrange("p (h w) -> p h w", w=W)
                    nc.scalar.activation(inside(dst, j, r0, rows), acc, ACT.Gelu,
                                         accum_out=GSUM[:, i:i + 1] if l == 2 else None).then_inc(gelu_set, 1)
                act.wait_ge(tap_pool, adds(l + 1) if l + 1 < LEVELS else TAPS - LEVELS)
                nc.scalar.activation(inside(dst, 2, 0, POOL_ROWS), POOL_ACC.rearrange("p (h w) -> p h w", w=W),
                                     ACT.Gelu, accum_out=GSUM[:, 2:3] if l == 2 else None).then_inc(gelu_set, 1)
                act.wait_ge(tap_pe, 2 * l + 1)
                rest = H - POOL_ROWS
                nc.scalar.activation(inside(dst, 2, POOL_ROWS, rest), PS[:, 2, 0:rest * W].rearrange("p (h w) -> p h w", w=W),
                                     ACT.Gelu, accum_out=GSUM[:, 4:5] if l == 2 else None).then_inc(gelu_set, 1)
                act.wait_ge(tap_pe, 2 * l + 2)
                nc.scalar.activation(inside(dst, 3).rearrange("p (a h) w -> p a h w", a=2),
                                     pair(0).rearrange("p a (h w) -> p a h w", w=W),
                                     ACT.Gelu, accum_out=GSUM[:, 3:4] if l == 2 else None).then_inc(gelu_set, 1)
            act.wait_ge(glob_sum, 1)
            nc.scalar.activation(GGLOB, GSUM[:, 0:4], ACT.Gelu, scale=1.0 / L).then_inc(glob_set, 1)
            ln_act(act, 1, 1, XN)
            ln_act(act, 2, 2, XN)
            for j in range(J):
                act.wait_ge(wx_mm, j + 1)
                nc.scalar.activation(img(WX, j), pair(j), ACT.Copy).then_inc(wx_set, 1)
            act.wait_ge(var_set, 1)
            nc.scalar.activation(SDEV, VAR, ACT.Sqrt, bias=EPS[:, 2:3]).then_inc(sdev_set, 1)
            act.wait_ge(sdiag_set, 1)

            def recur(k):
                return nc.scalar.activation(YP[:, :, k + 1:k + 2 + CHUNK * (CHUNKS - 1):CHUNK],
                                            PS[:, k % 2, 0:J * CHUNKS].rearrange("p (j c) -> p j c", j=J),
                                            ACT.Sigmoid, bias=BBIAS)

            for q, k in enumerate(REC_STEPS):
                act.wait_ge(rec_mm, q + 1)
                if q == len(REC_STEPS) - 1:
                    act.wait_ge(ends_saved, 1)
                recur(k).then_inc(rec_y, 1)
            act.wait_ge(flag_set, 1)
            moved = act.value_load(FLAG[0:1, 0:1], min_val=0, max_val=1)
            with act.If(moved == 1):
                act.sem_inc(slow_y, 1)
                with act.Fori(0, CHUNKS - 2) as p:
                    for k in range(CHUNK):
                        act.wait_ge(slow_mm, p * CHUNK + (k + 1))
                        recur(k).then_inc(slow_y, 1)
                act.wait_ge(slow_y, (CHUNKS - 2) * CHUNK + 1)
            act.sem_inc(rec_done, 1)
            ln_act(act, 3, 0, XN)
            for b in range(B + 3):
                if b < B:
                    act.wait_ge(in_mm, b + 1)
                    nc.scalar.activation(XI[0:64, b, DC - 1:].rearrange("p (a c) -> p a c", a=2),
                                         pair(b % 2, slice(0, 64)), ACT.Copy).then_inc(xi_set, 1)
                    nc.scalar.activation(XI[64:128, b, DC - 1:][:, ::-1].rearrange("p (a c) -> p a c", a=2),
                                         pair(b % 2, slice(64, 128)), ACT.Copy).then_inc(xi_set, 1)
                if 2 <= b < B + 2:
                    act.wait_ge(conv_step, DC * (b - 1))
                    xc_b = XC[:, (b - 2) * L:(b - 1) * L]
                    nc.scalar.activation(xc_b, xc_b, ACT.Silu, bias=par("convb")).then_inc(xc_set, 1)
                if b >= 3:
                    i = b - 3
                    act.wait_ge(dt_mm, i + 1)
                    nc.scalar.activation(img(DT, i), pair(2 + i % 2), ACT.Relu, bias=par("dtb")).then_inc(v_set, 1)
                    nc.scalar.activation(img(SP, i), pair(2 + i % 2), ACT.Abs, bias=par("dtb")).then_inc(abs_set, 1)
            nc.scalar.activation(AEXP, par("alog"), ACT.Exp).then_inc(aexp_set, 1)
            batches = [(f, b) for b0 in range(0, B, 4) for f in (ACT.Exp, ACT.Ln) for b in range(b0, b0 + 4)]
            for c in range(2 * B):
                act.wait_ge(part_mm[0], c + 1)
                nc.scalar.activation(img((SB, SC)[c % 2], c // 2, slice(0, 96)), pair(c % 4, slice(0, 96)),
                                     ACT.Copy).then_inc(part_set[0], 1)
                for f, b in batches[3 * c // 2:3 * (c + 1) // 2]:
                    sp_b = SP[:, b * L:(b + 1) * L]
                    if f == ACT.Exp:
                        act.wait_ge(abs_set, b + 1)
                        nc.scalar.activation(sp_b, sp_b, f, scale=-1.0).then_inc(sp_step, 1)
                    else:
                        act.wait_ge(sp_step, b + 1)
                        nc.scalar.activation(sp_b, sp_b, f, bias=1.0).then_inc(sp_set, 1)
            act.wait_ge(a_set, 1)
            act.wait_ge(dtx_set, B)
            act.wait_ge(part_set[2], 2 * B)
            act.sem_inc(bbc_copied, 1)

            def copy_b(i, s):
                act.wait_ge(bbc_mm, i + 1)
                act.wait_ge(y_added, i + 1)
                nc.scalar.activation(img(SLOT[s % SLOTS], 0), pair(1), ACT.Copy).then_inc(bbc_copied, 1)

            def decay(b, s, i):
                act.wait_ge(scanned, i + 1)
                act.sem_inc(decay_begun, 1)
                nc.scalar.activation(DECAY[s % 2], DT[:, bass.ds(b * L, L)], ACT.Exp,
                                     scale=ANEG[:, s:s + 1]).then_inc(decay_set, 1)

            for s in range(LEAD_B):
                copy_b(s, s)
            decay(0, 0, 0)
            with act.Fori(0, B - 1) as b:
                for s in range(DS):
                    decay(b + (s + 1) // DS, (s + 1) % DS, b * DS + (s + 1))
                    copy_b(b * DS + (s + LEAD_B), s + LEAD_B)
            for s in range(DS - 1):
                decay(B - 1, s + 1, (B - 1) * DS + s + 1)
                if s + LEAD_B < DS:
                    copy_b((B - 1) * DS + s + LEAD_B, s + LEAD_B)
            for i in range(B):
                j, b = i // GROUPS, (i % GROUPS) * J + i // GROUPS
                act.wait_ge(z_mm, i + 1)
                nc.scalar.activation(img(GZ, b), pair(i % 2), ACT.Silu).then_inc(z_set, 1)
            ln_act(act, 4, 2, XN)
            act.wait_ge(lg_sub, 1)
            nc.scalar.activation(LG, LG, ACT.Exp).then_inc(lg_exp, 1)

        @block.vector
        def _(dve):
            for i, eps in enumerate((1e-6, 1e-3, 1e-5)):
                nc.vector.memset(EPS[:, i:i + 1], eps).then_inc(eps_set, 1)
            for rows in (slice(32, 64), slice(64, 128)):
                nc.vector.memset(RSEL[rows, :], 0.0).then_inc(rest_zero, 1)
                nc.vector.memset(STD[rows, :], 0.0).then_inc(rest_zero, 1)
            ln_dve(dve, 0, XN)
            dve.wait_ge(sel_loaded, 16)
            nc.vector.tensor_copy(SEL[:, :], SELF).then_inc(sel_set, 1)
            dve.wait_ge(main_loaded, 16)
            nc.vector.tensor_scalar(NEGI[:, :], par("ident")[0:96, 0:96], -1.0, None, ALU.mult).then_inc(negi_set, 1)
            dve.wait_ge(front_loaded, 16)
            for l in range(LEVELS):
                src = CP[l % 2]
                for t in range(KS[l] ** 2):
                    for i, (j, r0, rows) in enumerate(DVE_PIECES):
                        if t == 0 and l == 0:
                            dve.wait_ge(ctx_set, j + 1)
                        elif t == 0:
                            dve.wait_ge(gelu_set, NP * (l - 1) + GELU_OF[j])
                        n = 2 * (TAP0[l] + t) + i
                        acc = ACC[:, j * L:j * L + rows * W].rearrange("p (h w) -> p h w", w=W)
                        win = window(src, l, t, j, r0, rows)
                        tap = fpar("taps")[:, TAP0[l] + t:TAP0[l] + t + 1]
                        if t == 0:
                            nc.vector.tensor_scalar(acc, win, tap, None, ALU.mult).then_inc(tap_dve, 1)
                        else:
                            dve.wait_ge(tap_dve, n - 1)
                            nc.vector.scalar_tensor_tensor(out=acc, in0=win, scalar=tap, in1=acc, op0=ALU.mult,
                                                           op1=ALU.add).then_inc(tap_dve, 1)
            dve.wait_ge(gelu_set, NP * LEVELS)
            nc.vector.tensor_tensor(GSUM[:, 2:3], GSUM[:, 2:3], GSUM[:, 4:5], ALU.add).then_inc(glob_sum, 1)
            nc.vector.tensor_scalar(WPG, fpar("wp"), fpar("gamma"), None, ALU.mult).then_inc(wpg_set, 1)
            for j in range(J - 1):
                gate, total = rows_of(GS[2], j), ALLC[:, j * L:(j + 1) * L]
                dve.wait_ge(ctx_sum, j + 1)
                nc.vector.tensor_tensor(rows_of(MT, j), inside(CP[1], j), gate, ALU.mult).then_inc(gated_dve, 1)
                dve.wait_ge(gated_dve, j + 1)
                nc.vector.tensor_tensor(total, total, MT[:, j * L:(j + 1) * L], ALU.add).then_inc(ctx_sum_dve, 1)
            dve.wait_ge(glob_set, 1)
            dve.wait_ge(lin_set, 5 * J)
            dve.wait_ge(ctx_sum_dve, J - 1)
            for j in range(J):
                if j == J - 1:
                    dve.wait_ge(ctx_sum, J + 1)
                here = slice(j * L, (j + 1) * L)
                nc.vector.scalar_tensor_tensor(out=ALLC[:, here], in0=GS[LEVELS][:, here], scalar=GGLOB[:, j:j + 1],
                                               in1=ALLC[:, here], op0=ALU.mult, op1=ALU.add).then_inc(glob_added, 1)
            for j in range(J):
                dve.wait_ge(mod_mm, j + 1)
                nc.vector.scalar_tensor_tensor(out=img(XO, j), in0=pair(j), scalar=fpar("bh"), in1=img(QS, j),
                                               op0=ALU.add, op1=ALU.mult).then_inc(xo_set, 1)
            ln_dve(dve, 1, XN)
            dve.wait_ge(bp_mm, 1)
            nc.vector.tensor_tensor(BPG, PS[:, 7, 0:1], fpar("bp"), ALU.add).then_inc(bp_set, 1)
            dve.wait_ge(bp_set, 1)
            for j in range(J):
                dve.wait_ge(proj_mm, j + 1)
                nc.vector.scalar_tensor_tensor(out=img(X, j), in0=pair(j), scalar=BPG, in1=img(X, j),
                                               op0=ALU.add, op1=ALU.add).then_inc(x1_set, 1)
            ln_dve(dve, 2, XN)
            nc.vector.memset(YP[:, :, 0:1], 0.0).then_inc(y_zero, 1)
            nc.vector.memset(YP[:, :, CHUNK - WARM:L:CHUNK], 0.0).then_inc(y_zero, 1)
            for i in range(2 * J):
                dve.wait_ge(wx_set, i // 2 + 1)
                nc.vector.bn_stats(STATS[:, 6 * i:6 * i + 6], WX[:, i * HALF:(i + 1) * HALF]).then_inc(stats_set, 1)
            dve.wait_ge(stats_set, 2 * J)
            steps = [0]

            def step(ins):
                steps[0] += 1
                ins.then_inc(bn_step, 1)
                dve.wait_ge(bn_step, steps[0])

            step(nc.vector.bn_aggr(MV, STATS))
            step(nc.vector.tensor_copy(MEX[:, 0:1], MV[:, 0:1]))
            step(nc.vector.scalar_tensor_tensor(out=MEX[:, 1:2], in0=MV[:, 0:1], scalar=MV[:, 0:1], in1=MV[:, 1:2],
                                                op0=ALU.mult, op1=ALU.add))
            dve.wait_ge(stats_mm, 1)
            step(nc.vector.tensor_copy(MEXT, PS[:, 7, 0:2]))
            step(nc.vector.tensor_tensor(MSQ, MEXT[:, 0:1], MEXT[:, 0:1], ALU.mult))
            nc.vector.tensor_tensor(VAR, MEXT[:, 1:2], MSQ, ALU.subtract).then_inc(var_set, 1)
            dve.wait_ge(sdev_set, 1)
            step(nc.vector.reciprocal(RSD, SDEV))
            step(nc.vector.tensor_tensor(BSCALE, RSD, par("fgam"), ALU.mult))
            step(nc.vector.tensor_tensor(MS, MEXT[:, 0:1], BSCALE, ALU.mult))
            step(nc.vector.tensor_tensor(BBIAS, par("fbet"), MS, ALU.subtract))
            nc.vector.tensor_scalar(SDIAG, par("ident"), BSCALE, None, ALU.mult).then_inc(sdiag_set, 1)
            nc.vector.memset(ONB, 1.0).then_inc(eb_step, 1)
            n_eb = [1]

            def estep(ins):
                n_eb[0] += 1
                ins.then_inc(eb_step, 1)
                dve.wait_ge(eb_step, n_eb[0])

            eb = par("eb")
            estep(nc.vector.tensor_copy(EBS[0:96, :], eb[0:96, :]))
            estep(nc.vector.tensor_tensor(EBF[0:96, :], eb[0:96, :], EBS[0:96, :], ALU.subtract))
            estep(nc.vector.tensor_copy(EBT[0:96, :], EBF[0:96, :]))
            estep(nc.vector.tensor_copy(EBS[32:64, :], EBF[32:64, :]))
            estep(nc.vector.tensor_tensor(EBF[0:96, :], EBF[0:96, :], EBT[0:96, :], ALU.subtract))
            nc.vector.tensor_copy(EBS[64:96, :], EBF[64:96, :]).then_inc(eb_set, 1)
            dve.wait_ge(wdt_mm, 1)
            nc.vector.tensor_copy(WDT[:, :], PS[:, 3, 0:128]).then_inc(wdt_set, 1)
            ends = YP[:, :, CHUNK:L + 1:CHUNK]
            dve.wait_ge(rec_y, len(REC_STEPS) - CHUNK)
            nc.vector.tensor_copy(ENDS, ends).then_inc(ends_saved, 1)
            dve.wait_ge(rec_y, len(REC_STEPS))
            nc.vector.tensor_tensor(DIFF, ends, ENDS, ALU.not_equal).then_inc(diff_step, 1)
            dve.wait_ge(diff_step, 1)
            nc.vector.tensor_reduce(NDIFF, DIFF, AX.XY, ALU.max).then_inc(ndiff_set, 1)
            dve.wait_ge(count_mm, 1)
            nc.vector.tensor_scalar(FLAG[0:1, 0:1], PS[0:1, 2, 0:1], 1.0, None, ALU.min).then_inc(flag_set, 1)
            for j in range(J):
                dve.wait_ge(rec_done, 1)
                nc.vector.tensor_tensor(X[:, j * L:(j + 1) * L], X[:, j * L:(j + 1) * L], YP[:, j, 1:L + 1],
                                        ALU.add).then_inc(x2_set, 1)
            ln_dve(dve, 3, XN)
            dve.wait_ge(xi_pad, 1)
            for b in range(B):
                dve.wait_ge(xi_set, 2 * (b + 1))
                dst = XC[:, b * L:(b + 1) * L]
                for k in range(DC):
                    tap = par("convw")[:, k:k + 1]
                    if k == 0:
                        nc.vector.tensor_scalar(dst, XI[:, b, 0:L], tap, None, ALU.mult).then_inc(conv_step, 1)
                    else:
                        dve.wait_ge(conv_step, DC * b + k)
                        nc.vector.scalar_tensor_tensor(out=dst, in0=XI[:, b, k:k + L], scalar=tap, in1=dst,
                                                       op0=ALU.mult, op1=ALU.add).then_inc(conv_step, 1)
            dve.wait_ge(aexp_set, 1)
            nc.vector.tensor_scalar(ANEG, AEXP, -1.0, None, ALU.mult).then_inc(a_set, 1)
            for q in range(1, 2 * B + 2):
                for b in DVE_DT:
                    if q == min(DT_STEP(b), 2 * B + 1):
                        here = slice(b * L, (b + 1) * L)
                        dve.wait_ge(sp_set, b + 1)
                        dve.wait_ge(v_set, b + 1)
                        nc.vector.tensor_tensor(DT[:, here], DT[:, here], SP[:, here], ALU.add).then_inc(dve_dt_set, 1)
                if q <= 2 * B:
                    c = q - 1
                    dve.wait_ge(part_mm[1], c + 1)
                    nc.vector.tensor_copy(img((SB, SC)[c % 2], c // 2, slice(0, 64)),
                                          pair(c % 4, slice(0, 64))).then_inc(part_set[1], 1)
                if q >= 2:
                    c = q - 2
                    dve.wait_ge(part_mm[2], c + 1)
                    nc.vector.tensor_copy(img((SB, SC)[c % 2], c // 2, slice(0, 32)),
                                          pair(c % 4, slice(0, 32))).then_inc(part_set[2], 1)
            dve.wait_ge(part_set[2], 2 * B)
            dve.sem_inc(scanned, 2)
            dve.sem_inc(weighted, 2)
            dve.sem_inc(y_read, 1)

            def scan(b, s):
                dve.wait_ge(decay_set, b * DS + (s + 1))
                dve.wait_ge(u_set, b * (DS // 2) + (s // 2 + 1))
                nc.vector.tensor_tensor_scan(SLOT[s % SLOTS], DECAY[s % 2], SLOT[s % SLOTS], 0.0, ALU.mult,
                                             ALU.add).then_inc(scanned, 1)

            def weigh(b, s):
                dve.wait_ge(cbc_mm, b * DS + (s + 1))
                dve.wait_ge(scanned, b * DS + (s + 3))
                slot = img(SLOT[s % SLOTS], 0)
                nc.vector.tensor_tensor(slot, slot, pair(C_PAIR[s % 2]),
                                        ALU.mult).then_inc(weighted, 1)

            def read_y(b):
                dve.wait_ge(y_added, b * DS + (DS + SLOTS))
                xc = XC[:, bass.ds(b * L, L)].rearrange("p (a c) -> p a c", a=2)
                nc.vector.scalar_tensor_tensor(out=xc, in0=xc, scalar=par("dvec"), in1=pair(3), op0=ALU.mult,
                                               op1=ALU.add).then_inc(y_read, 1)

            for s in range(DS):
                scan(0, s)
                if s >= 1:
                    weigh(0, s - 1)
            with dve.Fori(1, B) as b:
                for s in range(DS):
                    if s == 2:
                        read_y(b - 1)
                    scan(b, s)
                    weigh(b, s - 1)
            weigh(B - 1, DS - 1)
            read_y(B - 1)
            dve.wait_ge(y_read, B + 1)
            for i in range(B + 2):
                if i % GROUPS == 1 and i > GROUPS:
                    j = i // GROUPS - 1
                    dve.wait_ge(out_mm, GROUPS * (j + 1))
                    nc.vector.tensor_tensor(img(X, j), pair(2 + j % 2), img(X, j), ALU.add).then_inc(x3_set, 1)
                if i >= B:
                    continue
                b = (i % GROUPS) * J + i // GROUPS
                here = slice(b * L, (b + 1) * L)
                dve.wait_ge(z_set, i + 1)
                nc.vector.tensor_tensor(YG[0:64, here], XC[0:64, here], GZ[0:64, here], ALU.mult).then_inc(yg_set, 1)
                nc.vector.tensor_tensor(YG[64:128, here], XC[64:128, here][:, ::-1], GZ[64:128, here],
                                        ALU.mult).then_inc(yg_set, 1)
            ln_dve(dve, 4, XN)
            n_lg = [0]

            def lstep(ins):
                n_lg[0] += 1
                ins.then_inc(lg_step, 1)
                dve.wait_ge(lg_step, n_lg[0])

            def t3(t):
                return t.rearrange("p (n e) -> p n e", e=EX)

            def over(t):
                return t.unsqueeze(2).to_broadcast([TOK, NT, EX])

            m = MROW[:, 0:NT]
            lstep(nc.vector.memset(RST, 1.0))
            lstep(nc.vector.memset(t3(RST)[:, :, 0:1], 0.0))
            dve.wait_ge(lg_mm, 1)
            rb = par("rb").unsqueeze(1).to_broadcast([TOK, NT // 2, EX])
            for h in range(2):
                lstep(nc.vector.tensor_tensor(t3(LG)[:, h * NT // 2:(h + 1) * NT // 2, :],
                                              PS[:, h, 0:NT // 2 * EX].rearrange("p (n e) -> p n e", e=EX), rb, ALU.add))
            lstep(nc.vector.tensor_reduce(m, t3(LG), AX.X, ALU.max))
            nc.vector.tensor_tensor(t3(LG), t3(LG), over(m), ALU.subtract).then_inc(lg_sub, 1)
            dve.wait_ge(lg_exp, 1)
            lstep(nc.vector.tensor_reduce(m, t3(LG), AX.X, ALU.add))
            lstep(nc.vector.reciprocal(m, m))
            lstep(nc.vector.tensor_tensor(t3(PR), t3(LG), over(m), ALU.mult))

            def first_largest(probs, sel, best):
                lstep(nc.vector.tensor_reduce(best, t3(probs), AX.X, ALU.max))
                lstep(nc.vector.tensor_tensor(t3(sel), t3(probs), over(best), ALU.is_equal))
                lstep(nc.vector.tensor_tensor_scan(CNT, RST, sel, 0.0, ALU.mult, ALU.add))
                lstep(nc.vector.scalar_tensor_tensor(out=sel, in0=CNT, scalar=1.0, in1=sel,
                                                     op0=ALU.is_equal, op1=ALU.mult))

            first_largest(PR, S1, m)
            m2 = MROW[:, NT:2 * NT]
            lstep(nc.vector.scalar_tensor_tensor(out=LG, in0=S1, scalar=-2.0, in1=PR,
                                                 op0=ALU.mult, op1=ALU.add))
            first_largest(LG, S2, m2)
            lstep(nc.vector.tensor_tensor(S1, S1, S2, ALU.add))
            lstep(nc.vector.tensor_tensor(S1, S1, PR, ALU.mult))
            lstep(nc.vector.tensor_tensor(m, m, m2, ALU.add))
            lstep(nc.vector.reciprocal(m, m))
            nc.vector.tensor_tensor(t3(PR), t3(S1), over(m), ALU.mult).then_inc(weights_set, 1)
            dve.wait_ge(weights_set, 1)
            for u in range(2 * TI):
                i, h = u // 2, u % 2
                dve.wait_ge(ex_mm, u + 1)
                if u >= 4:
                    dve.wait_ge(ex_sum, u - 3)
                n = GROUPS * i + 2 * h
                wts = t3(PR)[:, n:n + 2, :].unsqueeze(3).to_broadcast([TOK, 2, EX, C])
                nc.vector.tensor_tensor(PROD[u % 4].rearrange("p (t e c) -> p t e c", t=2, e=EX),
                                        PS[:, 2 + u % 6, :].rearrange("p (t e c) -> p t e c", t=2, e=EX),
                                        wts, ALU.mult).then_inc(ex_prod, 1)
                if u >= 1:
                    add_experts(dve, u - 1)
                if i >= 1 and i % XT == 0 and h == 1:
                    finish_tiles(dve, i // XT - 1)
            add_experts(dve, 2 * TI - 1)
            finish_tiles(dve, BANKS_XT - 1)

        @block.tensor
        def _(pe):
            def each(semaphore):
                return lambda j: pe.wait_ge(semaphore, min(j + 1, J))

            pe.wait_ge(main_loaded, 16)
            ln_pe(pe, 0, X, lambda j: pe.wait_ge(x_loaded[j], 16) if j < J else None)
            pe.wait_ge(front_loaded, 16)
            pe.wait_ge(ln[0]["out"], J)
            for j in range(J):
                if j >= 2:
                    pe.wait_ge(ctx_set, j - 1)
                pair_matmul(j % 2, fpar("wctx"), XN, j * L).then_inc(ctx_mm, 1)

            def linear(i0, i1):
                for i in range(i0, i1):
                    if i >= 2:
                        pe.wait_ge(lin_set, i - 1)
                    pair_matmul(2 + i % 2, fpar(["wg0", "wg1", "wg2", "wq", "wg3"][i // J]), XN, i % J * L).then_inc(lin_mm, 1)

            pe.wait_ge(ctx_set, J)
            for l in range(LEVELS):
                if l >= 1:
                    pe.wait_ge(gelu_set, NP * l)
                taps = KS[l] ** 2
                for t in range(taps):
                    if l < 2:
                        pe.wait_ge(diag_made, TAP0[l] + t + 1)
                    else:
                        pe.wait_ge(diag2_made, t + 1)
                    for j, r0, rows, bank in PE_UNITS:
                        last = nc.tensor.matmul(PS[:, bank, 0:rows * W], DIAG[:, (TAP0[l] + t) * 128:(TAP0[l] + t + 1) * 128],
                                                window(CP[l % 2], l, t, j, r0, rows), start=t == 0, stop=t == taps - 1)
                        if t == taps - 1 and bank != 0:
                            last.then_inc(tap_pe, 1)
                if l == 1:
                    linear(0, 2 * J)
                if l == 2:
                    linear(2 * J, 5 * J)
            pe.wait_ge(lin_set, 5 * J)
            pe.wait_ge(sel_set, 1)
            pe.wait_ge(negi_set, 1)
            keep_warm(12)
            for j in range(J):
                pe.wait_ge(glob_added, j + 1)
                pair_matmul(j, fpar("wh"), ALLC, j * L).then_inc(mod_mm, 1)
            ln_pe(pe, 1, XO, each(xo_set))
            pe.wait_ge(ln[1]["out"], J)
            nc.tensor.matmul(PS[:, 7, 0:1], fpar("wp"), fpar("beta"), start=True, stop=True).then_inc(bp_mm, 1)
            pe.wait_ge(wpg_set, 1)
            pe.wait_ge(bp_set, 1)
            for j in range(J):
                pair_matmul(j, WPG, XN, j * L).then_inc(proj_mm, 1)
            ln_pe(pe, 2, X, each(x1_set))
            pe.wait_ge(ln[2]["out"], J)
            for j in range(J):
                pair_matmul(j, par("fw"), XN, j * L).then_inc(wx_mm, 1)
            pe.wait_ge(wx_set, J)
            keep_warm(12)
            pe.wait_ge(bn_step, 3)
            nc.tensor.matmul(PS[:, 7, 0:2], par("gavg"), MEX, start=True, stop=True).then_inc(stats_mm, 1)
            nc.tensor.matmul(PS[:, 3, 0:128], par("xwd")[0:4, :], par("dtw")[0:4, :], start=True, stop=True).then_inc(wdt_mm, 1)
            pe.wait_ge(sdiag_set, 1)
            pe.wait_ge(y_zero, 2)

            def drive(k):
                return nc.tensor.matmul(PS[:, k % 2, 0:J * CHUNKS], SDIAG,
                                        WX.rearrange("p (j c k) -> p j c k", j=J, k=CHUNK)[:, :, :, k],
                                        start=True, stop=False)

            def feed(k):
                return nc.tensor.matmul(PS[:, k % 2, 0:J * CHUNKS], par("vt"),
                                        YP[:, :, k:k + 1 + CHUNK * (CHUNKS - 1):CHUNK], start=False, stop=True)

            keep_warm(4)
            drive(REC_STEPS[0])
            for q, k in enumerate(REC_STEPS):
                if q >= 1:
                    pe.wait_ge(rec_y, q)
                feed(k).then_inc(rec_mm, 1)
                if q + 1 < len(REC_STEPS):
                    drive(REC_STEPS[q + 1])
                    keep_warm(1)
            pe.wait_ge(ndiff_set, 1)
            nc.tensor.matmul(PS[0:1, 2, 0:1], NDIFF, par("ones"), start=True, stop=True).then_inc(count_mm, 1)
            pe.wait_ge(flag_set, 1)
            moved = pe.value_load(FLAG[0:1, 0:1], min_val=0, max_val=1)
            with pe.If(moved == 1):
                with pe.Fori(0, CHUNKS - 2) as p:
                    for k in range(CHUNK):
                        pe.wait_ge(slow_y, p * CHUNK + (k + 1))
                        drive(k)
                        feed(k).then_inc(slow_mm, 1)
            ln_pe(pe, 3, X, each(x2_set))
            pe.wait_ge(ln[3]["out"], J)
            pe.wait_ge(wdt_set, 1)
            pe.wait_ge(xz_loaded, 32)
            for b in range(B + 3):
                if b < B:
                    g, j = b // J, b % J
                    if b >= 2:
                        pe.wait_ge(xi_set, 2 * (b - 1))
                    pair_matmul(b % 2, INX[:, g * 128:(g + 1) * 128], XN, j * L).then_inc(in_mm, 1)
                if b >= 3:
                    i = b - 3
                    pe.wait_ge(xc_set, i + 1)
                    if i >= 2:
                        pe.wait_ge(abs_set, i - 1)
                    pair_matmul(2 + i % 2, WDT, XC, i * L).then_inc(dt_mm, 1)
            pe.wait_ge(xi_set, 2 * B)
            pe.wait_ge(negi_set, 1)
            for q in range(2 * B + 2):
                if q < 2 * B:
                    if q in (2, 3):
                        pe.wait_ge(abs_set, B - 3 + q)
                    if q >= 4:
                        pe.wait_ge(part_set[2], q - 3)
                    pair_matmul(q % 4, par(("xwb", "xwc")[q % 2]), XC, q // 2 * L, slice(0, 96)).then_inc(part_mm[0], 1)
                for i in (1, 2):
                    c = q - i
                    if 0 <= c < 2 * B:
                        pe.wait_ge(part_set[i - 1], c + 1)
                        pair_matmul(c % 4, NEGI, (SB, SC)[c % 2][0:96, :], (c // 2) * L, slice(0, 96),
                                    start=False, again=True).then_inc(part_mm[i], 1)
            pe.wait_ge(sel_set, 1)
            pe.wait_ge(part_set[2], 2 * B)
            pe.sem_inc(y_added, SLOTS)

            def spread_b(b, s):
                pe.wait_ge(bbc_copied, b * DS + (s + 1))
                pair_matmul(1, SEL[:, s * 128:(s + 1) * 128], SB[0:96, :], b * L).then_inc(bbc_mm, 1)

            def spread_c(b, s):
                pe.wait_ge(weighted, b * DS + (s + 1))
                pair_matmul(C_PAIR[s % 2], SEL[:, s * 128:(s + 1) * 128], SC[0:96, :], b * L).then_inc(cbc_mm, 1)

            def add_state(b, s):
                pe.wait_ge(weighted, b * DS + (s + 3))
                if s == 0:
                    pe.wait_ge(y_read, b + 1)
                pair_matmul(3, par("ident"), SLOT[s % SLOTS], 0, start=s == 0, stop=s == DS - 1).then_inc(y_added, 1)

            def states(b, first=False, last=False):
                for s in range(DS):
                    spread_c(b, s)
                    if s == 2:
                        spread_b(b, s + LEAD_B + 1)
                    if s >= 2:
                        add_state(b, s - 2)
                    elif not first:
                        add_state(b - 1, DS - 2 + s)
                    if s + LEAD_B + 1 >= DS:
                        if not last:
                            spread_b(b + 1, s + LEAD_B + 1 - DS)
                    elif s != 2:
                        spread_b(b, s + LEAD_B + 1)

            for s in range(LEAD_B + 1):
                spread_b(0, s)
            states(0, first=True)
            with pe.Fori(1, B - 1) as b:
                states(b)
            states(B - 1, last=True)
            add_state(B - 1, DS - 2)
            add_state(B - 1, DS - 1)
            pe.wait_ge(weighted, B * DS + 2)
            pe.wait_ge(bbc_copied, B * DS + 1)
            for i in range(B + 2):
                if i < B:
                    j, g = i // GROUPS, i % GROUPS
                    if i >= 2:
                        pe.wait_ge(z_set, i - 1)
                    pair_matmul(i % 2, INZ[:, g * 128:(g + 1) * 128], XN, j * L).then_inc(z_mm, 1)
                if i >= 2:
                    j, g = (i - 2) // GROUPS, (i - 2) % GROUPS
                    pe.wait_ge(yg_set, 2 * (i - 1))
                    if j >= 2 and g == 0:
                        pe.wait_ge(x3_set, j - 1)
                    pair_matmul(2 + j % 2, par("outw"), YG, (g * J + j) * L, slice(C * g, C * (g + 1))).then_inc(out_mm, 1)
            ln_pe(pe, 4, X, each(x3_set))
            pe.wait_ge(ln[4]["out"], J)

            for i in range(TI):
                last = nc.tensor.matmul(PS[:, i // (TI // 2), i % (TI // 2) * GROUPS * EX:(i % (TI // 2) + 1) * GROUPS * EX],
                                        tokens(XN, i), par("rw"), start=True, stop=True)
            last.then_inc(lg_mm, 1)
            pe.wait_ge(eb_set, 1)
            pe.wait_ge(experts_loaded, 16)
            pe.wait_ge(lg_step, 4)
            for i in range(TI):
                if i % XT == 0:
                    m = i // XT
                    if m >= 2:
                        pe.wait_ge(yt_set, m - 1)
                    for k in range(i, min(i + XT, TI)):
                        last = nc.tensor.matmul(PS[:, m % 2, (k - i) * 128:(k - i + 1) * 128], tokens(X, k),
                                                par("ident"), start=True, stop=True)
                    last.then_inc(xt_mm, 1)
                for h in range(2):
                    u = 2 * i + h
                    if u >= 6:
                        pe.wait_ge(ex_prod, u - 5)
                    nc.tensor.matmul(PS[:, 2 + u % 6, :], tokens(XN, i), EWB[:, h * 2 * EX * C:(h + 1) * 2 * EX * C],
                                     start=True, stop=False)
                    nc.tensor.matmul(PS[:, 2 + u % 6, :], ONB, EBS, start=False, stop=True).then_inc(ex_mm, 1)


def lay_out(inputs):
    a = {k: np.asarray(v) for k, v in inputs.items()}
    f = np.float32
    x = np.ascontiguousarray(a["x"].reshape(GROUPS, J, L, C).transpose(0, 3, 1, 2)).reshape(128, N)

    def blocks(w, times=GROUPS):
        r, c = w.shape
        o = np.zeros((times * r, times * c), f)
        for i in range(times):
            o[i * r:(i + 1) * r, i * c:(i + 1) * c] = w
        return o

    def down(w, times=GROUPS):
        return np.tile(w.reshape(w.shape[0], -1), (times, 1))

    main, front = np.zeros((128, MAIN_W), f), np.zeros((128, FRONT_W), f)

    def put(name, w):
        where = MAIN_AT if name in MAIN_AT else FRONT_AT
        (main if name in MAIN_AT else front)[0:w.shape[0], where[name]] = w

    eye, one = np.eye(128, dtype=f), blocks(np.full((C, C), 1.0 / C, f))
    put("ident", eye)
    put("cent", eye - one)
    msel = np.zeros((GROUPS, C, 60), f)
    for g in range(GROUPS):
        msel[g, :, 28 + g] = 1.0 / C
    put("msel", msel.reshape(128, 60))
    rows = np.zeros((2 * J, GROUPS, 2 * J, GROUPS, C), f)
    for r in range(2 * J):
        for g in range(GROUPS):
            rows[r, g, r, g, :] = 1.0
    rows = rows.reshape(32, 2 * J * 128)
    put("gavg", np.tile(np.eye(C, dtype=f) / GROUPS, (GROUPS, GROUPS)))
    put("ones", np.ones((128, 1), f))
    sel = np.zeros((3, 2, DS, DS, 2, DI), f)
    for d in range(2):
        for s in range(DS):
            sel[:, d, s, s, d, :] = 1.0
    sel = sel.reshape(3 * 2 * DS, DS * 128)
    wf, bf = a["L0_conv_Wf"], a["L0_conv_bf"]
    put("wq", blocks(wf[:, 0:C]))
    put("wctx", blocks(wf[:, C:2 * C]))
    for l in range(LEVELS + 1):
        put(f"wg{l}", blocks(np.tile(wf[:, 2 * C + l:2 * C + l + 1], (1, C))))
    put("bq", down(bf[0:C]))
    put("bctx", down(bf[C:2 * C]))
    put("bg", np.tile(bf[2 * C:].reshape(1, -1), (128, 1)))
    put("wh", blocks(a["L0_conv_Wh"]))
    put("wp", blocks(a["L0_conv_Wp"]))
    put("taps", np.concatenate([down(a[f"L0_conv_k{l}"].reshape(-1, C).T) for l in range(LEVELS)], 1))
    for name, key in (("bh", "bh"), ("gamma", "gamma"), ("beta", "beta"), ("bp", "bp")):
        put(name, down(a["L0_conv_" + key]))
    put("fw", blocks(a["L0_ffn_W"].T))
    put("vt", blocks(a["L0_ffn_V"].T))
    put("fgam", down(a["L0_ffn_gamma"]))
    put("fbet", down(a["L0_ffn_beta"]))
    iw, xw = a["L1_conv_in_w"], a["L1_conv_x_w"]
    xz = np.zeros((GROUPS, C, 2, GROUPS, 2, DI), f)
    for g in range(GROUPS):
        for i in range(2):
            xz[g, :, i, g, :, :] = iw[i * DI:(i + 1) * DI].T[:, None, :]
    xz = xz.reshape(128, 2 * GROUPS * 128)
    put("xwd", blocks(xw[0:DR], 2))
    put("dtw", blocks(a["L1_conv_dt_w"].T, 2))
    for name, r0 in (("xwb", DR), ("xwc", DR + DS)):
        put(name, np.tile(blocks(xw[r0:r0 + DS].T, 2), (1, 3)))
    put("outw", down(a["L1_conv_out_w"].T, 2))
    put("convw", down(a["L1_conv_conv_w"], 2))
    put("convb", down(a["L1_conv_conv_b"], 2))
    put("dvec", down(a["L1_conv_D"], 2))
    put("dtb", down(a["L1_conv_dt_b"], 2))
    put("alog", down(a["L1_conv_A_log"], 2))
    put("rw", blocks(a["L1_ffn_router_w"]))
    put("rb", np.tile(a["L1_ffn_router_b"].reshape(1, EX), (128, 1)))
    experts = blocks(np.ascontiguousarray(a["L1_ffn_expert_w"].transpose(1, 0, 2)).reshape(C, EX * C))
    eb = np.zeros((96, 2 * EX * C), f)
    eb[0:96:32] = np.tile(a["L1_ffn_expert_b"].reshape(1, EX * C), (1, 2))
    put("eb", eb)
    return {"x_in": x, "main_in": main, "front_in": front, "sel_in": sel, "rows_in": rows, "xz_in": xz,
            "experts_in": experts}


def kernel(**inputs):
    import concourse.bacc as bacc
    from concourse.bass_utils import run_bass_kernel_spmd

    nc = bacc.Bacc("TRN2", target_bir_lowering=False, num_devices=1)
    arrays = lay_out(inputs)
    args = [nc.dram_tensor(name, a.shape, mybir.dt.float32, kind="ExternalInput").ap() for name, a in arrays.items()]
    out = nc.dram_tensor("out", (B * L, C), mybir.dt.float32, kind="ExternalOutput").ap()
    build_program(nc, *args, out)
    r = run_bass_kernel_spmd(nc, [arrays], core_ids=[0])
    return r.results[0]["out"].reshape(B, H, W, C)
```

```python
import numpy as np
import concourse.bass as bass
from concourse import mybir
from contextlib import ExitStack

B, H, W, C = 16, 24, 24, 32
L = H * W
HALF = L // 2
GROUPS = 4
J = B // GROUPS
N = J * L
LEVELS = 3
KS = [3, 5, 7]
TAP0 = [0, 9, 34]
TAPS = 83
PAD = 3
HP, WP = H + 2 * PAD, W + 2 * PAD
CHUNK = 24
CHUNKS = L // CHUNK
WARM = 16
DI, DS, DC = 64, 16, 4
T2 = B * L
DR = 2
XIW = L + DC - 1
POOL_ROWS = [18, 18, H]
EX = 8
BANK = 512
TOK = 128
TI = N // TOK
NT = GROUPS * TI
XT = BANK // 128
BANKS_XT = (TI + XT - 1) // XT

MAIN = [("ident", 128), ("cent", 128), ("msel", 60), ("gavg", 128), ("fw", 128), ("vt", 128),
        ("xwd", 128), ("dtw", 128), ("xwb", 96), ("xwc", 96),
        ("outw", 32), ("rw", GROUPS * EX), ("rb", EX), ("eb", 2 * EX * C), ("convw", DC),
        ("convb", 1), ("dvec", 1), ("dtb", 1), ("alog", DS), ("fgam", 1), ("fbet", 1), ("ones", 1)]
FRONT = [("wctx", 128), ("wq", 128), ("wg0", 128), ("wg1", 128), ("wg2", 128), ("wg3", 128),
         ("wh", 128), ("wp", 128), ("taps", TAPS), ("bctx", 1), ("bq", 1), ("bg", 4), ("bh", 1),
         ("gamma", 1), ("beta", 1), ("bp", 1)]


def places(fields):
    at, out = 0, {}
    for name, width in fields:
        out[name] = slice(at, at + width)
        at += width
    return out, at


MAIN_AT, MAIN_W = places(MAIN)
FRONT_AT, FRONT_W = places(FRONT)


def build_program(nc, x_in, main_in, front_in, sel_in, rows_in, xz_in, experts_in, out):
    f32, bf16, i32 = mybir.dt.float32, mybir.dt.bfloat16, mybir.dt.int32
    ALU, ACT, AX = mybir.AluOpType, mybir.ActivationFunctionType, mybir.AxisListType
    ctx = ExitStack()
    with ctx:
        def sb(name, shape, dt=f32):
            return ctx.enter_context(nc.sbuf_tensor(name, shape, dt))[:, :]

        def sem(name):
            return ctx.enter_context(nc.semaphore(name))

        PM = sb("main_params", [128, MAIN_W])
        SEL = sb("selectors", [3 * 2 * DS, DS * 128], bf16)
        RSEL = sb("row_selectors", [128, 2 * J * 128])
        IDLE = sb("idle", [128, BANK], bf16)
        STD = sb("std", [128, HALF])
        EBS = sb("expert_bias", [96, 2 * EX * C], bf16)
        ONB = sb("bf16_ones", [96, TOK], bf16)
        INZ = sb("z_weights", [128, GROUPS * 128])
        X = sb("residual", [128, N])
        XN = sb("normed", [128, N])
        RING = sb("ring", [128, 8 * L])
        EPS = sb("eps", [128, 3])
        SM = sb("small", [128, 128])
        WDT = sb("w_dt", [128, 128])
        NEGI = sb("neg_ident", [96, 96], bf16)
        FLAG = sb("flag", [1, 1], i32)
        DECAYS = sb("decays", [128, 2 * L])
        BIG = sb("big", [128, 4 * T2])
        PS = ctx.enter_context(nc.psum_tensor("banks", [128, 8, BANK], f32))

        pos = [0]

        def big(cols):
            v = BIG[:, pos[0]:pos[0] + cols]
            pos[0] += cols
            assert pos[0] <= 4 * T2
            return v

        PF = big(FRONT_W)
        DIAG = big(TAPS * 128)
        CP = [big(J * HP * WP).rearrange("p (j h w) -> p j h w", j=J, h=HP) for _ in range(2)]
        QS = big(N)
        GS = [big(N) for _ in range(LEVELS + 1)]
        ACC = big(2 * L)
        ALLC = big(N)
        MT = big(N)
        XO = MT
        WPG = big(128)
        pos[0] = 0
        WX = big(N)
        YP = big(J * (L + 1)).rearrange("p (j t) -> p j t", j=J)
        ENDS = big(J * CHUNKS).rearrange("p (j c) -> p j c", j=J)
        DIFF = big(J * CHUNKS).rearrange("p (j c) -> p j c", j=J)
        SDIAG = big(128)
        EBF = big(2 * EX * C)
        EBT = big(EX * C).bitcast(bf16)
        pos[0] = 0
        XC = big(T2)
        DT = big(T2)
        DTX = big(T2)
        SB = big(T2 // 2).bitcast(bf16)
        SC = big(T2 // 2).bitcast(bf16)
        XI = BIG[:, 4 * T2 - B * XIW:4 * T2].rearrange("p (b t) -> p b t", b=B)
        YG = DT
        GZ = DTX
        SP = DTX
        pos[0] = 0
        LG, PR, S1, S2, RST, CNT = (big(NT * EX) for _ in range(6))
        MROW = big(2 * NT)
        PROD = [big(2 * EX * C) for _ in range(6)]
        YT = big(NT * C)
        assert pos[0] <= T2
        EWB = BIG[:, 3 * T2:3 * T2 + GROUPS * EX * C]
        SQ = [RING[:, i * L:(i + 1) * L] for i in range(2)]
        SELF = RING[0:3 * 2 * DS, 4 * L:4 * L + DS * 128]
        INX = RING[:, 4 * L:4 * L + GROUPS * 128]
        POOL_ACC = RING[:, 2 * L:3 * L]
        PROD3 = [RING[:, (5 + i) * L:(6 + i) * L] for i in range(3)]
        SLOTS = 8
        SLOT = [RING[:, i * L:(i + 1) * L] for i in range(SLOTS)]
        DECAY = [DECAYS[:, i * L:(i + 1) * L] for i in range(2)]
        AEXP, ANEG = SM[:, 0:DS], SM[:, DS:2 * DS]
        GSUM, GGLOB, BPG = SM[:, 32:37], SM[:, 40:44], SM[:, 44:45]
        MV, MEX, MEXT = SM[:, 48:50], SM[:, 52:54], SM[:, 54:56]
        MSQ, VAR, SDEV, RSD, BSCALE, MS, BBIAS, NDIFF = (SM[:, 56 + i:57 + i] for i in range(8))
        STATS, SPARE = SM[:, 64:64 + 48], SM[:, 112:128]

        LEAD_B = 4
        C_PAIR = (0, 2)

        def par(name):
            return PM[:, MAIN_AT[name]]

        def fpar(name):
            return PF[:, FRONT_AT[name]]

        def pair(p, rows=slice(0, 128)):
            return PS[rows, 2 * p:2 * p + 2, 0:HALF]

        def img(t, j, rows=slice(0, 128)):
            return t[rows, j * L:(j + 1) * L].rearrange("p (a c) -> p a c", a=2)

        def pair_matmul(p, lhsT, rhs, at, rows=slice(0, 128), start=True, stop=True, again=False):
            for a in range(2):
                last = nc.tensor.matmul(PS[rows, 2 * p + a, 0:HALF], lhsT,
                                        rhs[:, bass.ds(at + a * HALF, HALF)], start=start, stop=stop,
                                        skip_group_check=again)
            return last

        x_loaded = [sem(f"x_loaded{j}") for j in range(J)]
        first_loaded = sem("first_loaded")
        main_loaded, front_loaded, sel_loaded = sem("main_loaded"), sem("front_loaded"), sem("sel_loaded")
        xz_loaded, rows_loaded, experts_loaded = sem("xz_loaded"), sem("rows_loaded"), sem("experts_loaded")
        sel_set, consts_set, negi_set = sem("sel_set"), sem("consts_set"), sem("negi_set")
        ln = [{k: sem(f"ln{n}_{k}") for k in ("cent", "copy", "sq", "var", "std", "rstd", "back", "out")} for n in range(5)]
        pads_zero, diag_made = sem("pads_zero"), sem("diag_made")
        ctx_mm, ctx_set, lin_mm, lin_set = sem("ctx_mm"), sem("ctx_set"), sem("lin_mm"), sem("lin_set")
        tap_dve, tap_pe, gelu_set = sem("tap_dve"), sem("tap_pe"), sem("gelu_set")
        diag2_made, prod_set, tap_pool = sem("diag2_made"), sem("prod_set"), sem("tap_pool")
        gated_dve, gated_pool, ctx_sum_dve = sem("gated_dve"), sem("gated_pool"), sem("ctx_sum_dve")
        gated, ctx_sum = sem("gated"), sem("ctx_sum")
        glob_set, glob_added = sem("glob_set"), sem("glob_added")
        mod_mm, xo_set = sem("mod_mm"), sem("xo_set")
        wpg_set, bp_mm, bp_set = sem("wpg_set"), sem("bp_mm"), sem("bp_set")
        proj_mm, x1_set = sem("proj_mm"), sem("x1_set")
        wx_mm, wx_set, stats_set, stats_mm = sem("wx_mm"), sem("wx_set"), sem("stats_set"), sem("stats_mm")
        bn_step, var_set, sdev_set, sdiag_set = sem("bn_step"), sem("var_set"), sem("sdev_set"), sem("sdiag_set")
        y_zero, rec_mm, rec_y = sem("y_zero"), sem("rec_mm"), sem("rec_y")
        ends_saved, diff_step, ndiff_set = sem("ends_saved"), sem("diff_step"), sem("ndiff_set")
        count_mm, flag_set = sem("count_mm"), sem("flag_set")
        slow_mm, slow_y, rec_done, x2_set = sem("slow_mm"), sem("slow_y"), sem("rec_done"), sem("x2_set")
        xi_pad, in_mm, xi_set = sem("xi_pad"), sem("in_mm"), sem("xi_set")
        conv_step, xc_set = sem("conv_step"), sem("xc_set")
        aexp_set, a_set, wdt_mm, wdt_set = sem("aexp_set"), sem("a_set"), sem("wdt_mm"), sem("wdt_set")
        dt_mm, abs_set, v_set, sp_step, sp_set = sem("dt_mm"), sem("abs_set"), sem("v_set"), sem("sp_step"), sem("sp_set")
        dt_set, dve_dt_set, dtx_set = sem("dt_set"), sem("dve_dt_set"), sem("dtx_set")
        part_mm = [sem(f"part{i}_mm") for i in range(3)]
        part_set = [sem(f"part{i}_set") for i in range(3)]
        wait_taken = sem("wait_taken")
        bbc_mm, bbc_copied, u_set, decay_set, scanned = (sem("bbc_mm"), sem("bbc_copied"), sem("u_set"),
                                                         sem("decay_set"), sem("scanned"))
        cbc_mm, weighted, y_added, y_read = sem("cbc_mm"), sem("weighted"), sem("y_added"), sem("y_read")
        z_mm, z_set, yg_set, out_mm, x3_set = sem("z_mm"), sem("z_set"), sem("yg_set"), sem("out_mm"), sem("x3_set")
        lg_mm, lg_step, lg_sub, lg_exp, weights_set = (sem("lg_mm"), sem("lg_step"), sem("lg_sub"), sem("lg_exp"),
                                                       sem("weights_set"))
        middle_act = sem("middle_act")
        halved = sem("halved")
        yg_turned, yg_turned_pool, ex_sum_pool = sem("yg_turned"), sem("yg_turned_pool"), sem("ex_sum_pool")
        eb_step, eb_set, ex_mm, ex_prod, ex_sum = sem("eb_step"), sem("eb_set"), sem("ex_mm"), sem("ex_prod"), sem("ex_sum")
        xt_mm, yt_set, stored = sem("xt_mm"), sem("yt_set"), sem("stored")

        DVE_PIECES = [(0, 0, H), (1, 0, H)]
        PE_UNITS = [(2, POOL_ROWS[0], H - POOL_ROWS[0], 2), (3, 0, H // 2, 0), (3, H // 2, H // 2, 1)]
        NP = 5
        LINEAR_AFTER = [[], list(range(3, 20, 5)), list(range(1, 48, 3))]
        GELU_OF = [[1, 2, 4, 5], [1, 2, 4, 5], [1, 2, 3, 4]]

        DVE_DT = [b for b in range(B) if b % 4 >= 2]
        BATCH = 8

        ACT_MIDDLES = 20

        def dt_step(b):
            return (2 * BATCH * (b // BATCH) + BATCH + b % BATCH + 1) * 2 // 3 + 3

        REC_STEPS = list(range(CHUNK - WARM, CHUNK)) + 2 * list(range(CHUNK))

        def inside(cp, j, r0=0, rows=H):
            return cp[:, j, PAD + r0:PAD + r0 + rows, PAD:PAD + W]

        def window(cp, l, tap, j, r0, rows):
            dy, dx = tap // KS[l] - KS[l] // 2, tap % KS[l] - KS[l] // 2
            return cp[:, j, PAD + r0 + dy:PAD + r0 + dy + rows, PAD + dx:PAD + dx + W]

        def adds(l, t=0):
            return TAP0[l] - l + max(t - 1, 0)

        def rows_of(t, j, r0=0, rows=H):
            return t[:, j * L + r0 * W:j * L + (r0 + rows) * W].rearrange("p (h w) -> p h w", w=W)

        BACK_PAIR = (2, 0, 1, 2)

        def keep_warm(times):
            for _ in range(times):
                nc.tensor.matmul(PS[:, 6, :], IDLE[:, 0:128], IDLE, start=True, stop=True)

        def ln_pe(pe, n, src, ready):
            s = ln[n]
            for j in range(J + 1):
                if j < J:
                    ready(j)
                    if j >= 2:
                        pe.wait_ge(s["copy"], j - 1)
                    pair_matmul(j % 2, par("cent"), src, j * L).then_inc(s["cent"], 1)
                if j == 1:
                    ready(J)
                if j >= 1:
                    i = j - 1
                    pe.wait_ge(s["sq"], i + 1)
                    for a in range(2):
                        r0 = GROUPS * (2 * i + a)
                        last = nc.tensor.matmul(PS[0:32, 7, 0:HALF], par("msel")[:, 28 - r0:60 - r0],
                                                SQ[i % 2][:, a * HALF:(a + 1) * HALF],
                                                start=r0 == 0, stop=r0 == 28)
                    last.then_inc(s["var"], 1)
            keep_warm(10)
            pe.wait_ge(s["rstd"], 1)
            if n == 0:
                pe.wait_ge(rows_loaded, 16)
                pe.wait_ge(consts_set, 8)
            for j in range(J):
                if j == 3:
                    pe.wait_ge(s["out"], 1)
                for a in range(2):
                    r = 2 * j + a
                    last = nc.tensor.matmul(PS[:, 2 * BACK_PAIR[j] + a, 0:HALF], RSEL[:, r * 128:(r + 1) * 128],
                                            STD, start=True, stop=True)
                last.then_inc(s["back"], 1)

        def bring_table(function, i):
            nc.scalar.activation(SPARE[:, i:i + 1], EPS[:, 0:1], function)

        def ln_act(act, n, eps, dst):
            s = ln[n]
            bring_table(ACT.Sqrt, n)
            for j in range(J):
                act.wait_ge(s["copy"], j + 1)
                if j >= 2:
                    act.wait_ge(s["var"], j - 1)
                nc.scalar.activation(SQ[j % 2], dst[:, j * L:(j + 1) * L], ACT.Square).then_inc(s["sq"], 1)
            act.wait_ge(s["var"], J)
            nc.scalar.activation(STD[0:32, :], PS[0:32, 7, 0:HALF], ACT.Sqrt, bias=EPS[0:32, eps:eps + 1]).then_inc(s["std"], 1)

        def ln_dve(dve, n, dst):
            s = ln[n]
            for j in range(J):
                dve.wait_ge(s["cent"], j + 1)
                nc.vector.tensor_copy(img(dst, j), pair(j % 2)).then_inc(s["copy"], 1)
            dve.wait_ge(s["std"], 1)
            nc.vector.reciprocal(STD[0:32, :], STD[0:32, :]).then_inc(s["rstd"], 1)
            dve.wait_ge(s["copy"], J)
            for j in range(J):
                dve.wait_ge(s["back"], j + 1)
                nc.vector.tensor_tensor(img(dst, j), img(dst, j), pair(BACK_PAIR[j]), ALU.mult).then_inc(s["out"], 1)

        def tokens(t, i):
            return t[:, i:N:TI]

        YT4 = YT.rearrange("p (g i c) -> p g i c", g=GROUPS, i=TI)

        POOL_SUMS = list(range(1, 2 * TI, 3))

        def wait_sums(engine, u):
            on_pool = len([v for v in POOL_SUMS if v < u])
            if u > on_pool:
                engine.wait_ge(ex_sum, u - on_pool)
            if on_pool:
                engine.wait_ge(ex_sum_pool, on_pool)

        def add_experts(dve, u):
            i, h = u // 2, u % 2
            dve.wait_ge(ex_prod, u + 1)
            nc.vector.tensor_reduce(YT4[:, 2 * h:2 * h + 2, i, :],
                                    PROD[u % 6].rearrange("p (t e c) -> p t c e", t=2, e=EX),
                                    AX.X, ALU.add).then_inc(ex_sum, 1)

        def finish_tiles(dve, m):
            i0, i1 = XT * m, min(XT * (m + 1), TI)
            dve.wait_ge(xt_mm, m + 1)
            wait_sums(dve, 2 * i1)
            here = YT4[:, :, i0:i1, :].rearrange("p g i c -> p i g c")
            res = PS[:, m % 2, 0:(i1 - i0) * 128].rearrange("p (i g c) -> p i g c", g=GROUPS, c=C)
            nc.vector.tensor_tensor(here, here, res, ALU.add).then_inc(yt_set, 1)

        block = ctx.enter_context(nc.Block())

        @block.sync
        def _(sp):
            sp.dma_start(X[:, 0:L], x_in[:, 0:L]).then_inc(x_loaded[0], 16)
            first = MAIN_AT["msel"].stop
            sp.dma_start(PM[:, 0:first], main_in[:, 0:first]).then_inc(first_loaded, 16)
            for j in range(1, J):
                sp.dma_start(X[:, j * L:(j + 1) * L], x_in[:, j * L:(j + 1) * L]).then_inc(x_loaded[j], 16)
            sp.dma_start(PM[:, first:], main_in[:, first:]).then_inc(main_loaded, 16)
            sp.dma_start(INZ, xz_in[:, GROUPS * 128:]).then_inc(xz_loaded, 16)
            sp.wait_ge(sel_set, 1)
            sp.dma_start(INX, xz_in[:, 0:GROUPS * 128]).then_inc(xz_loaded, 16)
            sp.wait_ge(bbc_copied, B * DS + 1)
            sp.dma_start(EWB, experts_in).then_inc(experts_loaded, 16)
            out_v = out.rearrange("(g p i) c -> p g (i c)", g=GROUPS, p=TOK)
            yt_v = YT.rearrange("p (g r) -> p g r", g=GROUPS)
            for m in range(0, BANKS_XT, 2):
                here = slice(XT * m * C, min(XT * (m + 2), TI) * C)
                sp.wait_ge(yt_set, min(m + 2, BANKS_XT))
                sp.dma_start(out_v[:, :, here], yt_v[:, :, here]).then_inc(stored, 16)
            sp.wait_ge(stored, 16 * ((BANKS_XT + 1) // 2))

        @block.gpsimd
        def _(pool):
            pool.dma_start(PF, front_in).then_inc(front_loaded, 16)
            pool.dma_start(RSEL[0:32, :], rows_in).then_inc(rows_loaded, 16)
            pool.dma_start(SELF, sel_in).then_inc(sel_loaded, 16)
            for cp in CP:
                nc.gpsimd.memset(cp, 0.0).then_inc(pads_zero, 1)
            pool.wait_ge(first_loaded, 16)
            pool.wait_ge(front_loaded, 16)
            for t in range(TAP0[2]):
                nc.gpsimd.tensor_scalar(DIAG[:, t * 128:(t + 1) * 128], par("ident"),
                                        fpar("taps")[:, t:t + 1], None, ALU.mult).then_inc(diag_made, 1)
            def add_taps(l):
                for t in range(1, KS[l] ** 2):
                    pool.wait_ge(prod_set, TAP0[l] + t + 1)
                    if t >= 2:
                        pool.wait_ge(tap_pool, adds(l, t))
                    nc.gpsimd.tensor_tensor(POOL_ACC[:, 0:POOL_ROWS[l] * W], POOL_ACC[:, 0:POOL_ROWS[l] * W],
                                            PROD3[(TAP0[l] + t) % 3][:, 0:POOL_ROWS[l] * W], ALU.add).then_inc(tap_pool, 1)

            add_taps(0)
            add_taps(1)
            add_taps(2)
            j = J - 1
            total, part = ALLC[:, j * L:(j + 1) * L], MT[:, j * L:(j + 1) * L]
            for l in (1, 2):
                pool.wait_ge(lin_set, (l + 1) * J)
                pool.wait_ge(gelu_set, NP * l + GELU_OF[l][j])
                if l == 2:
                    pool.wait_ge(ctx_sum, 1)
                nc.gpsimd.tensor_tensor(rows_of(MT, j), inside(CP[(l + 1) % 2], j), rows_of(GS[l], j),
                                        ALU.mult).then_inc(gated_pool, 1)
                pool.wait_ge(gated, J)
                pool.wait_ge(gated_pool, l)
                nc.gpsimd.tensor_tensor(total, total, part, ALU.add).then_inc(ctx_sum, 1)
            pool.wait_ge(x2_set, J)
            nc.gpsimd.memset(XI[:, :, 0:DC - 1], 0.0).then_inc(xi_pad, 1)
            for b in range(B):
                pool.wait_ge(v_set, b + 1)
                pool.wait_ge(sp_set, b + 1)
                here = slice(b * L, (b + 1) * L)
                if b in DVE_DT:
                    pool.wait_ge(dve_dt_set, DVE_DT.index(b) + 1)
                else:
                    nc.gpsimd.tensor_tensor(DT[:, here], DT[:, here], SP[:, here], ALU.add).then_inc(dt_set, 1)
                    pool.wait_ge(dt_set, b - len([i for i in DVE_DT if i < b]) + 1)
                nc.gpsimd.tensor_tensor(DTX[:, here], DT[:, here], XC[:, here], ALU.mult).then_inc(dtx_set, 1)
            pool.wait_ge(dtx_set, B)
            with pool.Fori(0, B) as b:
                for s in range(0, DS, 2):
                    pool.wait_ge(bbc_copied, b * DS + (s + 3))
                    pool.sem_inc(wait_taken, 1)
                    two = RING[:, s % SLOTS * L:(s % SLOTS + 2) * L].rearrange("p (s t) -> p s t", s=2)
                    nc.gpsimd.tensor_tensor(two, DTX[:, bass.ds(b * L, L)].unsqueeze(1).to_broadcast([128, 2, L]), two,
                                            ALU.mult).then_inc(u_set, 1)

            pool.wait_ge(y_read, B + 1)
            for i in range(1, B, 2):
                b = (i % GROUPS) * J + i // GROUPS
                here = slice(b * L, (b + 1) * L)
                pool.wait_ge(z_set, i + 1)
                nc.gpsimd.tensor_tensor(YG[64:128, here], XC[64:128, here][:, ::-1], GZ[64:128, here],
                                        ALU.mult).then_inc(yg_turned_pool, 1)
            for k, u in enumerate(POOL_SUMS):
                i, h = u // 2, u % 2
                halves = PROD[u % 6].rearrange("p (t r) -> p t r", t=2)
                pool.wait_ge(ex_prod, u + 1)
                for n, width in enumerate((4 * C, 2 * C)):
                    nc.gpsimd.tensor_tensor(halves[:, :, 0:width], halves[:, :, 0:width], halves[:, :, width:2 * width],
                                            ALU.add).then_inc(halved, 1)
                    pool.wait_ge(halved, 2 * k + n + 1)
                nc.gpsimd.tensor_tensor(YT4[:, 2 * h:2 * h + 2, i, :], halves[:, :, 0:C], halves[:, :, C:2 * C],
                                        ALU.add).then_inc(ex_sum_pool, 1)

        @block.scalar
        def _(act):
            act.wait_ge(consts_set, 4)
            ln_act(act, 0, 0, XN)
            act.wait_ge(front_loaded, 16)
            act.wait_ge(pads_zero, 2)
            for j in range(J):
                act.wait_ge(ctx_mm, j + 1)
                for a in range(2):
                    last = nc.scalar.activation(inside(CP[0], j, a * H // 2, H // 2),
                                                PS[:, 2 * (j % 2) + a, 0:HALF].rearrange("p (h w) -> p h w", w=W),
                                                ACT.Identity, bias=fpar("bctx"))
                last.then_inc(ctx_set, 1)

            def linear(i):
                m, j = i // J, i % J
                act.wait_ge(lin_mm, i + 1)
                dst = (GS[0], GS[1], GS[2], QS, GS[3])[m]
                bias = fpar("bq") if m == 3 else fpar("bg")[:, min(m, 3):min(m, 3) + 1]
                nc.scalar.activation(img(dst, j), pair(2 + i % 2), ACT.Identity, bias=bias).then_inc(lin_set, 1)

            bring_table(ACT.Gelu, 8)
            act.wait_ge(sel_set, 1)
            for l in range(LEVELS):
                dst = CP[(l + 1) % 2]
                if l == 0:
                    act.wait_ge(ctx_set, 3)
                else:
                    act.wait_ge(gelu_set, NP * l)
                for t in range(KS[l] ** 2):
                    n = TAP0[l] + t
                    if t >= 1 and adds(l, t) >= 3:
                        act.wait_ge(tap_pool, adds(l, t - 2) if t >= 3 else adds(l, 0))
                    prod = POOL_ACC if t == 0 else PROD3[n % 3]
                    nc.scalar.activation(rows_of(prod, 0, 0, POOL_ROWS[l]), window(CP[l % 2], l, t, 2, 0, POOL_ROWS[l]),
                                         ACT.Identity, scale=fpar("taps")[:, n:n + 1]).then_inc(prod_set, 1)
                    if l == 1:
                        for m in range(2 * t, min(2 * t + 2, KS[2] ** 2)):
                            nc.scalar.activation(DIAG[:, (TAP0[2] + m) * 128:(TAP0[2] + m + 1) * 128], par("ident"),
                                                 ACT.Identity, scale=fpar("taps")[:, TAP0[2] + m:TAP0[2] + m + 1]
                                                 ).then_inc(diag2_made, 1)
                    if t in LINEAR_AFTER[l]:
                        linear(LINEAR_AFTER[l].index(t) + (J if l == 2 else 0))
                if l == 2:
                    act.wait_ge(gated, J)
                for i, (j, r0, rows) in enumerate(DVE_PIECES):
                    act.wait_ge(tap_dve, 2 * (TAP0[l] + KS[l] ** 2 - 1) + i + 1)
                    acc = ACC[:, j * L:j * L + rows * W].rearrange("p (h w) -> p h w", w=W)
                    nc.scalar.activation(inside(dst, j, r0, rows), acc, ACT.Gelu,
                                         accum_out=GSUM[:, i:i + 1] if l == 2 else None).then_inc(gelu_set, 1)
                act.wait_ge(tap_pool, adds(l + 1) if l + 1 < LEVELS else TAPS - LEVELS)
                nc.scalar.activation(inside(dst, 2, 0, POOL_ROWS[l]), rows_of(POOL_ACC, 0, 0, POOL_ROWS[l]),
                                     ACT.Gelu, accum_out=GSUM[:, 2:3] if l == 2 else None).then_inc(gelu_set, 1)
                if l < 2:
                    act.wait_ge(tap_pe, 2 * l + 1)
                    j, r0, rows, bank = PE_UNITS[0]
                    nc.scalar.activation(inside(dst, j, r0, rows), PS[:, bank, 0:rows * W].rearrange("p (h w) -> p h w", w=W),
                                         ACT.Gelu).then_inc(gelu_set, 1)
                act.wait_ge(tap_pe, min(2 * l + 2, 5))
                nc.scalar.activation(inside(dst, 3).rearrange("p (a h) w -> p a h w", a=2),
                                     pair(0).rearrange("p a (h w) -> p a h w", w=W),
                                     ACT.Gelu, accum_out=GSUM[:, 3:4] if l == 2 else None).then_inc(gelu_set, 1)
            act.wait_ge(gelu_set, NP * LEVELS - 1)
            nc.scalar.activation(GGLOB, GSUM[:, 0:4], ACT.Gelu, scale=1.0 / L).then_inc(glob_set, 1)
            ln_act(act, 1, 1, XN)
            ln_act(act, 2, 2, XN)
            for j in range(J):
                act.wait_ge(wx_mm, j + 1)
                nc.scalar.activation(img(WX, j), pair(j), ACT.Copy).then_inc(wx_set, 1)
            act.wait_ge(var_set, 1)
            nc.scalar.activation(SDEV, VAR, ACT.Sqrt, bias=EPS[:, 2:3]).then_inc(sdev_set, 1)
            bring_table(ACT.Sigmoid, 5)
            act.wait_ge(sdiag_set, 1)

            def recur(k):
                return nc.scalar.activation(YP[:, :, k + 1:k + 2 + CHUNK * (CHUNKS - 1):CHUNK],
                                            PS[:, k % 2, 0:J * CHUNKS].rearrange("p (j c) -> p j c", j=J),
                                            ACT.Sigmoid, bias=BBIAS)

            for q, k in enumerate(REC_STEPS):
                act.wait_ge(rec_mm, q + 1)
                if q == len(REC_STEPS) - 1:
                    act.wait_ge(ends_saved, 1)
                recur(k).then_inc(rec_y, 1)
            act.wait_ge(flag_set, 1)
            moved = act.value_load(FLAG[0:1, 0:1], min_val=0, max_val=1)
            with act.If(moved == 1):
                act.sem_inc(slow_y, 1)
                with act.Fori(0, CHUNKS - 2) as p:
                    for k in range(CHUNK):
                        act.wait_ge(slow_mm, p * CHUNK + (k + 1))
                        recur(k).then_inc(slow_y, 1)
                act.wait_ge(slow_y, (CHUNKS - 2) * CHUNK + 1)
            act.sem_inc(rec_done, 1)
            ln_act(act, 3, 0, XN)
            bring_table(ACT.Silu, 6)
            for b in range(B + 3):
                if b < B:
                    act.wait_ge(in_mm, b + 1)
                    nc.scalar.activation(XI[0:64, b, DC - 1:].rearrange("p (a c) -> p a c", a=2),
                                         pair(b % 2, slice(0, 64)), ACT.Copy).then_inc(xi_set, 1)
                    nc.scalar.activation(XI[64:128, b, DC - 1:][:, ::-1].rearrange("p (a c) -> p a c", a=2),
                                         pair(b % 2, slice(64, 128)), ACT.Copy).then_inc(xi_set, 1)
                if 2 <= b < B + 2:
                    act.wait_ge(conv_step, DC * (b - 1))
                    xc_b = XC[:, (b - 2) * L:(b - 1) * L]
                    nc.scalar.activation(xc_b, xc_b, ACT.Silu, bias=par("convb")).then_inc(xc_set, 1)
                if b >= 3:
                    i = b - 3
                    act.wait_ge(dt_mm, i + 1)
                    nc.scalar.activation(img(DT, i), pair(2 + i % 2), ACT.Relu, bias=par("dtb")).then_inc(v_set, 1)
                    nc.scalar.activation(img(SP, i), pair(2 + i % 2), ACT.Abs, bias=par("dtb")).then_inc(abs_set, 1)
            nc.scalar.activation(AEXP, par("alog"), ACT.Exp).then_inc(aexp_set, 1)
            batches = [(f, b) for b0 in range(0, B, BATCH) for f in (ACT.Exp, ACT.Ln)
                       for b in range(b0, b0 + BATCH)]
            for c in range(2 * B + 1):
                if c < 2 * B:
                    act.wait_ge(part_mm[0], c + 1)
                    nc.scalar.activation(img((SB, SC)[c % 2], c // 2, slice(0, 96)), pair(c % 4, slice(0, 96)),
                                         ACT.Copy).then_inc(part_set[0], 1)
                if c > ACT_MIDDLES:
                    act.wait_ge(part_mm[1], c)
                    nc.scalar.activation(img((SB, SC)[(c - 1) % 2], (c - 1) // 2, slice(0, 64)),
                                         pair((c - 1) % 4, slice(0, 64)), ACT.Copy).then_inc(middle_act, 1)
                for f, b in batches[3 * c // 2:3 * (c + 1) // 2]:
                    sp_b = SP[:, b * L:(b + 1) * L]
                    if f == ACT.Exp:
                        act.wait_ge(abs_set, b + 1)
                        nc.scalar.activation(sp_b, sp_b, f, scale=-1.0).then_inc(sp_step, 1)
                    else:
                        act.wait_ge(sp_step, b + 1)
                        nc.scalar.activation(sp_b, sp_b, f, bias=1.0).then_inc(sp_set, 1)
            act.wait_ge(a_set, 1)
            bring_table(ACT.Exp, 7)
            act.wait_ge(part_set[2], 2 * B - 2)
            act.sem_inc(bbc_copied, 1)

            def copy_b(i, s):
                act.wait_ge(bbc_mm, i + 1)
                act.wait_ge(y_added, i + 1)
                nc.scalar.activation(img(SLOT[s % SLOTS], 0), pair(1), ACT.Copy).then_inc(bbc_copied, 1)

            def decay(b, s, i):
                act.wait_ge(scanned, i + 1)
                act.sem_inc(wait_taken, 1)
                nc.scalar.activation(DECAY[s % 2], DT[:, bass.ds(b * L, L)], ACT.Exp,
                                     scale=ANEG[:, s:s + 1]).then_inc(decay_set, 1)

            for s in range(LEAD_B):
                copy_b(s, s)
            act.wait_ge(dtx_set, B)
            decay(0, 0, 0)
            with act.Fori(0, B - 1) as b:
                for s in range(DS):
                    decay(b + (s + 1) // DS, (s + 1) % DS, b * DS + (s + 1))
                    copy_b(b * DS + (s + LEAD_B), s + LEAD_B)
            for s in range(DS - 1):
                decay(B - 1, s + 1, (B - 1) * DS + s + 1)
                if s + LEAD_B < DS:
                    copy_b((B - 1) * DS + s + LEAD_B, s + LEAD_B)
            for i in range(B):
                j, b = i // GROUPS, (i % GROUPS) * J + i // GROUPS
                act.wait_ge(z_mm, i + 1)
                nc.scalar.activation(img(GZ, b), pair(i % 2), ACT.Silu).then_inc(z_set, 1)
            ln_act(act, 4, 2, XN)
            act.wait_ge(lg_sub, 1)
            nc.scalar.activation(LG, LG, ACT.Exp).then_inc(lg_exp, 1)

        @block.vector
        def _(dve):
            nc.vector.memset(IDLE, 0.0).then_inc(consts_set, 1)
            for i, eps in enumerate((1e-6, 1e-3, 1e-5)):
                nc.vector.memset(EPS[:, i:i + 1], eps).then_inc(consts_set, 1)
            for rows in (slice(32, 64), slice(64, 128)):
                nc.vector.memset(RSEL[rows, :], 0.0).then_inc(consts_set, 1)
                nc.vector.memset(STD[rows, :], 0.0).then_inc(consts_set, 1)
            ln_dve(dve, 0, XN)
            dve.wait_ge(sel_loaded, 16)
            nc.vector.tensor_copy(SEL[:, :], SELF).then_inc(sel_set, 1)
            dve.wait_ge(main_loaded, 16)
            nc.vector.tensor_scalar(NEGI[:, :], par("ident")[0:96, 0:96], -1.0, None, ALU.mult).then_inc(negi_set, 1)
            dve.wait_ge(front_loaded, 16)
            for l in range(LEVELS):
                src = CP[l % 2]
                if l == 2:
                    dve.wait_ge(lin_set, J)
                    dve.wait_ge(gelu_set, NP)
                    for j in range(J):
                        nc.vector.tensor_tensor(rows_of(ALLC, j), inside(CP[1], j), rows_of(GS[0], j),
                                                ALU.mult).then_inc(gated, 1)
                for t in range(KS[l] ** 2):
                    for i, (j, r0, rows) in enumerate(DVE_PIECES):
                        if t == 0 and l == 0:
                            dve.wait_ge(ctx_set, j + 1)
                        elif t == 0:
                            dve.wait_ge(gelu_set, NP * (l - 1) + GELU_OF[l - 1][j])
                        n = 2 * (TAP0[l] + t) + i
                        acc = ACC[:, j * L:j * L + rows * W].rearrange("p (h w) -> p h w", w=W)
                        win = window(src, l, t, j, r0, rows)
                        tap = fpar("taps")[:, TAP0[l] + t:TAP0[l] + t + 1]
                        if t == 0:
                            nc.vector.tensor_scalar(acc, win, tap, None, ALU.mult).then_inc(tap_dve, 1)
                        else:
                            dve.wait_ge(tap_dve, n - 1)
                            nc.vector.scalar_tensor_tensor(out=acc, in0=win, scalar=tap, in1=acc, op0=ALU.mult,
                                                           op1=ALU.add).then_inc(tap_dve, 1)
            dve.wait_ge(lin_set, 2 * J)
            dve.wait_ge(gelu_set, 2 * NP)
            dve.wait_ge(gated, J)

            def gate(l, j, n):
                total = ALLC[:, j * L:(j + 1) * L]
                nc.vector.tensor_tensor(rows_of(MT, j), inside(CP[(l + 1) % 2], j), rows_of(GS[l], j),
                                        ALU.mult).then_inc(gated_dve, 1)
                dve.wait_ge(gated_dve, n)
                nc.vector.tensor_tensor(total, total, MT[:, j * L:(j + 1) * L], ALU.add).then_inc(ctx_sum_dve, 1)

            for j in range(J - 1):
                gate(1, j, j + 1)
            dve.wait_ge(lin_set, 3 * J)
            for j in range(J - 1):
                dve.wait_ge(gelu_set, NP * 2 + GELU_OF[2][j])
                dve.wait_ge(ctx_sum_dve, j + 1)
                gate(2, j, J + j)
            nc.vector.tensor_scalar(WPG, fpar("wp"), fpar("gamma"), None, ALU.mult).then_inc(wpg_set, 1)
            dve.wait_ge(glob_set, 1)
            dve.wait_ge(lin_set, 5 * J)
            dve.wait_ge(ctx_sum_dve, 2 * (J - 1))
            for j in range(J):
                if j == J - 1:
                    dve.wait_ge(ctx_sum, 2)
                here = slice(j * L, (j + 1) * L)
                nc.vector.scalar_tensor_tensor(out=ALLC[:, here], in0=GS[LEVELS][:, here], scalar=GGLOB[:, j:j + 1],
                                               in1=ALLC[:, here], op0=ALU.mult, op1=ALU.add).then_inc(glob_added, 1)
            for j in range(J):
                dve.wait_ge(mod_mm, j + 1)
                nc.vector.scalar_tensor_tensor(out=img(XO, j), in0=pair(j), scalar=fpar("bh"), in1=img(QS, j),
                                               op0=ALU.add, op1=ALU.mult).then_inc(xo_set, 1)
            ln_dve(dve, 1, XN)
            dve.wait_ge(bp_mm, 1)
            nc.vector.tensor_tensor(BPG, PS[:, 7, 0:1], fpar("bp"), ALU.add).then_inc(bp_set, 1)
            dve.wait_ge(bp_set, 1)
            for j in range(J):
                dve.wait_ge(proj_mm, j + 1)
                nc.vector.scalar_tensor_tensor(out=img(X, j), in0=pair(j), scalar=BPG, in1=img(X, j),
                                               op0=ALU.add, op1=ALU.add).then_inc(x1_set, 1)
            ln_dve(dve, 2, XN)
            nc.vector.memset(YP[:, :, 0:1], 0.0).then_inc(y_zero, 1)
            nc.vector.memset(YP[:, :, CHUNK - WARM:L:CHUNK], 0.0).then_inc(y_zero, 1)
            for i in range(2 * J):
                dve.wait_ge(wx_set, i // 2 + 1)
                nc.vector.bn_stats(STATS[:, 6 * i:6 * i + 6], WX[:, i * HALF:(i + 1) * HALF]).then_inc(stats_set, 1)
            dve.wait_ge(stats_set, 2 * J)
            steps = [0]

            def step(ins):
                steps[0] += 1
                ins.then_inc(bn_step, 1)
                dve.wait_ge(bn_step, steps[0])

            step(nc.vector.bn_aggr(MV, STATS))
            step(nc.vector.tensor_copy(MEX[:, 0:1], MV[:, 0:1]))
            step(nc.vector.scalar_tensor_tensor(out=MEX[:, 1:2], in0=MV[:, 0:1], scalar=MV[:, 0:1], in1=MV[:, 1:2],
                                                op0=ALU.mult, op1=ALU.add))
            dve.wait_ge(stats_mm, 1)
            step(nc.vector.tensor_copy(MEXT, PS[:, 7, 0:2]))
            step(nc.vector.tensor_tensor(MSQ, MEXT[:, 0:1], MEXT[:, 0:1], ALU.mult))
            nc.vector.tensor_tensor(VAR, MEXT[:, 1:2], MSQ, ALU.subtract).then_inc(var_set, 1)
            dve.wait_ge(sdev_set, 1)
            step(nc.vector.reciprocal(RSD, SDEV))
            step(nc.vector.tensor_tensor(BSCALE, RSD, par("fgam"), ALU.mult))
            step(nc.vector.tensor_tensor(MS, MEXT[:, 0:1], BSCALE, ALU.mult))
            step(nc.vector.tensor_tensor(BBIAS, par("fbet"), MS, ALU.subtract))
            nc.vector.tensor_scalar(SDIAG, par("ident"), BSCALE, None, ALU.mult).then_inc(sdiag_set, 1)
            nc.vector.memset(ONB, 1.0).then_inc(eb_step, 1)
            n_eb = [1]

            def estep(ins):
                n_eb[0] += 1
                ins.then_inc(eb_step, 1)
                dve.wait_ge(eb_step, n_eb[0])

            eb = par("eb")
            estep(nc.vector.tensor_copy(EBS[0:96, :], eb[0:96, :]))
            estep(nc.vector.tensor_tensor(EBF[0:96, :], eb[0:96, :], EBS[0:96, :], ALU.subtract))
            estep(nc.vector.tensor_copy(EBT[0:96, :], EBF[0:96, :]))
            estep(nc.vector.tensor_copy(EBS[32:64, :], EBF[32:64, :]))
            estep(nc.vector.tensor_tensor(EBF[0:96, :], EBF[0:96, :], EBT[0:96, :], ALU.subtract))
            nc.vector.tensor_copy(EBS[64:96, :], EBF[64:96, :]).then_inc(eb_set, 1)
            dve.wait_ge(wdt_mm, 1)
            nc.vector.tensor_copy(WDT[:, :], PS[:, 3, 0:128]).then_inc(wdt_set, 1)
            ends = YP[:, :, CHUNK:L + 1:CHUNK]
            dve.wait_ge(rec_y, len(REC_STEPS) - CHUNK)
            nc.vector.tensor_copy(ENDS, ends).then_inc(ends_saved, 1)
            dve.wait_ge(rec_y, len(REC_STEPS))
            nc.vector.tensor_tensor(DIFF, ends, ENDS, ALU.not_equal).then_inc(diff_step, 1)
            dve.wait_ge(diff_step, 1)
            nc.vector.tensor_reduce(NDIFF, DIFF, AX.XY, ALU.max).then_inc(ndiff_set, 1)
            dve.wait_ge(count_mm, 1)
            nc.vector.tensor_scalar(FLAG[0:1, 0:1], PS[0:1, 2, 0:1], 1.0, None, ALU.min).then_inc(flag_set, 1)
            for j in range(J):
                dve.wait_ge(rec_done, 1)
                nc.vector.tensor_tensor(X[:, j * L:(j + 1) * L], X[:, j * L:(j + 1) * L], YP[:, j, 1:L + 1],
                                        ALU.add).then_inc(x2_set, 1)
            ln_dve(dve, 3, XN)
            dve.wait_ge(xi_pad, 1)
            for b in range(B):
                dve.wait_ge(xi_set, 2 * (b + 1))
                dst = XC[:, b * L:(b + 1) * L]
                for k in range(DC):
                    tap = par("convw")[:, k:k + 1]
                    if k == 0:
                        nc.vector.tensor_scalar(dst, XI[:, b, 0:L], tap, None, ALU.mult).then_inc(conv_step, 1)
                    else:
                        dve.wait_ge(conv_step, DC * b + k)
                        nc.vector.scalar_tensor_tensor(out=dst, in0=XI[:, b, k:k + L], scalar=tap, in1=dst,
                                                       op0=ALU.mult, op1=ALU.add).then_inc(conv_step, 1)
            dve.wait_ge(aexp_set, 1)
            nc.vector.tensor_scalar(ANEG, AEXP, -1.0, None, ALU.mult).then_inc(a_set, 1)
            for q in range(1, 2 * B + 2):
                for b in DVE_DT:
                    if q == min(dt_step(b), 2 * B + 1):
                        here = slice(b * L, (b + 1) * L)
                        dve.wait_ge(sp_set, b + 1)
                        dve.wait_ge(v_set, b + 1)
                        nc.vector.tensor_tensor(DT[:, here], DT[:, here], SP[:, here], ALU.add).then_inc(dve_dt_set, 1)
                if q <= ACT_MIDDLES:
                    c = q - 1
                    dve.wait_ge(part_mm[1], c + 1)
                    nc.vector.tensor_copy(img((SB, SC)[c % 2], c // 2, slice(0, 64)),
                                          pair(c % 4, slice(0, 64))).then_inc(part_set[1], 1)
                if q >= 2:
                    c = q - 2
                    dve.wait_ge(part_mm[2], c + 1)
                    nc.vector.tensor_copy(img((SB, SC)[c % 2], c // 2, slice(0, 32)),
                                          pair(c % 4, slice(0, 32))).then_inc(part_set[2], 1)
            dve.wait_ge(part_set[2], 2 * B)
            dve.sem_inc(scanned, 2)
            dve.sem_inc(weighted, 2)
            dve.sem_inc(y_read, 1)

            def scan(b, s):
                dve.wait_ge(decay_set, b * DS + (s + 1))
                dve.wait_ge(u_set, b * (DS // 2) + (s // 2 + 1))
                nc.vector.tensor_tensor_scan(SLOT[s % SLOTS], DECAY[s % 2], SLOT[s % SLOTS], 0.0, ALU.mult,
                                             ALU.add).then_inc(scanned, 1)

            def weigh(b, s):
                dve.wait_ge(cbc_mm, b * DS + (s + 1))
                dve.wait_ge(scanned, b * DS + (s + 3))
                slot = img(SLOT[s % SLOTS], 0)
                nc.vector.tensor_tensor(slot, slot, pair(C_PAIR[s % 2]),
                                        ALU.mult).then_inc(weighted, 1)

            def read_y(b):
                dve.wait_ge(y_added, b * DS + (DS + SLOTS))
                xc = XC[:, bass.ds(b * L, L)].rearrange("p (a c) -> p a c", a=2)
                nc.vector.scalar_tensor_tensor(out=xc, in0=xc, scalar=par("dvec"), in1=pair(3), op0=ALU.mult,
                                               op1=ALU.add).then_inc(y_read, 1)

            for s in range(DS):
                scan(0, s)
                if s >= 1:
                    weigh(0, s - 1)
            with dve.Fori(1, B) as b:
                for s in range(DS):
                    scan(b, s)
                    if s == 2:
                        read_y(b - 1)
                    weigh(b, s - 1)
            weigh(B - 1, DS - 1)
            read_y(B - 1)
            dve.wait_ge(y_read, B + 1)
            for i in range(B + 2):
                if i % GROUPS == 1 and i > GROUPS:
                    j = i // GROUPS - 1
                    dve.wait_ge(out_mm, GROUPS * (j + 1))
                    nc.vector.tensor_tensor(img(X, j), pair(2 + j % 2), img(X, j), ALU.add).then_inc(x3_set, 1)
                if i >= B:
                    continue
                b = (i % GROUPS) * J + i // GROUPS
                here = slice(b * L, (b + 1) * L)
                dve.wait_ge(z_set, i + 1)
                nc.vector.tensor_tensor(YG[0:64, here], XC[0:64, here], GZ[0:64, here], ALU.mult).then_inc(yg_set, 1)
                if i % 2 == 0:
                    nc.vector.tensor_tensor(YG[64:128, here], XC[64:128, here][:, ::-1], GZ[64:128, here],
                                            ALU.mult).then_inc(yg_turned, 1)
            ln_dve(dve, 4, XN)
            n_lg = [0]

            def lstep(ins):
                n_lg[0] += 1
                ins.then_inc(lg_step, 1)
                dve.wait_ge(lg_step, n_lg[0])

            def t3(t):
                return t.rearrange("p (n e) -> p n e", e=EX)

            def over(t):
                return t.unsqueeze(2).to_broadcast([TOK, NT, EX])

            m = MROW[:, 0:NT]
            lstep(nc.vector.memset(RST, 1.0))
            lstep(nc.vector.memset(t3(RST)[:, :, 0:1], 0.0))
            dve.wait_ge(lg_mm, 1)
            rb = par("rb").unsqueeze(1).to_broadcast([TOK, NT // 2, EX])
            for h in range(2):
                lstep(nc.vector.tensor_tensor(t3(LG)[:, h * NT // 2:(h + 1) * NT // 2, :],
                                              PS[:, h, 0:NT // 2 * EX].rearrange("p (n e) -> p n e", e=EX), rb, ALU.add))
            lstep(nc.vector.tensor_reduce(m, t3(LG), AX.X, ALU.max))
            nc.vector.tensor_tensor(t3(LG), t3(LG), over(m), ALU.subtract).then_inc(lg_sub, 1)
            dve.wait_ge(lg_exp, 1)
            lstep(nc.vector.tensor_reduce(m, t3(LG), AX.X, ALU.add))
            lstep(nc.vector.reciprocal(m, m))
            lstep(nc.vector.tensor_tensor(t3(PR), t3(LG), over(m), ALU.mult))

            def first_largest(probs, sel, best):
                lstep(nc.vector.tensor_reduce(best, t3(probs), AX.X, ALU.max))
                lstep(nc.vector.tensor_tensor(t3(sel), t3(probs), over(best), ALU.is_equal))
                lstep(nc.vector.tensor_tensor_scan(CNT, RST, sel, 0.0, ALU.mult, ALU.add))
                lstep(nc.vector.scalar_tensor_tensor(out=sel, in0=CNT, scalar=1.0, in1=sel,
                                                     op0=ALU.is_equal, op1=ALU.mult))

            first_largest(PR, S1, m)
            m2 = MROW[:, NT:2 * NT]
            lstep(nc.vector.scalar_tensor_tensor(out=LG, in0=S1, scalar=-2.0, in1=PR,
                                                 op0=ALU.mult, op1=ALU.add))
            first_largest(LG, S2, m2)
            lstep(nc.vector.tensor_tensor(S1, S1, S2, ALU.add))
            lstep(nc.vector.tensor_tensor(S1, S1, PR, ALU.mult))
            lstep(nc.vector.tensor_tensor(m, m, m2, ALU.add))
            lstep(nc.vector.reciprocal(m, m))
            nc.vector.tensor_tensor(t3(PR), t3(S1), over(m), ALU.mult).then_inc(weights_set, 1)
            dve.wait_ge(weights_set, 1)
            for u in range(2 * TI):
                i, h = u // 2, u % 2
                dve.wait_ge(ex_mm, u + 1)
                if u >= 6:
                    wait_sums(dve, u - 5)
                n = GROUPS * i + 2 * h
                wts = t3(PR)[:, n:n + 2, :].unsqueeze(3).to_broadcast([TOK, 2, EX, C])
                nc.vector.tensor_tensor(PROD[u % 6].rearrange("p (t e c) -> p t e c", t=2, e=EX),
                                        PS[:, 2 + u % 6, :].rearrange("p (t e c) -> p t e c", t=2, e=EX),
                                        wts, ALU.mult).then_inc(ex_prod, 1)
                if u >= 1 and u - 1 not in POOL_SUMS:
                    add_experts(dve, u - 1)
                if i >= 1 and i % XT == 1 and h == 1 and i > 1:
                    finish_tiles(dve, i // XT - 1)
            add_experts(dve, 2 * TI - 1)
            finish_tiles(dve, BANKS_XT - 1)

        @block.tensor
        def _(pe):
            def each(semaphore):
                return lambda j: pe.wait_ge(semaphore, min(j + 1, J))

            pe.wait_ge(consts_set, 1)
            keep_warm(12)
            pe.wait_ge(first_loaded, 16)
            ln_pe(pe, 0, X, lambda j: pe.wait_ge(x_loaded[j], 16) if j < J else None)
            pe.wait_ge(front_loaded, 16)
            pe.wait_ge(main_loaded, 16)
            pe.wait_ge(ln[0]["out"], J)
            for j in range(J):
                if j >= 2:
                    pe.wait_ge(ctx_set, j - 1)
                pair_matmul(j % 2, fpar("wctx"), XN, j * L).then_inc(ctx_mm, 1)

            def linear(i):
                if i >= 2:
                    pe.wait_ge(lin_set, i - 1)
                pair_matmul(2 + i % 2, fpar(["wg0", "wg1", "wg2", "wq", "wg3"][i // J]), XN, i % J * L).then_inc(lin_mm, 1)

            pe.wait_ge(ctx_set, J)
            for l in range(LEVELS):
                if l >= 1:
                    pe.wait_ge(gelu_set, NP * l)
                taps = KS[l] ** 2
                for t in range(taps):
                    if l < 2:
                        pe.wait_ge(diag_made, TAP0[l] + t + 1)
                    else:
                        pe.wait_ge(diag2_made, t + 1)
                    for j, r0, rows, bank in PE_UNITS[0 if l < 2 else 1:]:
                        last = nc.tensor.matmul(PS[:, bank, 0:rows * W], DIAG[:, (TAP0[l] + t) * 128:(TAP0[l] + t + 1) * 128],
                                                window(CP[l % 2], l, t, j, r0, rows), start=t == 0, stop=t == taps - 1)
                        if t == taps - 1 and bank != 0:
                            last.then_inc(tap_pe, 1)
                    if t in LINEAR_AFTER[l]:
                        linear(LINEAR_AFTER[l].index(t) + (J if l == 2 else 0))
            pe.wait_ge(lin_set, 5 * J)
            keep_warm(12)
            for j in range(J):
                pe.wait_ge(glob_added, j + 1)
                pair_matmul(j, fpar("wh"), ALLC, j * L).then_inc(mod_mm, 1)
            ln_pe(pe, 1, XO, each(xo_set))
            pe.wait_ge(ln[1]["out"], J)
            nc.tensor.matmul(PS[:, 7, 0:1], fpar("wp"), fpar("beta"), start=True, stop=True).then_inc(bp_mm, 1)
            pe.wait_ge(wpg_set, 1)
            pe.wait_ge(bp_set, 1)
            for j in range(J):
                pair_matmul(j, WPG, XN, j * L).then_inc(proj_mm, 1)
            ln_pe(pe, 2, X, each(x1_set))
            pe.wait_ge(ln[2]["out"], J)
            for j in range(J):
                pair_matmul(j, par("fw"), XN, j * L).then_inc(wx_mm, 1)
            pe.wait_ge(wx_set, J)
            keep_warm(12)
            pe.wait_ge(bn_step, 3)
            nc.tensor.matmul(PS[:, 7, 0:2], par("gavg"), MEX, start=True, stop=True).then_inc(stats_mm, 1)
            nc.tensor.matmul(PS[:, 3, 0:128], par("xwd")[0:4, :], par("dtw")[0:4, :], start=True, stop=True).then_inc(wdt_mm, 1)
            pe.wait_ge(sdiag_set, 1)
            pe.wait_ge(y_zero, 2)

            def drive(k):
                return nc.tensor.matmul(PS[:, k % 2, 0:J * CHUNKS], SDIAG,
                                        WX.rearrange("p (j c k) -> p j c k", j=J, k=CHUNK)[:, :, :, k],
                                        start=True, stop=False)

            def feed(k):
                return nc.tensor.matmul(PS[:, k % 2, 0:J * CHUNKS], par("vt"),
                                        YP[:, :, k:k + 1 + CHUNK * (CHUNKS - 1):CHUNK], start=False, stop=True)

            keep_warm(4)
            drive(REC_STEPS[0])
            for q, k in enumerate(REC_STEPS):
                if q >= 1:
                    pe.wait_ge(rec_y, q)
                feed(k).then_inc(rec_mm, 1)
                if q + 1 < len(REC_STEPS):
                    drive(REC_STEPS[q + 1])
                    keep_warm(1)
            pe.wait_ge(ndiff_set, 1)
            nc.tensor.matmul(PS[0:1, 2, 0:1], NDIFF, par("ones"), start=True, stop=True).then_inc(count_mm, 1)
            pe.wait_ge(flag_set, 1)
            moved = pe.value_load(FLAG[0:1, 0:1], min_val=0, max_val=1)
            with pe.If(moved == 1):
                with pe.Fori(0, CHUNKS - 2) as p:
                    for k in range(CHUNK):
                        pe.wait_ge(slow_y, p * CHUNK + (k + 1))
                        drive(k)
                        feed(k).then_inc(slow_mm, 1)
            ln_pe(pe, 3, X, each(x2_set))
            pe.wait_ge(ln[3]["out"], J)
            pe.wait_ge(wdt_set, 1)
            pe.wait_ge(xz_loaded, 32)
            for b in range(B + 3):
                if b < B:
                    g, j = b // J, b % J
                    if b >= 2:
                        pe.wait_ge(xi_set, 2 * (b - 1))
                    pair_matmul(b % 2, INX[:, g * 128:(g + 1) * 128], XN, j * L).then_inc(in_mm, 1)
                if b >= 3:
                    i = b - 3
                    pe.wait_ge(xc_set, i + 1)
                    if i >= 2:
                        pe.wait_ge(abs_set, i - 1)
                    pair_matmul(2 + i % 2, WDT, XC, i * L).then_inc(dt_mm, 1)
            pe.wait_ge(xi_set, 2 * B)
            pe.wait_ge(negi_set, 1)
            for q in range(2 * B + 2):
                if q < 2 * B:
                    if q in (2, 3):
                        pe.wait_ge(abs_set, B - 3 + q)
                    if q >= 4:
                        pe.wait_ge(part_set[2], q - 3)
                    pair_matmul(q % 4, par(("xwb", "xwc")[q % 2]), XC, q // 2 * L, slice(0, 96)).then_inc(part_mm[0], 1)
                for i in (1, 2):
                    c = q - i
                    if 0 <= c < 2 * B:
                        if i == 2 and c >= ACT_MIDDLES:
                            pe.wait_ge(middle_act, c - ACT_MIDDLES + 1)
                        else:
                            pe.wait_ge(part_set[i - 1], c + 1)
                        pair_matmul(c % 4, NEGI, (SB, SC)[c % 2][0:96, :], (c // 2) * L, slice(0, 96),
                                    start=False, again=True).then_inc(part_mm[i], 1)
            pe.wait_ge(sel_set, 1)
            pe.wait_ge(part_set[2], 2 * B - 2)
            pe.sem_inc(y_added, SLOTS)

            def spread_b(b, s):
                pe.wait_ge(bbc_copied, b * DS + (s + 1))
                pair_matmul(1, SEL[:, s * 128:(s + 1) * 128], SB[0:96, :], b * L).then_inc(bbc_mm, 1)

            def spread_c(b, s):
                pe.wait_ge(weighted, b * DS + (s + 1))
                pair_matmul(C_PAIR[s % 2], SEL[:, s * 128:(s + 1) * 128], SC[0:96, :], b * L).then_inc(cbc_mm, 1)

            def add_state(b, s):
                pe.wait_ge(weighted, b * DS + (s + 3))
                if s == 0:
                    pe.wait_ge(y_read, b + 1)
                pair_matmul(3, par("ident"), SLOT[s % SLOTS], 0, start=s == 0, stop=s == DS - 1).then_inc(y_added, 1)

            def states(b, first=False, last=False):
                for s in range(DS):
                    spread_c(b, s)
                    if s == 2:
                        spread_b(b, s + LEAD_B + 1)
                    if s >= 2:
                        add_state(b, s - 2)
                    elif not first:
                        add_state(b - 1, DS - 2 + s)
                    if s + LEAD_B + 1 >= DS:
                        if not last:
                            spread_b(b + 1, s + LEAD_B + 1 - DS)
                    elif s != 2:
                        spread_b(b, s + LEAD_B + 1)

            for s in range(LEAD_B + 1):
                spread_b(0, s)
            pe.wait_ge(part_set[2], 2 * B)
            states(0, first=True)
            with pe.Fori(1, B - 1) as b:
                states(b)
            states(B - 1, last=True)
            add_state(B - 1, DS - 2)
            add_state(B - 1, DS - 1)
            pe.wait_ge(weighted, B * DS + 2)
            pe.wait_ge(bbc_copied, B * DS + 1)
            for i in range(B + 2):
                if i < B:
                    j, g = i // GROUPS, i % GROUPS
                    if i >= 2:
                        pe.wait_ge(z_set, i - 1)
                    pair_matmul(i % 2, INZ[:, g * 128:(g + 1) * 128], XN, j * L).then_inc(z_mm, 1)
                if i >= 2:
                    j, g = (i - 2) // GROUPS, (i - 2) % GROUPS
                    pe.wait_ge(yg_set, i - 1)
                    if i % 2 == 0:
                        pe.wait_ge(yg_turned, i // 2)
                    else:
                        pe.wait_ge(yg_turned_pool, (i - 1) // 2)
                    if j >= 2 and g == 0:
                        pe.wait_ge(x3_set, j - 1)
                    pair_matmul(2 + j % 2, par("outw"), YG, (g * J + j) * L, slice(C * g, C * (g + 1))).then_inc(out_mm, 1)
            ln_pe(pe, 4, X, each(x3_set))
            pe.wait_ge(ln[4]["out"], J)

            for i in range(TI):
                last = nc.tensor.matmul(PS[:, i // (TI // 2), i % (TI // 2) * GROUPS * EX:(i % (TI // 2) + 1) * GROUPS * EX],
                                        tokens(XN, i), par("rw"), start=True, stop=True)
            last.then_inc(lg_mm, 1)
            pe.wait_ge(eb_set, 1)
            pe.wait_ge(experts_loaded, 16)
            pe.wait_ge(lg_step, 4)
            for i in range(TI):
                if i % XT == 0:
                    m = i // XT
                    if m >= 2:
                        pe.wait_ge(yt_set, m - 1)
                    for k in range(i, min(i + XT, TI)):
                        last = nc.tensor.matmul(PS[:, m % 2, (k - i) * 128:(k - i + 1) * 128], tokens(X, k),
                                                par("ident"), start=True, stop=True)
                    last.then_inc(xt_mm, 1)
                for h in range(2):
                    u = 2 * i + h
                    if u >= 6:
                        pe.wait_ge(ex_prod, u - 5)
                    nc.tensor.matmul(PS[:, 2 + u % 6, :], tokens(XN, i), EWB[:, h * 2 * EX * C:(h + 1) * 2 * EX * C],
                                     start=True, stop=False)
                    nc.tensor.matmul(PS[:, 2 + u % 6, :], ONB, EBS, start=False, stop=True).then_inc(ex_mm, 1)


def lay_out(inputs):
    a = {k: np.asarray(v) for k, v in inputs.items()}
    f = np.float32
    x = np.ascontiguousarray(a["x"].reshape(GROUPS, J, L, C).transpose(0, 3, 1, 2)).reshape(128, N)

    def blocks(w, times=GROUPS):
        r, c = w.shape
        o = np.zeros((times * r, times * c), f)
        for i in range(times):
            o[i * r:(i + 1) * r, i * c:(i + 1) * c] = w
        return o

    def down(w, times=GROUPS):
        return np.tile(w.reshape(w.shape[0], -1), (times, 1))

    main, front = np.zeros((128, MAIN_W), f), np.zeros((128, FRONT_W), f)

    def put(name, w):
        where = MAIN_AT if name in MAIN_AT else FRONT_AT
        (main if name in MAIN_AT else front)[0:w.shape[0], where[name]] = w

    eye, one = np.eye(128, dtype=f), blocks(np.full((C, C), 1.0 / C, f))
    put("ident", eye)
    put("cent", eye - one)
    msel = np.zeros((GROUPS, C, 60), f)
    for g in range(GROUPS):
        msel[g, :, 28 + g] = 1.0 / C
    put("msel", msel.reshape(128, 60))
    rows = np.zeros((2 * J, GROUPS, 2 * J, GROUPS, C), f)
    for r in range(2 * J):
        for g in range(GROUPS):
            rows[r, g, r, g, :] = 1.0
    rows = rows.reshape(32, 2 * J * 128)
    put("gavg", np.tile(np.eye(C, dtype=f) / GROUPS, (GROUPS, GROUPS)))
    put("ones", np.ones((128, 1), f))
    sel = np.zeros((3, 2, DS, DS, 2, DI), f)
    for d in range(2):
        for s in range(DS):
            sel[:, d, s, s, d, :] = 1.0
    sel = sel.reshape(3 * 2 * DS, DS * 128)
    wf, bf = a["L0_conv_Wf"], a["L0_conv_bf"]
    put("wq", blocks(wf[:, 0:C]))
    put("wctx", blocks(wf[:, C:2 * C]))
    for l in range(LEVELS + 1):
        put(f"wg{l}", blocks(np.tile(wf[:, 2 * C + l:2 * C + l + 1], (1, C))))
    put("bq", down(bf[0:C]))
    put("bctx", down(bf[C:2 * C]))
    put("bg", np.tile(bf[2 * C:].reshape(1, -1), (128, 1)))
    put("wh", blocks(a["L0_conv_Wh"]))
    put("wp", blocks(a["L0_conv_Wp"]))
    put("taps", np.concatenate([down(a[f"L0_conv_k{l}"].reshape(-1, C).T) for l in range(LEVELS)], 1))
    for name, key in (("bh", "bh"), ("gamma", "gamma"), ("beta", "beta"), ("bp", "bp")):
        put(name, down(a["L0_conv_" + key]))
    put("fw", blocks(a["L0_ffn_W"].T))
    put("vt", blocks(a["L0_ffn_V"].T))
    put("fgam", down(a["L0_ffn_gamma"]))
    put("fbet", down(a["L0_ffn_beta"]))
    iw, xw = a["L1_conv_in_w"], a["L1_conv_x_w"]
    xz = np.zeros((GROUPS, C, 2, GROUPS, 2, DI), f)
    for g in range(GROUPS):
        for i in range(2):
            xz[g, :, i, g, :, :] = iw[i * DI:(i + 1) * DI].T[:, None, :]
    xz = xz.reshape(128, 2 * GROUPS * 128)
    put("xwd", blocks(xw[0:DR], 2))
    put("dtw", blocks(a["L1_conv_dt_w"].T, 2))
    for name, r0 in (("xwb", DR), ("xwc", DR + DS)):
        put(name, np.tile(blocks(xw[r0:r0 + DS].T, 2), (1, 3)))
    put("outw", down(a["L1_conv_out_w"].T, 2))
    put("convw", down(a["L1_conv_conv_w"], 2))
    put("convb", down(a["L1_conv_conv_b"], 2))
    put("dvec", down(a["L1_conv_D"], 2))
    put("dtb", down(a["L1_conv_dt_b"], 2))
    put("alog", down(a["L1_conv_A_log"], 2))
    put("rw", blocks(a["L1_ffn_router_w"]))
    put("rb", np.tile(a["L1_ffn_router_b"].reshape(1, EX), (128, 1)))
    experts = blocks(np.ascontiguousarray(a["L1_ffn_expert_w"].transpose(1, 0, 2)).reshape(C, EX * C))
    eb = np.zeros((96, 2 * EX * C), f)
    eb[0:96:32] = np.tile(a["L1_ffn_expert_b"].reshape(1, EX * C), (1, 2))
    put("eb", eb)
    return {"x_in": x, "main_in": main, "front_in": front, "sel_in": sel, "rows_in": rows, "xz_in": xz,
            "experts_in": experts}


def kernel(**inputs):
    import concourse.bacc as bacc
    from concourse.bass_utils import run_bass_kernel_spmd

    nc = bacc.Bacc("TRN2", target_bir_lowering=False, num_devices=1)
    arrays = lay_out(inputs)
    args = [nc.dram_tensor(name, a.shape, mybir.dt.float32, kind="ExternalInput").ap() for name, a in arrays.items()]
    out = nc.dram_tensor("out", (B * L, C), mybir.dt.float32, kind="ExternalOutput").ap()
    build_program(nc, *args, out)
    r = run_bass_kernel_spmd(nc, [arrays], core_ids=[0])
    return r.results[0]["out"].reshape(B, H, W, C)
```
